# Optimizing a Trainium2 kernel written in Bass

```python
import numpy as np
import jax
import jax.numpy as jnp

def _softmax(x, axis=-1):
    return jax.nn.softmax(x, axis=axis)

def _gelu(x):
    return jax.nn.gelu(x, approximate=True)

def _silu(x):
    return jax.nn.silu(x)

def _sigmoid(x):
    return jax.nn.sigmoid(x)

def _layernorm(x, axis=-1, eps=1e-05):
    m = jnp.mean(x, axis=axis, keepdims=True)
    v = jnp.var(x, axis=axis, keepdims=True)
    return (x - m) / jnp.sqrt(v + eps)

def _scatter_add(tgt, idx, src, axis=0):
    return tgt.at[idx].add(src)

def _segment_sum(src, seg, n):
    return jax.ops.segment_sum(src, seg, n)
kernel_name = 'mk_decoder_postln_d1_seqx_r2_afa989'

def setup_inputs(seed: int=0):
    np.random.seed(seed)
    _w = jnp.asarray

    def _rec_inputs():
        import jax
        import jax.numpy as jnp
        _rk = jax.random.key(seed)
        x = -0.0002928 + 1 * jax.random.normal(jax.random.fold_in(_rk, 1), (8, 512, 512), jnp.float32)
        _lenS = 512 - jax.random.randint(jax.random.fold_in(_rk, 7), (8,), 0, max(1, 512 // 4) + 1, jnp.int32)
        _lenS2 = 512 - jax.random.randint(jax.random.fold_in(_rk, 8), (8,), 0, max(1, 512 // 4) + 1, jnp.int32)
        _ctx_768P = jax.random.normal(jax.random.fold_in(_rk, 11), (8, 16, 384), jnp.float32)
        _ctx_768c = jax.random.dirichlet(jax.random.fold_in(_rk, 511), 0.3 * jnp.ones((16,), jnp.float32), (8, 512))
        _ctx_768t = jnp.einsum('bsk,bkd->bsd', _ctx_768c, _ctx_768P)
        _ctx_768t = _ctx_768t * jax.lax.rsqrt(jnp.mean(jnp.square(_ctx_768t)) + 1e-12) * 0.953939
        ctx_768 = 2.09791e-05 + 1.00001 * (_ctx_768t + 0.3 * jax.random.normal(jax.random.fold_in(_rk, 611), (8, 512, 384), jnp.float32))
        return (x, ctx_768)
    x, ctx_768 = _rec_inputs()

    def _L0_attn_setup():
        import jax, jax.numpy as jnp
        import numpy as np
        D_MODEL = 512
        NUM_HEADS = 16
        D_K = D_MODEL // NUM_HEADS
        MAX_LEN = 512
        BATCH = 8
        SEQ = 512
        key = jax.random.key(seed)
        ks = jax.random.split(key, 12)
        s = 0.02
        inp = {'x': jax.random.normal(ks[0], (BATCH, SEQ, D_MODEL), dtype=jnp.float32), 'Wq': jax.random.normal(ks[1], (D_MODEL, D_MODEL), dtype=jnp.float32) * s, 'bq': jnp.zeros((D_MODEL,), dtype=jnp.float32), 'Wk': jax.random.normal(ks[2], (D_MODEL, D_MODEL), dtype=jnp.float32) * s, 'bk': jnp.zeros((D_MODEL,), dtype=jnp.float32), 'Wv': jax.random.normal(ks[3], (D_MODEL, D_MODEL), dtype=jnp.float32) * s, 'bv': jnp.zeros((D_MODEL,), dtype=jnp.float32), 'Wo': jax.random.normal(ks[4], (D_MODEL, D_MODEL), dtype=jnp.float32) * s, 'bo': jnp.zeros((D_MODEL,), dtype=jnp.float32), 'relative_k': jax.random.normal(ks[5], (2 * MAX_LEN - 1, D_K), dtype=jnp.float32), 'relative_v': jax.random.normal(ks[6], (2 * MAX_LEN - 1, D_K), dtype=jnp.float32)}
        return inp
    _L0_attn_all = _L0_attn_setup()
    _L0_attn_in = {k: v for k, v in _L0_attn_all.items() if k in ('Wq', 'bq', 'Wk', 'bk', 'Wv', 'bv', 'Wo', 'bo', 'relative_k', 'relative_v')}
    del _L0_attn_all

    def _L0_xattn_setup():
        import jax, jax.numpy as jnp
        import numpy as np
        N_HEADS = 16
        D_EMBED = 512
        N_CROSS = 384
        D_HEAD = D_EMBED // N_HEADS
        key = jax.random.key(seed)
        ks = jax.random.split(key, 10)
        B, S = (2, 1024)
        x = jax.random.normal(ks[0], (B, S, D_EMBED), dtype=jnp.float32)
        context = jax.random.normal(ks[1], (B, S, N_CROSS), dtype=jnp.float32)
        sq = 1.0 / np.sqrt(D_EMBED)
        sc = 1.0 / np.sqrt(N_CROSS)
        Wq = jax.random.normal(ks[2], (D_EMBED, D_EMBED), dtype=jnp.float32) * sq
        bq = jnp.zeros((D_EMBED,), dtype=jnp.float32)
        Wk = jax.random.normal(ks[3], (N_CROSS, D_EMBED), dtype=jnp.float32) * sc
        bk = jnp.zeros((D_EMBED,), dtype=jnp.float32)
        Wv = jax.random.normal(ks[4], (N_CROSS, D_EMBED), dtype=jnp.float32) * sc
        bv = jnp.zeros((D_EMBED,), dtype=jnp.float32)
        Wo = jax.random.normal(ks[5], (D_EMBED, D_EMBED), dtype=jnp.float32) * sq
        bo = jnp.zeros((D_EMBED,), dtype=jnp.float32)
        return {'x': x, 'context': context, 'Wq': Wq, 'bq': bq, 'Wk': Wk, 'bk': bk, 'Wv': Wv, 'bv': bv, 'Wo': Wo, 'bo': bo}
    _L0_xattn_all = _L0_xattn_setup()
    _L0_xattn_in = {k: v for k, v in _L0_xattn_all.items() if k in ('Wq', 'bq', 'Wk', 'bk', 'Wv', 'bv', 'Wo', 'bo')}
    del _L0_xattn_all

    def _L0_ffn_setup():
        import jax, jax.numpy as jnp
        import numpy as np
        BS, L, D = (4, 1024, 512)
        H, E, K = (8, 16, 2)
        HD = D // H
        I = 2048 // H
        key = jax.random.key(seed)
        ks = jax.random.split(key, 10)
        s = lambda k, shp, fan: jax.random.normal(k, shp, jnp.float32) / np.sqrt(fan)
        return {'x': jax.random.normal(ks[0], (BS, L, D), jnp.float32), 'Wm': s(ks[1], (D, D), D), 'bm': jnp.zeros((D,), jnp.float32), 'expert_emb': jax.random.normal(ks[2], (HD, E), jnp.float32), 'W1': s(ks[3], (E, HD, I), HD), 'b1': jnp.zeros((E, I), jnp.float32), 'W2': s(ks[4], (E, I, HD), I), 'b2': jnp.zeros((E, HD), jnp.float32), 'Wo': s(ks[5], (D, D), D), 'bo': jnp.zeros((D,), jnp.float32)}
    _L0_ffn_all = _L0_ffn_setup()
    _L0_ffn_in = {k: v for k, v in _L0_ffn_all.items() if k in ('Wm', 'bm', 'expert_emb', 'W1', 'b1', 'W2', 'b2', 'Wo', 'bo')}
    del _L0_ffn_all
    return {'x': x, 'ctx_768': ctx_768, 'L0_attn_Wq': _L0_attn_in['Wq'], 'L0_attn_bq': _L0_attn_in['bq'], 'L0_attn_Wk': _L0_attn_in['Wk'], 'L0_attn_bk': _L0_attn_in['bk'], 'L0_attn_Wv': _L0_attn_in['Wv'], 'L0_attn_bv': _L0_attn_in['bv'], 'L0_attn_Wo': _L0_attn_in['Wo'], 'L0_attn_bo': _L0_attn_in['bo'], 'L0_attn_relative_k': _L0_attn_in['relative_k'], 'L0_attn_relative_v': _L0_attn_in['relative_v'], 'L0_xattn_Wq': _L0_xattn_in['Wq'], 'L0_xattn_bq': _L0_xattn_in['bq'], 'L0_xattn_Wk': _L0_xattn_in['Wk'], 'L0_xattn_bk': _L0_xattn_in['bk'], 'L0_xattn_Wv': _L0_xattn_in['Wv'], 'L0_xattn_bv': _L0_xattn_in['bv'], 'L0_xattn_Wo': _L0_xattn_in['Wo'], 'L0_xattn_bo': _L0_xattn_in['bo'], 'L0_ffn_Wm': _L0_ffn_in['Wm'], 'L0_ffn_bm': _L0_ffn_in['bm'], 'L0_ffn_expert_emb': _L0_ffn_in['expert_emb'], 'L0_ffn_W1': _L0_ffn_in['W1'], 'L0_ffn_b1': _L0_ffn_in['b1'], 'L0_ffn_W2': _L0_ffn_in['W2'], 'L0_ffn_b2': _L0_ffn_in['b2'], 'L0_ffn_Wo': _L0_ffn_in['Wo'], 'L0_ffn_bo': _L0_ffn_in['bo']}

def reference(x, ctx_768, L0_attn_Wq, L0_attn_bq, L0_attn_Wk, L0_attn_bk, L0_attn_Wv, L0_attn_bv, L0_attn_Wo, L0_attn_bo, L0_attn_relative_k, L0_attn_relative_v, L0_xattn_Wq, L0_xattn_bq, L0_xattn_Wk, L0_xattn_bk, L0_xattn_Wv, L0_xattn_bv, L0_xattn_Wo, L0_xattn_bo, L0_ffn_Wm, L0_ffn_bm, L0_ffn_expert_emb, L0_ffn_W1, L0_ffn_b1, L0_ffn_W2, L0_ffn_b2, L0_ffn_Wo, L0_ffn_bo):
    import jax
    import jax.numpy as jnp

    def _L0_attn_ref(x, Wq, bq, Wk, bk, Wv, bv, Wo, bo, relative_k, relative_v):
        import jax, jax.numpy as jnp
        import numpy as np
        D_MODEL = 512
        NUM_HEADS = 16
        D_K = D_MODEL // NUM_HEADS
        MAX_LEN = 512
        BATCH = 8
        SEQ = 512
        B, L, D = x.shape
        H, dk = (NUM_HEADS, D_K)
        Q = (x @ Wq.T + bq).reshape(B, L, H, dk).transpose(0, 2, 1, 3)
        K = (x @ Wk.T + bk).reshape(B, L, H, dk).transpose(0, 2, 1, 3)
        V = (x @ Wv.T + bv).reshape(B, L, H, dk).transpose(0, 2, 1, 3)
        rel_pos = jnp.arange(L)[None, :] - jnp.arange(L)[:, None] + (MAX_LEN - 1)
        rel_k = relative_k[rel_pos]
        rel_v = relative_v[rel_pos]
        scale = 1.0 / np.sqrt(dk).astype(np.float32)
        scores = jnp.einsum('bhld,bhrd->bhlr', Q, K) * scale
        scores = scores + jnp.einsum('bhld,lrd->bhlr', Q, rel_k)
        attn = jax.nn.softmax(scores, axis=-1)
        out = jnp.einsum('bhlr,bhrd->bhld', attn, V)
        out = out + jnp.einsum('bhlr,lrd->bhld', attn, rel_v)
        out = out.transpose(0, 2, 1, 3).reshape(B, L, D)
        return out @ Wo.T + bo

    def _L0_xattn_ref(x, context, Wq, bq, Wk, bk, Wv, bv, Wo, bo):
        import jax, jax.numpy as jnp
        import numpy as np
        N_HEADS = 16
        D_EMBED = 512
        N_CROSS = 384
        D_HEAD = D_EMBED // N_HEADS
        B, S, _ = x.shape

        def split_heads(t):
            return t.reshape(B, S, N_HEADS, D_HEAD).transpose(0, 2, 1, 3)
        q = split_heads(x @ Wq + bq)
        k = split_heads(context @ Wk + bk)
        v = split_heads(context @ Wv + bv)
        scale = 1.0 / np.sqrt(D_HEAD)
        scores = jnp.einsum('bhqd,bhkd->bhqk', q, k) * scale
        attn = jax.nn.softmax(scores, axis=-1)
        out = jnp.einsum('bhqk,bhkd->bhqd', attn, v)
        out = out.transpose(0, 2, 1, 3).reshape(B, S, D_EMBED)
        return out @ Wo + bo

    def _L0_ffn_ref(x, Wm, bm, expert_emb, W1, b1, W2, b2, Wo, bo):
        import jax, jax.numpy as jnp
        import numpy as np
        BS, L, D = (4, 1024, 512)
        H, E, K = (8, 16, 2)
        HD = D // H
        I = 2048 // H
        bs, L_, d = x.shape
        h = x @ Wm + bm
        t = h.reshape(bs * L_ * H, HD)
        logits = t @ expert_emb
        w = jax.nn.softmax(logits, axis=-1)
        topw, topi = jax.lax.top_k(w, K)
        hmid = jax.nn.gelu(jnp.einsum('td,edi->tei', t, W1) + b1, approximate=False)
        eo = jnp.einsum('tei,eio->teo', hmid, W2) + b2
        sel = jnp.take_along_axis(eo, topi[:, :, None], axis=1)
        comb = (sel * topw[:, :, None]).sum(axis=1)
        out = comb.reshape(bs, L_, d)
        return out @ Wo + bo
    x = _layernorm(x + _L0_attn_ref(x, L0_attn_Wq, L0_attn_bq, L0_attn_Wk, L0_attn_bk, L0_attn_Wv, L0_attn_bv, L0_attn_Wo, L0_attn_bo, L0_attn_relative_k, L0_attn_relative_v), axis=-1)
    x = _layernorm(x + _L0_xattn_ref(x, ctx_768, L0_xattn_Wq, L0_xattn_bq, L0_xattn_Wk, L0_xattn_bk, L0_xattn_Wv, L0_xattn_bv, L0_xattn_Wo, L0_xattn_bo), axis=-1)
    x = _layernorm(x + _L0_ffn_ref(x, L0_ffn_Wm, L0_ffn_bm, L0_ffn_expert_emb, L0_ffn_W1, L0_ffn_b1, L0_ffn_W2, L0_ffn_b2, L0_ffn_Wo, L0_ffn_bo), axis=-1)
    return x

_drawn_inputs = setup_inputs


def setup_inputs(seed=0):
    import zlib

    import numpy as np

    out = dict(_drawn_inputs(seed))
    spreads = {'L0_attn_bq': (0.0, 0.1),
     'L0_attn_bk': (0.0, 0.1),
     'L0_attn_bv': (0.0, 0.1),
     'L0_attn_bo': (0.0, 0.1),
     'L0_xattn_bq': (0.0, 0.1),
     'L0_xattn_bk': (0.0, 0.1),
     'L0_xattn_bv': (0.0, 0.1),
     'L0_xattn_bo': (0.0, 0.1),
     'L0_ffn_bm': (0.0, 0.1),
     'L0_ffn_b1': (0.0, 0.1),
     'L0_ffn_b2': (0.0, 0.1),
     'L0_ffn_bo': (0.0, 0.1)}
    factors = {}
    for name, (base, spread) in spreads.items():
        noise = np.random.default_rng([zlib.crc32(name.encode()), seed]).standard_normal(out[name].shape)
        drawn = base * np.exp(spread * noise) if base else spread * noise
        out[name] = jnp.asarray(drawn.astype(out[name].dtype))
    for name, factor in factors.items():
        out[name] = (out[name] * factor).astype(out[name].dtype)
    return out
```

```python
from contextlib import ExitStack

import numpy as np

import concourse.bass as bass
from concourse import mybir

ACT = mybir.ActivationFunctionType
ALU = mybir.AluOpType
AX_X = mybir.AxisListType.X
F32 = mybir.dt.float32
I32 = mybir.dt.int32
U32 = mybir.dt.uint32

P = 128
BATCH, SEQ, D_MODEL, D_CTX = 8, 512, 512, 384
HEADS, D_HEAD = 16, 32
CHUNKS = D_MODEL // P
TOK_TILES = SEQ // P
HEADS_PER_CHUNK = P // D_HEAD
SCALE = float(1.0 / np.sqrt(np.float32(D_HEAD)))
LN_EPS = 1e-5


class Memory:

    def __init__(self, nc, ctx, stage):
        self.nc, self.ctx, self.stage, self.sems = nc, ctx, stage, []
        ctx.callback(self.clear)

    def sbuf(self, name, shape, dtype=F32):
        return self.ctx.enter_context(self.nc.sbuf_tensor(f"{self.stage}_{name}", shape, dtype))

    def psum(self, name, shape, dtype=F32):
        return self.ctx.enter_context(self.nc.psum_tensor(f"{self.stage}_{name}", shape, dtype))

    def sem(self, name):
        self.sems.append(self.nc.alloc_semaphore(name=f"{self.stage}_{name}"))
        return self.sems[-1]

    def clear(self):
        if self.sems:
            self.nc.clear_and_free_semaphores(self.sems)
            self.nc.all_engine_barrier()


def stand(engine, alone):
    engine.sem_inc(alone, 1)


def by_partition(ap, offset, dims):
    return bass.AP(ap.tensor, offset, dims)


def project(nc, stage, q_src, kv_src, weights, biases, q_out, k_out, v_out):
    q_rows, kv_rows = q_src.shape[1] // P, kv_src.shape[1] // P
    w_q, w_k, w_v = weights
    b_q, b_k, b_v = biases
    banks = 4
    turns = BATCH // 2
    with ExitStack() as ctx:
        mem = Memory(nc, ctx, f"{stage}_project")
        wq = mem.sbuf("wq", [P, q_rows, D_MODEL])
        wk = mem.sbuf("wk", [P, kv_rows, D_MODEL])
        wv = mem.sbuf("wv", [P, kv_rows, D_MODEL])
        bias_q = mem.sbuf("bias_q", [P, CHUNKS])
        bias_k = mem.sbuf("bias_k", [P, CHUNKS])
        bias_k_scaled = mem.sbuf("bias_k_scaled", [P, CHUNKS])
        bias_v = mem.sbuf("bias_v", [P, D_MODEL])
        src_q = [mem.sbuf(f"src_q{n}", [P, q_rows, SEQ]) for n in range(2)]
        src_kv = [mem.sbuf(f"src_kv{n}", [P, kv_rows, SEQ]) for n in range(2)]
        out_q = [mem.sbuf(f"out_q{n}", [P, CHUNKS, SEQ]) for n in range(2)]
        out_k = [mem.sbuf(f"out_k{n}", [P, CHUNKS, SEQ]) for n in range(2)]
        out_v = [mem.sbuf(f"out_v{n}", [P, TOK_TILES, D_MODEL]) for n in range(2)]
        ps_qk = mem.psum("ps_qk", [P, banks, SEQ])
        ps_v = mem.psum("ps_v", [P, banks, D_MODEL])
        weights_in = mem.sem("weights_in")
        biases_in = mem.sem("biases_in")
        bias_scaled = mem.sem("bias_scaled")
        src_in = [mem.sem(f"src_in{n}") for n in range(2)]
        src_free = mem.sem("src_free")
        qk_product = mem.sem("qk_product")
        qk_bank_free = mem.sem("qk_bank_free")
        v_product = mem.sem("v_product")
        v_bank_free = mem.sem("v_bank_free")
        qk_stored = [mem.sem(f"qk_stored{n}") for n in range(2)]
        v_stored = [mem.sem(f"v_stored{n}") for n in range(2)]
        block = ctx.enter_context(nc.Block())

        @block.sync
        def _(sp):
            sp.dma_start(wq[:, :, :], w_q.rearrange("(r p) n -> p r n", p=P)).then_inc(weights_in, 16)
            sp.dma_start(wk[:, :, :], w_k.rearrange("(r p) n -> p r n", p=P)).then_inc(weights_in, 16)
            sp.dma_start(wv[:, :, :], w_v.rearrange("(r p) n -> p r n", p=P)).then_inc(weights_in, 16)
            sp.dma_start(bias_q[:, :], b_q.rearrange("(c p) -> p c", p=P),
                         allow_slow_non_contiguous=True).then_inc(biases_in, 16)
            sp.dma_start(bias_k[:, :], b_k.rearrange("(c p) -> p c", p=P),
                         allow_slow_non_contiguous=True).then_inc(biases_in, 16)
            sp.dma_start(bias_v[:, :], by_partition(b_v, 0, [[0, P], [1, D_MODEL]])).then_inc(biases_in, 16)
            with sp.Fori(0, turns) as turn:
                for half in range(2):
                    sp.wait_ge(src_free, 2 * turn + half + 1)
                    for dst, src in ((src_q, q_src), (src_kv, kv_src)):
                        sp.dma_start(dst[half][:, :, :],
                                     src[2 * turn + half].rearrange("(r p) t -> p r t", p=P)).then_inc(src_in[half], 16)

        @block.gpsimd
        def _(pool):
            with pool.Fori(0, turns) as turn:
                for half in range(2):
                    pool.wait_ge(v_bank_free, TOK_TILES * (2 * turn + half + 1) + banks)
                    pool.dma_start(v_out[2 * turn + half].rearrange("(r p) n -> p r n", p=P),
                                   out_v[half][:, :, :]).then_inc(v_stored[half], 16)
            for half in range(2):
                pool.wait_ge(v_stored[half], 16 * turns)

        @block.tensor
        def _(pe):
            pe.sem_inc(src_free, 2)
            pe.wait_ge(weights_in, 48)
            with pe.Fori(0, turns) as turn:
                for half in range(2):
                    pe.wait_ge(src_in[half], 32 * (turn + 1))
                    groups = [(wq, src_q, q_rows)] * CHUNKS + [(wk, src_kv, kv_rows)] * CHUNKS
                    for n, (w, src, rows) in enumerate(groups):
                        chunk = n % CHUNKS
                        pe.wait_ge(qk_bank_free, 2 * CHUNKS * (2 * turn + half) + n + 1)
                        for r in range(rows):
                            last = nc.tensor.matmul(ps_qk[:, n % banks, :], w[:, r, chunk * P:(chunk + 1) * P],
                                                    src[half][:, r, :], start=(r == 0), stop=(r == rows - 1))
                        last.then_inc(qk_product, 1)
                    for t in range(TOK_TILES):
                        pe.wait_ge(v_bank_free, TOK_TILES * (2 * turn + half) + t + 1)
                        for r in range(kv_rows):
                            last = nc.tensor.matmul(ps_v[:, t % banks, :], src_kv[half][:, r, t * P:(t + 1) * P],
                                                    wv[:, r, :], start=(r == 0), stop=(r == kv_rows - 1))
                        last.then_inc(v_product, 1)
                        if t == TOK_TILES - 1:
                            pe.wait_ge(v_product, TOK_TILES * (2 * turn + half + 1))
                            pe.sem_inc(src_free, 1)

        @block.scalar
        def _(act):
            act.sem_inc(qk_bank_free, banks)
            act.wait_ge(biases_in, 48)
            nc.scalar.activation(bias_k_scaled[:, :], bias_k[:, :], ACT.Copy, scale=SCALE).then_inc(bias_scaled, 1)
            act.wait_ge(bias_scaled, 1)
            with act.Fori(0, turns) as turn:
                for half in range(2):
                    act.wait_ge(qk_stored[half], 32 * turn)
                    for n in range(2 * CHUNKS):
                        chunk = n % CHUNKS
                        out, bias, scale = ((out_q, bias_q, 1.0), (out_k, bias_k_scaled, SCALE))[n // CHUNKS]
                        act.wait_ge(qk_product, 2 * CHUNKS * (2 * turn + half) + n + 1)
                        nc.scalar.activation(out[half][:, chunk, :], ps_qk[:, n % banks, :], ACT.Identity,
                                             bias=bias[:, chunk:chunk + 1], scale=scale).then_inc(qk_bank_free, 1)
                    act.wait_ge(qk_bank_free, 2 * CHUNKS * (2 * turn + half + 1) + banks)
                    for dst, out in ((q_out, out_q), (k_out, out_k)):
                        act.dma_start(dst[2 * turn + half].rearrange("(c p) t -> p c t", p=P),
                                      out[half][:, :, :]).then_inc(qk_stored[half], 16)
            for half in range(2):
                act.wait_ge(qk_stored[half], 32 * turns)

        @block.vector
        def _(dve):
            dve.sem_inc(v_bank_free, banks)
            dve.wait_ge(biases_in, 48)
            with dve.Fori(0, turns) as turn:
                for half in range(2):
                    dve.wait_ge(v_stored[half], 16 * turn)
                    for t in range(TOK_TILES):
                        dve.wait_ge(v_product, TOK_TILES * (2 * turn + half) + t + 1)
                        nc.vector.tensor_tensor(out_v[half][:, t, :], ps_v[:, t % banks, :], bias_v[:, :],
                                                ALU.add).then_inc(v_bank_free, 1)


BATCHES_AT_ONCE = 2
ROWS = 64
UNITS_PER_PAIR = SEQ // ROWS
UNITS = BATCH // BATCHES_AT_ONCE * UNITS_PER_PAIR
TILES = BATCHES_AT_ONCE * HEADS // 2
GROUPS = BATCHES_AT_ONCE * CHUNKS
WINDOW = SEQ + ROWS - 1
PITCH = WINDOW + 1
KEY_TILES = SEQ // P
BIG = 3.0e38


def identity_matrix(pool, nc, ident, zeroed, ready):
    nc.gpsimd.memset(ident[:, :], 0.0).then_inc(zeroed, 1)
    pool.wait_ge(zeroed, 1)
    nc.gpsimd.affine_select(out=ident[:, :], in_=ident[:, :], compare_op=ALU.not_equal, fill=1.0, base=0,
                            pattern=[[-1, P]], channel_multiplier=1).then_inc(ready, 1)


def attend(nc, stage, q_t, k_t, v, out_t, rel=None):
    with ExitStack() as ctx:
        mem = Memory(nc, ctx, f"{stage}_attend")
        ident = mem.sbuf("ident", [P, P])
        queries = mem.sbuf("queries", [P, TILES, 2, ROWS])
        keys = mem.sbuf("keys", [P, BATCHES_AT_ONCE, CHUNKS, SEQ])
        values = mem.sbuf("values", [P, KEY_TILES, BATCHES_AT_ONCE, D_MODEL])
        probs = mem.sbuf("probs", [P, TILES, SEQ])
        probs_t = mem.sbuf("probs_t", [P, KEY_TILES, TILES, 2, ROWS])
        low = mem.sbuf("low", [P, TILES])
        total = mem.sbuf("total", [P, TILES])
        inverse = mem.sbuf("inverse", [P, TILES])
        own_head = mem.sbuf("own_head", [P, 2, D_HEAD])
        own_row = mem.sbuf("own_row", [P, ROWS])
        spread = mem.sbuf("spread", [P, TILES, 2, D_HEAD])
        sums = mem.sbuf("sums", [P, GROUPS, ROWS])
        out = mem.sbuf("out", [P, GROUPS, ROWS])
        ps_scores = mem.psum("ps_scores", [P, 2, SEQ])
        ps_turned = mem.psum("ps_turned", [P, 2, SEQ])
        ps_out = mem.psum("ps_out", [P, GROUPS, ROWS])
        if rel:
            rel_k_t, rel_v, scratch = rel
            window_k = mem.sbuf("window_k", [P, PITCH])
            window_v = mem.sbuf("window_v", [P, KEY_TILES, ROWS, D_HEAD])
            shifted = [mem.sbuf(f"shifted{n}", [P, 2, PITCH]) for n in range(2)]
            rel_out = mem.sbuf("rel_out", [P, GROUPS, ROWS])
            ps_rel = mem.psum("ps_rel", [P, 2, SEQ])
            ps_rel_out = mem.psum("ps_rel_out", [P, ROWS // 4, TILES * 2])
        ident_zeroed = mem.sem("ident_zeroed")
        ident_ready = mem.sem("ident_ready")
        queries_zeroed = mem.sem("queries_zeroed")
        queries_in = mem.sem("queries_in")
        window_k_in = mem.sem("window_k_in")
        window_v_in = mem.sem("window_v_in")
        keys_in = mem.sem("keys_in")
        values_in = mem.sem("values_in")
        rel_product = mem.sem("rel_product")
        rel_copied = mem.sem("rel_copied")
        rel_stored = [mem.sem(f"rel_stored{n}") for n in range(2)]
        rel_in = [mem.sem(f"rel_in{n}") for n in range(2)]
        scored = mem.sem("scored")
        scores_read = mem.sem("scores_read")
        own_ready = mem.sem("own_ready")
        exps = mem.sem("exps")
        inverted = mem.sem("inverted")
        spread_ready = mem.sem("spread_ready")
        factors_ready = mem.sem("factors_ready")
        sums_ready = mem.sem("sums_ready")
        turned = mem.sem("turned")
        turned_copied = mem.sem("turned_copied")
        values_summed = mem.sem("values_summed")
        unit_done = mem.sem("unit_done")
        rel_out_act = mem.sem("rel_out_act")
        rel_out_dve = mem.sem("rel_out_dve")
        out_ready = mem.sem("out_ready")
        out_stored = mem.sem("out_stored")
        alone = mem.sem("alone")
        block = ctx.enter_context(nc.Block())

        LEAD = 4
        LAG = 2

        def relative_rows(sp, unit, row_block):
            for head in range(HEADS_PER_CHUNK):
                sp.dma_start(
                    window_k[D_HEAD * head:D_HEAD * (head + 1), 0:WINDOW],
                    by_partition(rel_k_t, SEQ - ROWS - row_block * ROWS,
                                 [[2 * SEQ - 1, D_HEAD], [1, WINDOW]])).then_inc(window_k_in, 16)
            for group in range(TILES // 2 + 1):
                if group == 2:
                    sp.wait_ge(unit_done, unit)
                    sp.dma_start(window_v[:, :, :, :],
                                 by_partition(rel_v, (SEQ - ROWS - row_block * ROWS) * D_HEAD,
                                              [[D_HEAD, P], [P * D_HEAD, KEY_TILES], [1, ROWS * D_HEAD]])
                                 ).then_inc(window_v_in, 16)
                if group < TILES // 2:
                    sp.wait_ge(rel_copied, TILES * unit + 2 * group + 2)
                    sp.dma_start(by_partition(scratch, 2 * group * P * PITCH,
                                              [[PITCH, P], [P * PITCH, 2], [1, WINDOW]]),
                                 shifted[group % 2][:, :, 0:WINDOW]).then_inc(rel_stored[group % 2], 16)
                if group > 0:
                    back = group - 1
                    sp.wait_ge(rel_stored[back % 2], 16 * (TILES // 4 * unit + back // 2 + 1))
                    stand(sp, alone)
                    sp.wait_ge(turned, TILES * unit + 2 * back + 2)
                    stand(sp, alone)
                    sp.wait_ge(rel_in[back % 2], 32 * (TILES // 4 * unit + back // 2))
                    for tile in range(2 * back, 2 * back + 2):
                        sp.dma_start(probs[:, tile, :],
                                     by_partition(scratch, tile * P * PITCH + ROWS - 1,
                                                  [[ROWS * PITCH, 2], [PITCH - 1, ROWS], [1, SEQ]])
                                     ).then_inc(rel_in[back % 2], 16)

        @block.sync
        def _(sp):
            sp.wait_ge(queries_zeroed, 1)
            with sp.Fori(0, UNITS // UNITS_PER_PAIR) as pair:
                sp.wait_ge(scored, TILES * UNITS_PER_PAIR * pair)
                sp.dma_start(keys[:, :, :, :],
                             by_partition(k_t, pair * (BATCHES_AT_ONCE * D_MODEL * SEQ),
                                          [[SEQ, P], [P * SEQ, GROUPS], [1, SEQ]])).then_inc(keys_in, 16)
                with sp.Fori(0, UNITS_PER_PAIR) as row_block:
                    unit = UNITS_PER_PAIR * pair + row_block
                    sp.wait_ge(scored, TILES * unit)
                    for head in range(HEADS_PER_CHUNK):
                        sp.dma_start(
                            queries[D_HEAD * head:D_HEAD * (head + 1), head // 2:TILES:2, head % 2, :],
                            by_partition(q_t, pair * (BATCHES_AT_ONCE * D_MODEL * SEQ) + row_block * ROWS
                                         + D_HEAD * head * SEQ,
                                         [[SEQ, D_HEAD], [P * SEQ, GROUPS], [1, ROWS]])).then_inc(queries_in, 16)
                    if rel:
                        relative_rows(sp, unit, row_block)

        @block.gpsimd
        def _(pool):
            nc.gpsimd.memset(queries[:, :, :, :], 0.0).then_inc(queries_zeroed, 1)
            identity_matrix(pool, nc, ident, ident_zeroed, ident_ready)
            nc.gpsimd.memset(own_head[:, :, :], 0.0).then_inc(ident_zeroed, 1)
            pool.wait_ge(ident_zeroed, 2)
            for h in range(2):
                nc.gpsimd.memset(own_head[ROWS * h:ROWS * (h + 1), h, :], 1.0).then_inc(own_ready, 1)
            pool.wait_ge(ident_ready, 1)
            pool.wait_ge(own_ready, 2)
            nc.gpsimd.tensor_tensor(own_row[:, :], ident[:, 0:ROWS], ident[:, ROWS:P], ALU.add).then_inc(own_ready, 1)
            with pool.Fori(0, UNITS // UNITS_PER_PAIR) as pair:
                pool.wait_ge(values_summed, UNITS_PER_PAIR * pair)
                for b in range(BATCHES_AT_ONCE):
                    pool.dma_start(values[:, :, b, :],
                                 by_partition(v, pair * (BATCHES_AT_ONCE * D_MODEL * SEQ) + b * SEQ * D_MODEL,
                                              [[D_MODEL, P], [P * D_MODEL, KEY_TILES], [1, D_MODEL]])
                                 ).then_inc(values_in, 16)
                with pool.Fori(0, UNITS_PER_PAIR) as row_block:
                    unit = UNITS_PER_PAIR * pair + row_block
                    pool.wait_ge(out_ready, unit + 1)
                    pool.dma_start(
                        by_partition(out_t, pair * (BATCHES_AT_ONCE * D_MODEL * SEQ) + row_block * ROWS,
                                     [[SEQ, P], [P * SEQ, GROUPS], [1, ROWS]]), out[:, :, :]).then_inc(out_stored, 16)
            pool.wait_ge(out_stored, 16 * UNITS)

        @block.tensor
        def _(pe):
            def relative_scores(unit, tile):
                pe.wait_ge(rel_copied, TILES * unit + tile)
                lhs = queries[:, tile, :, :]
                nc.tensor.matmul(ps_rel[:, 0, :], lhs, window_k[:, 0:SEQ], start=True, stop=True)
                nc.tensor.matmul(ps_rel[:, 1, 0:WINDOW - SEQ], lhs, window_k[:, SEQ:WINDOW],
                                 start=True, stop=True).then_inc(rel_product, 1)

            def scores(unit, tile):
                if tile == 0:
                    pe.wait_ge(out_ready, unit)
                pe.wait_ge(scores_read, TILES * unit + tile + 1)
                nc.tensor.matmul(ps_scores[:, tile % 2, :], queries[:, tile, :, :],
                                 keys[:, tile // (TILES // 2), tile // 2 % CHUNKS, :],
                                 start=True, stop=True).then_inc(scored, 1)

            def transpose(unit, tile):
                pe.wait_ge(exps, TILES * unit + tile + 1)
                pe.wait_ge(turned_copied, TILES * unit + tile + 1)
                for part in range(KEY_TILES):
                    last = nc.tensor.transpose(ps_turned[:, tile % 2, part * P:(part + 1) * P],
                                               probs[:, tile, part * P:(part + 1) * P], ident[:, :])
                last.then_inc(turned, 1)

            def values_product(group):
                b, chunk = group // CHUNKS, group % CHUNKS
                for part in range(KEY_TILES):
                    for head in range(HEADS_PER_CHUNK):
                        first = chunk * P + head * D_HEAD
                        last = nc.tensor.matmul(ps_out[D_HEAD * head:D_HEAD * (head + 1), group, :],
                                                values[:, part, b, first:first + D_HEAD],
                                                probs_t[:, part, 2 * group + head // 2, head % 2, :],
                                                start=(part == 0), stop=(part == KEY_TILES - 1))
                return last

            def factors():
                for group in range(GROUPS):
                    last = nc.tensor.matmul(ps_scores[:, 0, group * ROWS:(group + 1) * ROWS],
                                            spread[:, 2 * group:2 * group + 2, :, :], own_row[:, :],
                                            start=True, stop=True)
                return last

            def relative_values_product():
                for n in range(ROWS // 4):
                    for part in range(KEY_TILES):
                        for lane in range(4):
                            row = 4 * n + lane
                            last = nc.tensor.matmul(
                                ps_rel_out[D_HEAD * lane:D_HEAD * (lane + 1), n, :],
                                window_v[:, part, ROWS - 1 - row, :],
                                probs_t[:, part, :, :, row], start=(part == 0), stop=(part == KEY_TILES - 1))
                return last

            def unit_program(unit, has_next):
                for tile in range(TILES + LAG):
                    if rel and tile + LEAD < TILES:
                        relative_scores(unit, tile + LEAD)
                    if tile < TILES:
                        scores(unit, tile)
                    if tile >= LAG:
                        transpose(unit, tile - LAG)
                pe.wait_ge(turned_copied, TILES * (unit + 1) + 2)
                pe.wait_ge(out_ready, unit)
                if rel and has_next:
                    pe.wait_ge(queries_in, 16 * HEADS_PER_CHUNK * (unit + 2))
                    pe.wait_ge(window_k_in, 16 * HEADS_PER_CHUNK * (unit + 2))
                for group in range(GROUPS):
                    last = values_product(group)
                    if rel and has_next and group % 2 == 1 and group // 2 < LEAD:
                        relative_scores(unit + 1, group // 2)
                last.then_inc(values_summed, 1)
                pe.wait_ge(spread_ready, unit + 1)
                factors().then_inc(factors_ready, 1)
                if rel:
                    pe.wait_ge(window_v_in, 16 * (unit + 1))
                    pe.wait_ge(rel_out_act, 8 * unit)
                    pe.wait_ge(rel_out_dve, 8 * unit)
                    relative_values_product().then_inc(unit_done, 1)

            pe.wait_ge(ident_ready, 1)
            pe.wait_ge(own_ready, 3)
            pe.wait_ge(queries_in, 16 * HEADS_PER_CHUNK)
            if rel:
                pe.wait_ge(window_k_in, 16 * HEADS_PER_CHUNK)
                for tile in range(LEAD):
                    relative_scores(0, tile)
            with pe.Fori(0, UNITS - 1) as unit:
                pe.wait_ge(keys_in, 16 * (unit // UNITS_PER_PAIR + 1))
                pe.wait_ge(values_in, 16 * BATCHES_AT_ONCE * (unit // UNITS_PER_PAIR + 1))
                if not rel:
                    pe.wait_ge(queries_in, 16 * HEADS_PER_CHUNK * (unit + 1))
                unit_program(unit, True)
            if not rel:
                pe.wait_ge(queries_in, 16 * HEADS_PER_CHUNK * UNITS)
            unit_program(UNITS - 1, False)

        def relative_out(head, lane):
            return (rel_out[D_HEAD * head:D_HEAD * (head + 1), :, lane:ROWS:4],
                    ps_rel_out[D_HEAD * lane:D_HEAD * (lane + 1), :, head:TILES * 2:HEADS_PER_CHUNK]
                    .rearrange("p n g -> p g n"))

        @block.scalar
        def _(act):
            def copy_relative_scores(unit, tile):
                act.wait_ge(rel_product, TILES * unit + tile + 1)
                if tile % 2 == 0:
                    act.wait_ge(rel_stored[tile // 2 % 2], 16 * (TILES // 4 * unit + tile // 4))
                nc.scalar.activation(shifted[tile // 2 % 2][:, tile % 2, 0:WINDOW],
                                     ps_rel[:, :, :].rearrange("p b n -> p (b n)")[:, 0:WINDOW],
                                     ACT.Copy).then_inc(rel_copied, 1)

            def unit_program(unit, has_next):
                for tile in range(TILES):
                    if rel and tile + LEAD < TILES:
                        copy_relative_scores(unit, tile + LEAD)
                    act.wait_ge(scores_read, TILES * unit + tile + 3)
                    nc.scalar.activation(probs[:, tile, :], probs[:, tile, :], ACT.Exp, bias=low[:, tile:tile + 1],
                                         scale=-1.0, accum_out=total[:, tile:tile + 1]).then_inc(exps, 1)
                if rel and has_next:
                    for tile in range(LEAD):
                        copy_relative_scores(unit + 1, tile)
                if rel:
                    act.wait_ge(unit_done, unit + 1)
                    act.wait_ge(out_ready, unit)
                    for head in range(HEADS_PER_CHUNK):
                        for lane in range(2):
                            nc.scalar.activation(*relative_out(head, lane), ACT.Copy).then_inc(rel_out_act, 1)

            if rel:
                for tile in range(LEAD):
                    copy_relative_scores(0, tile)
            with act.Fori(0, UNITS - 1) as unit:
                unit_program(unit, True)
            unit_program(UNITS - 1, False)

        @block.vector
        def _(dve):
            dve.sem_inc(scores_read, 2)
            dve.sem_inc(turned_copied, 2)
            dve.sem_inc(turned, TILES)
            dve.wait_ge(own_ready, 3)
            with dve.Fori(0, UNITS) as unit:
                for tile in range(TILES + LAG):
                    if tile < TILES:
                        dve.wait_ge(scored, TILES * unit + tile + 1)
                        if rel:
                            if tile % 2 == 0:
                                dve.wait_ge(rel_in[tile // 2 % 2], 32 * (TILES // 4 * unit + tile // 4 + 1))
                            stand(dve, alone)
                            nc.vector.tensor_tensor_reduce(
                                out=probs[:, tile, :], in0=ps_scores[:, tile % 2, :], in1=probs[:, tile, :],
                                scale=-1.0, scalar=BIG, op0=ALU.add, op1=ALU.min,
                                accum_out=low[:, tile:tile + 1]).then_inc(scores_read, 1)
                        else:
                            dve.wait_ge(turned, TILES * unit + tile + 1)
                            nc.vector.tensor_scalar(
                                probs[:, tile, :], ps_scores[:, tile % 2, :], -1.0, BIG, ALU.mult, ALU.min,
                                accum_out=low[:, tile:tile + 1]).then_inc(scores_read, 1)
                    if tile >= LAG:
                        done = tile - LAG
                        if done == 0:
                            dve.wait_ge(unit_done if rel else values_summed, unit)
                        dve.wait_ge(turned, TILES * (unit + 1) + done + 1)
                        nc.vector.tensor_copy(
                            probs_t[:, :, done, :, :].rearrange("p k h r -> p k (h r)"),
                            ps_turned[:, done % 2, :].rearrange("p (k r) -> p k r", k=KEY_TILES)
                        ).then_inc(turned_copied, 1)
                    if tile == TILES:
                        dve.wait_ge(exps, TILES * (unit + 1))
                        nc.vector.reciprocal(inverse[:, :], total[:, :]).then_inc(inverted, 1)
                        dve.wait_ge(inverted, unit + 1)
                        dve.wait_ge(factors_ready, unit)
                        nc.vector.tensor_tensor(
                            spread[:, :, :, :].rearrange("p t h d -> p t (h d)"),
                            own_head[:, :, :].rearrange("p h d -> p (h d)").unsqueeze(1).to_broadcast(
                                [P, TILES, 2 * D_HEAD]),
                            inverse[:, :].unsqueeze(2).to_broadcast([P, TILES, 2 * D_HEAD]),
                            ALU.mult).then_inc(spread_ready, 1)
                dve.wait_ge(values_summed, unit + 1)
                dve.wait_ge(out_ready, unit)
                if rel:
                    dve.wait_ge(unit_done, unit + 1)
                    for head in range(HEADS_PER_CHUNK):
                        for lane in range(2, 4):
                            nc.vector.tensor_copy(*relative_out(head, lane)).then_inc(rel_out_dve, 1)
                    dve.wait_ge(rel_out_act, 8 * (unit + 1))
                    dve.wait_ge(rel_out_dve, 8 * (unit + 1))
                    nc.vector.tensor_tensor(sums[:, :, :], ps_out[:, :, :], rel_out[:, :, :],
                                            ALU.add).then_inc(sums_ready, 1)
                else:
                    nc.vector.tensor_copy(sums[:, :, :], ps_out[:, :, :]).then_inc(sums_ready, 1)
                dve.wait_ge(sums_ready, unit + 1)
                dve.wait_ge(factors_ready, unit + 1)
                dve.wait_ge(out_stored, 16 * unit)
                nc.vector.tensor_tensor(out[:, :, :], ps_scores[:, 0, :].rearrange("p (g r) -> p g r", g=GROUPS),
                                        sums[:, :, :], ALU.mult).then_inc(out_ready, 1)


def finish(nc, stage, a_t, w, bias, residual, out, out_t=None):
    turns = BATCH // 2
    tiles = TOK_TILES
    with ExitStack() as ctx:
        mem = Memory(nc, ctx, f"{stage}_finish")
        ident = mem.sbuf("ident", [P, P])
        weights = mem.sbuf("weights", [P, CHUNKS, D_MODEL])
        bias_all = mem.sbuf("bias_all", [P, D_MODEL])
        eps = mem.sbuf("eps", [P, 1])
        src = [mem.sbuf(f"src{n}", [P, CHUNKS, SEQ]) for n in range(2)]
        res = [mem.sbuf(f"res{n}", [P, tiles, D_MODEL]) for n in range(2)]
        stats = [mem.sbuf(f"stats{n}", [P, tiles, 6]) for n in range(2)]
        moments = [mem.sbuf(f"moments{n}", [P, tiles, 2]) for n in range(2)]
        deviation = [mem.sbuf(f"deviation{n}", [P, tiles]) for n in range(2)]
        factor = [mem.sbuf(f"factor{n}", [P, tiles]) for n in range(2)]
        turned_out = [mem.sbuf(f"turned_out{n}", [P, CHUNKS, SEQ]) for n in range(2)]
        ps = mem.psum("ps", [P, tiles, D_MODEL])
        ps_turned = mem.psum("ps_turned", [P, 2, D_MODEL])
        weights_in = mem.sem("weights_in")
        src_in = [mem.sem(f"src_in{n}") for n in range(2)]
        ident_zeroed = mem.sem("ident_zeroed")
        ident_ready = mem.sem("ident_ready")
        biased = mem.sem("biased")
        product = mem.sem("product")
        summed = mem.sem("summed")
        stats_ready = mem.sem("stats_ready")
        moments_ready = mem.sem("moments_ready")
        deviation_ready = mem.sem("deviation_ready")
        factor_ready = mem.sem("factor_ready")
        normalised = mem.sem("normalised")
        turned = mem.sem("turned")
        turned_copied = mem.sem("turned_copied")
        stored = [mem.sem(f"stored{n}") for n in range(2)]
        turned_stored = [mem.sem(f"turned_stored{n}") for n in range(2)]
        alone = mem.sem("alone")
        block = ctx.enter_context(nc.Block())

        @block.sync
        def _(sp):
            sp.dma_start(weights[:, :, :], w.rearrange("(r p) n -> p r n", p=P)).then_inc(weights_in, 16)
            sp.dma_start(bias_all[:, :], by_partition(bias, 0, [[0, P], [1, D_MODEL]])).then_inc(weights_in, 16)
            with sp.Fori(0, turns) as turn:
                for half in range(2):
                    sp.wait_ge(summed, tiles * (2 * turn + half))
                    sp.dma_start(src[half][:, :, :],
                                 a_t[2 * turn + half].rearrange("(r p) t -> p r t", p=P)).then_inc(src_in[half], 16)
                    sp.wait_ge(stored[half], 16 * turn)
                    stand(sp, alone)
                    if out_t is not None:
                        sp.wait_ge(turned, 2 * tiles * turn)
                    sp.dma_start(res[half][:, :, :],
                                 residual[2 * turn + half].rearrange("(t p) n -> p t n", p=P)).then_inc(src_in[half], 16)

        @block.gpsimd
        def _(pool):
            identity_matrix(pool, nc, ident, ident_zeroed, ident_ready)
            pool.wait_ge(weights_in, 32)
            with pool.Fori(0, turns) as turn:
                for half in range(2):
                    pool.wait_ge(src_in[half], 32 * (turn + 1))
                    for tile in range(tiles):
                        nc.gpsimd.tensor_tensor(res[half][:, tile, :], res[half][:, tile, :], bias_all[:, :],
                                                ALU.add).then_inc(biased, 1)

        @block.tensor
        def _(pe):
            pe.wait_ge(weights_in, 32)
            pe.wait_ge(ident_ready, 1)
            with pe.Fori(0, turns) as turn:
                for half in range(2):
                    pe.wait_ge(src_in[half], 32 * (turn + 1))
                    for tile in range(tiles):
                        pe.wait_ge(summed, tiles * (2 * turn + half) + tile + 1)
                        for r in range(CHUNKS):
                            last = nc.tensor.matmul(ps[:, tile, :], src[half][:, r, tile * P:(tile + 1) * P],
                                                    weights[:, r, :], start=(r == 0), stop=(r == CHUNKS - 1))
                        last.then_inc(product, 1)
                if out_t is not None:
                    for half in range(2):
                        for tile in range(tiles):
                            number = tiles * (2 * turn + half) + tile
                            pe.wait_ge(normalised, number + 1)
                            pe.wait_ge(turned_copied, number + 1)
                            for chunk in range(CHUNKS):
                                last = nc.tensor.transpose(ps_turned[:, tile % 2, chunk * P:(chunk + 1) * P],
                                                           res[half][:, tile, chunk * P:(chunk + 1) * P], ident[:, :])
                            last.then_inc(turned, 1)

        @block.scalar
        def _(act):
            act.wait_ge(summed, tiles)
            with act.Fori(0, turns) as turn:
                for half in range(2):
                    act.wait_ge(moments_ready, tiles * (2 * turn + half + 1))
                    nc.scalar.activation(deviation[half][:, :], moments[half][:, :, 1], ACT.Sqrt,
                                         bias=eps[:, :]).then_inc(deviation_ready, 1)
                    act.wait_ge(normalised, tiles * (2 * turn + half + 1))
                    act.dma_start(out[2 * turn + half].rearrange("(t p) n -> p t n", p=P),
                                  res[half][:, :, :]).then_inc(stored[half], 16)
                if out_t is not None:
                    for half in range(2):
                        act.wait_ge(turned_stored[half], 16 * turn)
                        for tile in range(tiles):
                            act.wait_ge(turned, tiles * (2 * turn + half) + tile + 1)
                            nc.scalar.activation(
                                turned_out[half][:, :, tile * P:(tile + 1) * P],
                                ps_turned[:, tile % 2, :].rearrange("p (c t) -> p c t", c=CHUNKS),
                                ACT.Copy).then_inc(turned_copied, 1)
                        act.wait_ge(turned_copied, tiles * (2 * turn + half + 1) + 2)
                        act.dma_start(out_t[2 * turn + half].rearrange("(c p) t -> p c t", p=P),
                                      turned_out[half][:, :, :]).then_inc(turned_stored[half], 16)
            for half in range(2):
                act.wait_ge(stored[half], 16 * turns)
                if out_t is not None:
                    act.wait_ge(turned_stored[half], 16 * turns)

        @block.vector
        def _(dve):
            nc.vector.memset(eps[:, :], LN_EPS).then_inc(summed, tiles)
            if out_t is not None:
                dve.sem_inc(turned_copied, 2)
            with dve.Fori(0, turns) as turn:
                for half in range(2):
                    batch = 2 * turn + half
                    for tile in range(tiles):
                        number = tiles * batch + tile
                        dve.wait_ge(product, number + 1)
                        dve.wait_ge(biased, number + 1)
                        nc.vector.tensor_tensor(res[half][:, tile, :], ps[:, tile, :], res[half][:, tile, :],
                                                ALU.add).then_inc(summed, 1)
                        dve.wait_ge(summed, number + 1 + tiles)
                        nc.vector.bn_stats(stats[half][:, tile, :], res[half][:, tile, :]).then_inc(stats_ready, 1)
                        dve.wait_ge(stats_ready, number + 1)
                        stand(dve, alone)
                        nc.vector.bn_aggr(moments[half][:, tile, :], stats[half][:, tile, :]).then_inc(moments_ready, 1)
                    dve.wait_ge(deviation_ready, batch + 1)
                    nc.vector.reciprocal(factor[half][:, :], deviation[half][:, :]).then_inc(factor_ready, 1)
                    dve.wait_ge(factor_ready, batch + 1)
                    for tile in range(tiles):
                        nc.vector.tensor_scalar(res[half][:, tile, :], res[half][:, tile, :],
                                                moments[half][:, tile, 0:1], factor[half][:, tile:tile + 1],
                                                ALU.subtract, ALU.mult).then_inc(normalised, 1)


EXPERTS, SUB, HIDDEN = 16, 64, 256
PARTS = D_MODEL // SUB
TOKEN_TILES = BATCH * TOK_TILES
COLUMNS = TOKEN_TILES * PARTS
ROWS_AT_ONCE = 512
BLOCKS = (2 * BATCH * SEQ * PARTS + EXPERTS * (ROWS_AT_ONCE - 1)) // ROWS_AT_ONCE + 1
BF16 = mybir.dt.bfloat16


def feed_forward(nc, x_t, w_m, b_m, expert_emb, w_1, b_1, w_2, b_2, hidden, rows_in, rows_out, mixed_t):
    assert BLOCKS % 2 == 0
    with ExitStack() as ctx:
        mem = Memory(nc, ctx, "moe")
        weight = [mem.sbuf(f"weight{n}", [P, COLUMNS]) for n in range(2)]
        place = [mem.sbuf(f"place{n}", [P, COLUMNS], I32) for n in range(2)]
        block_expert = mem.sbuf("block_expert", [P, BLOCKS], I32)
        route(nc, x_t, w_m, b_m, expert_emb, rows_in, hidden, weight, place, block_expert)
        dispatch(nc, hidden, place, rows_in)
        run_experts(nc, w_1, b_1, w_2, b_2, block_expert, rows_in, rows_out)
        collect(nc, place, weight, rows_out, mixed_t)


def route(nc, x_t, w_m, b_m, expert_emb, rows_in, hidden, weight, place, block_expert):
    per_batch = TOK_TILES * PARTS
    turns = BATCH // 2
    zero_len = 2048
    with ExitStack() as ctx:
        mem = Memory(nc, ctx, "route")
        ident = mem.sbuf("ident", [P, P])
        weights = mem.sbuf("weights", [P, CHUNKS, D_MODEL])
        bias_all = mem.sbuf("bias_all", [P, D_MODEL])
        emb = mem.sbuf("emb", [P, 2, EXPERTS])
        zeros = mem.sbuf("zeros", [P, zero_len])
        src = [mem.sbuf(f"src{n}", [P, CHUNKS, SEQ]) for n in range(2)]
        hid = [mem.sbuf(f"hid{n}", [P, TOK_TILES, D_MODEL]) for n in range(2)]
        hid_t = [mem.sbuf(f"hid_t{n}", [P, CHUNKS, P]) for n in range(2)]
        steps_int = mem.sbuf("steps_int", [P, BLOCKS], I32)
        steps = mem.sbuf("steps", [P, BLOCKS])
        limits = mem.sbuf("limits", [P, COLUMNS // 4])
        countdown = mem.sbuf("countdown", [P, EXPERTS])
        best = mem.sbuf("best", [P, per_batch])
        second = mem.sbuf("second", [P, per_batch])
        picked = mem.sbuf("picked", [P, per_batch])
        gap = mem.sbuf("gap", [P, per_batch])
        gap_exp = mem.sbuf("gap_exp", [P, per_batch])
        exp_sum = mem.sbuf("exp_sum", [P, per_batch])
        inverse = mem.sbuf("inverse", [P, per_batch])
        work = mem.sbuf("work", [P, per_batch, EXPERTS])
        logits = mem.sbuf("logits", [P, per_batch, EXPERTS])
        exps = mem.sbuf("exps", [P, per_batch, EXPERTS])
        chosen = [mem.sbuf(f"chosen{n}", [P, COLUMNS, EXPERTS], BF16) for n in range(2)]
        mask = mem.sbuf("mask", [P, COLUMNS, EXPERTS], BF16)
        before = mem.sbuf("before", [P, P], BF16)
        ones = mem.sbuf("ones", [P, P], BF16)
        rank = mem.sbuf("rank", [P, COLUMNS, EXPERTS])
        counts = mem.sbuf("counts", [P, EXPERTS, COLUMNS])
        until = mem.sbuf("until", [P, EXPERTS, COLUMNS])
        carry = mem.sbuf("carry", [P, EXPERTS, COLUMNS])
        over = mem.sbuf("over", [P, EXPERTS * BLOCKS])
        blocks = mem.sbuf("blocks", [P, EXPERTS])
        blocks_until = mem.sbuf("blocks_until", [P, EXPERTS])
        first_row = mem.sbuf("first_row", [P, EXPERTS])
        place_float = mem.sbuf("place_float", [P, COLUMNS])
        expert_float = mem.sbuf("expert_float", [P, BLOCKS])
        ps = mem.psum("ps", [P, TOK_TILES, D_MODEL])
        ps_turned = mem.psum("ps_turned", [P, 2, D_MODEL])
        ps_logits = mem.psum("ps_logits", [P, per_batch, EXPERTS])
        weights_in = mem.sem("weights_in")
        emb_zeroed = mem.sem("emb_zeroed")
        emb_in = mem.sem("emb_in")
        zeroed = mem.sem("zeroed")
        rows_zeroed = mem.sem("rows_zeroed")
        src_in = [mem.sem(f"src_in{n}") for n in range(2)]
        ident_zeroed = mem.sem("ident_zeroed")
        ident_ready = mem.sem("ident_ready")
        masks_ready = mem.sem("masks_ready")
        product = mem.sem("product")
        summed = mem.sem("summed")
        stored = [mem.sem(f"stored{n}") for n in range(2)]
        turned = mem.sem("turned")
        turned_copied = mem.sem("turned_copied")
        scored = mem.sem("scored")
        logits_read = mem.sem("logits_read")
        chain = mem.sem("chain")
        shifted = mem.sem("shifted")
        exps_ready = mem.sem("exps_ready")
        gap_ready = mem.sem("gap_ready")
        gap_exp_ready = mem.sem("gap_exp_ready")
        mask_ready = mem.sem("mask_ready")
        counted = mem.sem("counted")
        rank_copied = mem.sem("rank_copied")
        counts_copied = mem.sem("counts_copied")
        block = ctx.enter_context(nc.Block())

        @block.sync
        def _(sp):
            sp.dma_start(weights[:, :, :], w_m.rearrange("(r p) n -> p r n", p=P)).then_inc(weights_in, 16)
            sp.dma_start(bias_all[:, :], by_partition(b_m, 0, [[0, P], [1, D_MODEL]])).then_inc(weights_in, 16)
            sp.wait_ge(emb_zeroed, 1)
            for part in range(2):
                sp.dma_start(emb[SUB * part:SUB * (part + 1), part, :], expert_emb).then_inc(emb_in, 16)
            with sp.Fori(0, turns) as turn:
                for half in range(2):
                    sp.wait_ge(product, 2 * TOK_TILES * turn)
                    sp.dma_start(src[half][:, :, :],
                                 x_t[2 * turn + half].rearrange("(r p) t -> p r t", p=P)).then_inc(src_in[half], 16)
            sp.wait_ge(zeroed, 1)
            repeats = BLOCKS * ROWS_AT_ONCE * SUB // P // zero_len
            sp.dma_start(by_partition(rows_in, 0, [[repeats * zero_len, P], [zero_len, repeats], [1, zero_len]]),
                         zeros[:, :].unsqueeze(1).to_broadcast([P, repeats, zero_len])).then_inc(rows_zeroed, 16)
            sp.wait_ge(rows_zeroed, 16)

        @block.gpsimd
        def _(pool):
            nc.gpsimd.memset(emb[:, :, :], 0.0).then_inc(emb_zeroed, 1)
            nc.gpsimd.memset(zeros[:, :], 0.0).then_inc(zeroed, 1)
            identity_matrix(pool, nc, ident, ident_zeroed, ident_ready)
            nc.gpsimd.memset(before[:, :], 0.0).then_inc(masks_ready, 1)
            nc.gpsimd.memset(ones[:, :], 1.0).then_inc(masks_ready, 1)
            nc.gpsimd.iota(steps_int[:, :], pattern=[[1, BLOCKS]], base=0, channel_multiplier=0).then_inc(masks_ready, 1)
            pool.wait_ge(masks_ready, 3)
            nc.gpsimd.affine_select(out=before[:, :], in_=before[:, :], compare_op=ALU.is_ge, fill=1.0, base=0,
                                    pattern=[[-1, P]], channel_multiplier=1).then_inc(masks_ready, 1)

        @block.tensor
        def _(pe):
            def hidden_product(batch, half, tile):
                pe.wait_ge(summed, TOK_TILES * batch + tile + 1)
                for r in range(CHUNKS):
                    last = nc.tensor.matmul(ps[:, tile, :], src[half][:, r, tile * P:(tile + 1) * P],
                                            weights[:, r, :], start=(r == 0), stop=(r == CHUNKS - 1))
                last.then_inc(product, 1)

            def transpose(batch, half, tile):
                pe.wait_ge(summed, TOK_TILES * (batch + 1) + tile + 1)
                pe.wait_ge(turned_copied, TOK_TILES * batch + tile + 1)
                for chunk in range(CHUNKS):
                    last = nc.tensor.transpose(ps_turned[:, tile % 2, chunk * P:(chunk + 1) * P],
                                               hid[half][:, tile, chunk * P:(chunk + 1) * P], ident[:, :])
                last.then_inc(turned, 1)

            def logits_product(batch, tile):
                if tile == 0:
                    pe.wait_ge(logits_read, batch)
                pe.wait_ge(turned_copied, TOK_TILES * batch + tile + 3)
                for chunk in range(CHUNKS):
                    first = tile * PARTS + 2 * chunk
                    last = nc.tensor.matmul(ps_logits[:, first:first + 2, :], hid_t[tile % 2][:, chunk, :],
                                            emb[:, :, :], start=True, stop=True)
                last.then_inc(scored, 1)

            pe.wait_ge(weights_in, 32)
            pe.wait_ge(ident_ready, 1)
            pe.wait_ge(emb_in, 32)
            with pe.Fori(0, turns) as turn:
                for half in range(2):
                    batch = 2 * turn + half
                    pe.wait_ge(src_in[half], 16 * (turn + 1))
                    for tile in range(TOK_TILES + 2):
                        if tile < TOK_TILES:
                            hidden_product(batch, half, tile)
                        if 1 <= tile <= TOK_TILES:
                            transpose(batch, half, tile - 1)
                        if tile >= 2:
                            logits_product(batch, tile - 2)
            pe.wait_ge(masks_ready, 4)
            pe.wait_ge(mask_ready, BATCH)
            with pe.Fori(0, BATCH) as batch:
                pe.wait_ge(rank_copied, batch)
                pe.wait_ge(counts_copied, batch)
                chose = mask[:, bass.ds(per_batch * batch, per_batch), :].rearrange("p c e -> p (c e)")
                nc.tensor.matmul(ps_turned[:, 0, :], before[:, :], chose, start=True, stop=True)
                nc.tensor.matmul(ps_turned[:, 1, :], ones[:, :], chose, start=True, stop=True).then_inc(counted, 1)

        @block.scalar
        def _(act):
            with act.Fori(0, turns) as turn:
                for half in range(2):
                    batch = 2 * turn + half
                    for tile in range(TOK_TILES):
                        act.wait_ge(turned, TOK_TILES * batch + tile + 1)
                        act.wait_ge(scored, TOK_TILES * batch + tile + 1)
                        nc.scalar.activation(hid_t[tile % 2][:, :, :].rearrange("p c t -> p (c t)"),
                                             ps_turned[:, tile % 2, :], ACT.Copy).then_inc(turned_copied, 1)
                    act.wait_ge(summed, TOK_TILES * (batch + 2))
                    act.dma_start(hidden[batch].rearrange("(t p) n -> p t n", p=P),
                                  hid[half][:, :, :]).then_inc(stored[half], 16)
                    act.wait_ge(shifted, batch + 1)
                    nc.scalar.activation(exps[:, :, :], work[:, :, :], ACT.Exp).then_inc(exps_ready, 1)
                    act.wait_ge(gap_ready, batch + 1)
                    nc.scalar.activation(gap_exp[:, :], gap[:, :], ACT.Exp).then_inc(gap_exp_ready, 1)
            with act.Fori(0, BATCH) as batch:
                act.wait_ge(counted, batch + 1)
                nc.scalar.activation(rank[:, bass.ds(per_batch * batch, per_batch), :].rearrange("p c e -> p (c e)"),
                                     ps_turned[:, 0, :], ACT.Copy).then_inc(rank_copied, 1)
            for half in range(2):
                act.wait_ge(stored[half], 16 * turns)

        @block.vector
        def _(dve):
            setup_steps, batch_steps = 4, 13

            def over_experts(ap, count):
                return ap.unsqueeze(2).to_broadcast([P, count, EXPERTS])

            def over_columns(ap, count):
                return ap.unsqueeze(1).to_broadcast([P, count, EXPERTS])

            def choose(values, top, batch, out, number):
                nc.vector.tensor_tensor(work[:, :, :], values, over_experts(top, per_batch),
                                        ALU.is_equal).then_inc(chain, 1)
                dve.wait_ge(chain, number + 1)
                nc.vector.tensor_tensor(work[:, :, :], work[:, :, :], over_columns(countdown[:, :], per_batch),
                                        ALU.mult).then_inc(chain, 1)
                dve.wait_ge(chain, number + 2)
                nc.vector.tensor_reduce(picked[:, :], work[:, :, :], AX_X, ALU.max).then_inc(chain, 1)
                dve.wait_ge(chain, number + 3)
                nc.vector.tensor_tensor(out[:, bass.ds(per_batch * batch, per_batch), :],
                                        over_columns(countdown[:, :], per_batch),
                                        over_experts(picked[:, :], per_batch), ALU.is_equal).then_inc(chain, 1)
                dve.wait_ge(chain, number + 4)

            dve.sem_inc(turned_copied, 2)
            dve.sem_inc(scored, 2)
            dve.sem_inc(summed, TOK_TILES)
            dve.wait_ge(masks_ready, 3)
            nc.vector.tensor_copy(steps[:, :], steps_int[:, :]).then_inc(chain, 1)
            nc.vector.memset(carry[:, :, :], 1.0).then_inc(chain, 1)
            dve.wait_ge(chain, 2)
            nc.vector.tensor_scalar(countdown[:, :], steps[:, 0:EXPERTS], -1.0, float(EXPERTS),
                                    ALU.mult, ALU.add).then_inc(chain, 1)
            nc.vector.memset(carry[:, :, 0:1], 0.0).then_inc(chain, 1)
            dve.wait_ge(chain, setup_steps)
            dve.wait_ge(weights_in, 32)
            with dve.Fori(0, turns) as turn:
                for half in range(2):
                    batch = 2 * turn + half
                    number = setup_steps + batch_steps * batch
                    dve.wait_ge(stored[half], 16 * turn)
                    for tile in range(TOK_TILES):
                        dve.wait_ge(product, TOK_TILES * batch + tile + 1)
                        nc.vector.tensor_tensor(hid[half][:, tile, :], ps[:, tile, :], bias_all[:, :],
                                                ALU.add).then_inc(summed, 1)
                    dve.wait_ge(scored, TOK_TILES * (batch + 1) + 2)
                    nc.vector.tensor_copy(logits[:, :, :], ps_logits[:, :, :]).then_inc(logits_read, 1)
                    dve.wait_ge(logits_read, batch + 1)
                    nc.vector.tensor_reduce(best[:, :], logits[:, :, :], AX_X, ALU.max).then_inc(chain, 1)
                    dve.wait_ge(chain, number + 1)
                    nc.vector.tensor_tensor(work[:, :, :], logits[:, :, :], over_experts(best[:, :], per_batch),
                                            ALU.subtract).then_inc(shifted, 1)
                    dve.wait_ge(exps_ready, batch + 1)
                    choose(logits[:, :, :], best[:, :], batch, chosen[0], number + 1)
                    nc.vector.scalar_tensor_tensor(
                        logits[:, :, :], chosen[0][:, bass.ds(per_batch * batch, per_batch), :], -BIG,
                        logits[:, :, :], ALU.mult, ALU.add).then_inc(chain, 1)
                    dve.wait_ge(chain, number + 6)
                    nc.vector.tensor_reduce(second[:, :], logits[:, :, :], AX_X, ALU.max).then_inc(chain, 1)
                    dve.wait_ge(chain, number + 7)
                    nc.vector.tensor_tensor(gap[:, :], second[:, :], best[:, :], ALU.subtract).then_inc(gap_ready, 1)
                    choose(logits[:, :, :], second[:, :], batch, chosen[1], number + 7)
                    nc.vector.tensor_tensor(mask[:, bass.ds(per_batch * batch, per_batch), :],
                                            chosen[0][:, bass.ds(per_batch * batch, per_batch), :],
                                            chosen[1][:, bass.ds(per_batch * batch, per_batch), :],
                                            ALU.add).then_inc(mask_ready, 1)
                    nc.vector.tensor_reduce(exp_sum[:, :], exps[:, :, :], AX_X, ALU.add).then_inc(chain, 1)
                    dve.wait_ge(chain, number + 12)
                    nc.vector.reciprocal(weight[0][:, bass.ds(per_batch * batch, per_batch)],
                                         exp_sum[:, :]).then_inc(chain, 1)
                    dve.wait_ge(chain, number + 13)
                    dve.wait_ge(gap_exp_ready, batch + 1)
                    nc.vector.tensor_tensor(weight[1][:, bass.ds(per_batch * batch, per_batch)], gap_exp[:, :],
                                            weight[0][:, bass.ds(per_batch * batch, per_batch)], ALU.mult)
            with dve.Fori(0, BATCH) as batch:
                dve.wait_ge(counted, batch + 1)
                nc.vector.tensor_copy(counts[:, :, bass.ds(per_batch * batch, per_batch)],
                                      ps_turned[:, 1, :].rearrange("p (c e) -> p e c", e=EXPERTS)
                                      ).then_inc(counts_copied, 1)
            dve.wait_ge(counts_copied, BATCH)

            done = [setup_steps + batch_steps * BATCH]

            def then(instruction):
                done[0] += 1
                instruction.then_inc(chain, 1)
                dve.wait_ge(chain, done[0])

            flat = "p e c -> p (e c)"
            then(nc.vector.tensor_tensor_scan(until[:, :, :].rearrange(flat), carry[:, :, :].rearrange(flat),
                                              counts[:, :, :].rearrange(flat), 0.0, ALU.mult, ALU.add))
            then(nc.vector.tensor_tensor(counts[:, :, :].rearrange(flat), until[:, :, :].rearrange(flat),
                                         counts[:, :, :].rearrange(flat), ALU.subtract))
            most = COLUMNS // 4
            then(nc.vector.tensor_scalar(limits[:, :], steps[:, 0:most], float(ROWS_AT_ONCE), None, ALU.mult))
            is_over = over[:, 0:EXPERTS * most].rearrange("p (e k) -> p e k", e=EXPERTS)
            then(nc.vector.tensor_tensor(is_over, until[:, :, COLUMNS - 1:COLUMNS].to_broadcast([P, EXPERTS, most]),
                                         limits[:, :].unsqueeze(1).to_broadcast([P, EXPERTS, most]), ALU.is_gt))
            then(nc.vector.tensor_reduce(blocks[:, :], is_over, AX_X, ALU.add))
            then(nc.vector.tensor_tensor_scan(blocks_until[:, :], carry[:, 0, 1:EXPERTS + 1], blocks[:, :], 0.0,
                                              ALU.mult, ALU.add))
            then(nc.vector.tensor_tensor(first_row[:, :], blocks_until[:, :], blocks[:, :], ALU.subtract))
            then(nc.vector.tensor_scalar(first_row[:, :], first_row[:, :], float(ROWS_AT_ONCE), None, ALU.mult))
            then(nc.vector.tensor_tensor(counts[:, :, :], counts[:, :, :],
                                         first_row[:, :].unsqueeze(2).to_broadcast([P, EXPERTS, COLUMNS]), ALU.add))
            dve.wait_ge(rank_copied, BATCH)
            then(nc.vector.tensor_tensor(rank[:, :, :], rank[:, :, :], counts[:, :, :].rearrange("p e c -> p c e"),
                                         ALU.add))
            by_column = until[:, :, :].rearrange(flat).rearrange("p (c e) -> p c e", e=EXPERTS)
            for n in range(2):
                then(nc.vector.tensor_tensor(by_column, rank[:, :, :], chosen[n][:, :, :], ALU.mult))
                then(nc.vector.tensor_reduce(place_float[:, :], by_column, AX_X, ALU.add))
                then(nc.vector.tensor_copy(place[n][:, :], place_float[:, :]))
            is_past = over[:, :].rearrange("p (b e) -> p b e", e=EXPERTS)
            then(nc.vector.tensor_tensor(is_past, steps[:, :].unsqueeze(2).to_broadcast([P, BLOCKS, EXPERTS]),
                                         blocks_until[:, :].unsqueeze(1).to_broadcast([P, BLOCKS, EXPERTS]),
                                         ALU.is_ge))
            then(nc.vector.tensor_reduce(expert_float[:, :], is_past, AX_X, ALU.add))
            then(nc.vector.tensor_scalar(expert_float[:, :], expert_float[:, :], float(EXPERTS - 1), None, ALU.min))
            then(nc.vector.tensor_copy(block_expert[:, :], expert_float[:, :]))


def dispatch(nc, hidden, place, rows_in):
    turns = TOKEN_TILES // 2
    with ExitStack() as ctx:
        mem = Memory(nc, ctx, "dispatch")
        tokens = [mem.sbuf(f"tokens{n}", [P, D_MODEL]) for n in range(2)]
        places = [mem.sbuf(f"places{n}", [P, 2, PARTS], I32) for n in range(2)]
        tokens_in = [mem.sem(f"tokens_in{n}") for n in range(2)]
        places_in = mem.sem("places_in")
        sent = [mem.sem(f"sent{n}") for n in range(2)]
        alone = mem.sem("alone")
        block = ctx.enter_context(nc.Block())
        per_tile = 16 * 2 * PARTS

        @block.sync
        def _(sp):
            with sp.Fori(0, turns) as turn:
                for half in range(2):
                    sp.wait_ge(sent[half], per_tile * turn)
                    sp.dma_start(tokens[half][:, :],
                                 by_partition(hidden, (2 * turn + half) * (P * D_MODEL), [[D_MODEL, P], [1, D_MODEL]])
                                 ).then_inc(tokens_in[half], 16)

        @block.vector
        def _(dve):
            with dve.Fori(0, turns) as turn:
                for half in range(2):
                    dve.wait_ge(sent[half], per_tile * turn)
                    for n in range(2):
                        nc.vector.tensor_copy(places[half][:, n, :],
                                              place[n][:, bass.ds(PARTS * (2 * turn + half), PARTS)]
                                              ).then_inc(places_in, 1)

        @block.gpsimd
        def _(pool):
            with pool.Fori(0, turns) as turn:
                for half in range(2):
                    pool.wait_ge(tokens_in[half], 16 * (turn + 1))
                    pool.wait_ge(places_in, 2 * (2 * turn + half + 1))
                    stand(pool, alone)
                    for n in range(2):
                        for part in range(PARTS):
                            pool.indirect_dma_start(
                                out=rows_in, out_offset=bass.IndirectOffsetOnAxis(
                                    ap=places[half][:, n, part:part + 1], axis=0),
                                in_=tokens[half][:, part * SUB:(part + 1) * SUB], in_offset=None
                            ).then_inc(sent[half], 16)
            for half in range(2):
                pool.wait_ge(sent[half], per_tile * turns)


def run_experts(nc, w_1, b_1, w_2, b_2, block_expert, rows_in, rows_out):
    turns = BLOCKS // 2
    quarters = ROWS_AT_ONCE // P
    depth = 96
    with ExitStack() as ctx:
        mem = Memory(nc, ctx, "experts")
        ident = mem.sbuf("ident", [P, P])
        rows = [mem.sbuf(f"rows{n}", [P, quarters, SUB]) for n in range(2)]
        rows_t = [mem.sbuf(f"rows_t{n}", [depth, ROWS_AT_ONCE]) for n in range(2)]
        first = [mem.sbuf(f"first{n}", [depth, HIDDEN]) for n in range(2)]
        second = [mem.sbuf(f"second{n}", [P, HIDDEN // P, SUB]) for n in range(2)]
        bias = [mem.sbuf(f"bias{n}", [P, SUB]) for n in range(2)]
        middle = [mem.sbuf(f"middle{n}", [P, HIDDEN // P, ROWS_AT_ONCE]) for n in range(2)]
        result = [mem.sbuf(f"result{n}", [P, quarters, SUB]) for n in range(2)]
        ps_turned = mem.psum("ps_turned", [P, 2, ROWS_AT_ONCE])
        ps_middle = mem.psum("ps_middle", [P, 4, ROWS_AT_ONCE])
        ps_result = mem.psum("ps_result", [P, 2, 2 * ROWS_AT_ONCE // 2])
        ident_zeroed = mem.sem("ident_zeroed")
        ident_ready = mem.sem("ident_ready")
        padded = mem.sem("padded")
        rows_arrived = [mem.sem(f"rows_arrived{n}") for n in range(2)]
        first_in = [mem.sem(f"first_in{n}") for n in range(2)]
        second_in = [mem.sem(f"second_in{n}") for n in range(2)]
        turned = mem.sem("turned")
        turned_copied = mem.sem("turned_copied")
        multiplied = mem.sem("multiplied")
        activated = mem.sem("activated")
        produced = mem.sem("produced")
        biased = mem.sem("biased")
        stored = [mem.sem(f"stored{n}") for n in range(2)]
        alone = mem.sem("alone")
        block = ctx.enter_context(nc.Block())

        @block.sync
        def _(sp):
            sp.wait_ge(padded, 4)
            with sp.Fori(0, turns) as turn:
                for half in range(2):
                    number = 2 * turn + half
                    sp.wait_ge(turned, 2 * turn)
                    stand(sp, alone)
                    sp.wait_ge(rows_arrived[half], 16 * turn)
                    stand(sp, alone)
                    sp.dma_start(rows[half][:, :, :],
                                 by_partition(rows_in, number * (ROWS_AT_ONCE * SUB),
                                              [[quarters * SUB, P], [SUB, quarters], [1, SUB]])
                                 ).then_inc(rows_arrived[half], 16)
                    expert = sp.value_load(block_expert[0:1, bass.ds(number, 1)], min_val=0, max_val=EXPERTS - 1)
                    sp.wait_ge(multiplied, 2 * turn)
                    sp.dma_start(first[half][0:SUB, :],
                                 by_partition(w_1, expert * (SUB * HIDDEN), [[HIDDEN, SUB], [1, HIDDEN]])
                                 ).then_inc(first_in[half], 16)
                    sp.dma_start(first[half][SUB:SUB + 1, :],
                                 by_partition(b_1, expert * HIDDEN, [[HIDDEN, 1], [1, HIDDEN]])
                                 ).then_inc(first_in[half], 16)
                    sp.wait_ge(biased, 2 * turn)
                    sp.dma_start(second[half][:, :, :],
                                 by_partition(w_2, expert * (HIDDEN * SUB), [[SUB, P], [P * SUB, HIDDEN // P], [1, SUB]])
                                 ).then_inc(second_in[half], 16)
                    sp.dma_start(bias[half][:, :],
                                 by_partition(b_2, expert * SUB, [[0, P], [1, SUB]])).then_inc(second_in[half], 16)

        @block.gpsimd
        def _(pool):
            identity_matrix(pool, nc, ident, ident_zeroed, ident_ready)
            with pool.Fori(0, turns) as turn:
                for half in range(2):
                    pool.wait_ge(biased, 2 * turn + half + 1)
                    pool.dma_start(by_partition(rows_out, (2 * turn + half) * (ROWS_AT_ONCE * SUB),
                                                [[quarters * SUB, P], [SUB, quarters], [1, SUB]]),
                                   result[half][:, :, :]).then_inc(stored[half], 16)
            for half in range(2):
                pool.wait_ge(stored[half], 16 * turns)

        @block.tensor
        def _(pe):
            pe.wait_ge(ident_ready, 1)
            with pe.Fori(0, turns) as turn:
                for half in range(2):
                    number = 2 * turn + half
                    pe.wait_ge(rows_arrived[half], 16 * (turn + 1))
                    pe.wait_ge(turned_copied, 2 * turn)
                    stand(pe, alone)
                    for quarter in range(quarters):
                        last = nc.tensor.transpose(ps_turned[0:SUB, half, quarter * P:(quarter + 1) * P],
                                                   rows[half][:, quarter, :], ident[:, :])
                    last.then_inc(turned, 1)
                for half in range(2):
                    number = 2 * turn + half
                    pe.wait_ge(turned_copied, number + 1)
                    pe.wait_ge(first_in[half], 32 * (turn + 1))
                    for part in range(HIDDEN // P):
                        last = nc.tensor.matmul(ps_middle[:, 2 * half + part, :],
                                                first[half][:, part * P:(part + 1) * P], rows_t[half][:, :],
                                                start=True, stop=True)
                    last.then_inc(multiplied, 1)
                for half in range(2):
                    number = 2 * turn + half
                    pe.wait_ge(activated, 2 * (number + 1))
                    pe.wait_ge(second_in[half], 32 * (turn + 1))
                    for quarter in range(quarters):
                        for part in range(HIDDEN // P):
                            last = nc.tensor.matmul(ps_result[:, half, quarter * SUB:(quarter + 1) * SUB],
                                                    middle[half][:, part, quarter * P:(quarter + 1) * P],
                                                    second[half][:, part, :],
                                                    start=(part == 0), stop=(part == HIDDEN // P - 1))
                    last.then_inc(produced, 1)

        @block.scalar
        def _(act):
            with act.Fori(0, turns) as turn:
                for half in range(2):
                    number = 2 * turn + half
                    act.wait_ge(multiplied, number + 1)
                    act.wait_ge(produced, 2 * turn)
                    for part in range(HIDDEN // P):
                        nc.scalar.activation(middle[half][:, part, :], ps_middle[:, 2 * half + part, :],
                                             ACT.Gelu).then_inc(activated, 1)

        @block.vector
        def _(dve):
            for half in range(2):
                nc.vector.memset(first[half][SUB:depth, :], 0.0).then_inc(padded, 1)
                nc.vector.memset(rows_t[half][SUB:depth, :], 1.0).then_inc(padded, 1)
            dve.wait_ge(padded, 4)
            with dve.Fori(0, turns) as turn:
                for half in range(2):
                    number = 2 * turn + half
                    dve.wait_ge(turned, number + 1)
                    dve.wait_ge(multiplied, 2 * turn)
                    nc.vector.tensor_copy(rows_t[half][0:SUB, :], ps_turned[0:SUB, half, :]).then_inc(turned_copied, 1)
                for half in range(2):
                    number = 2 * turn + half
                    dve.wait_ge(produced, number + 1)
                    dve.wait_ge(stored[half], 16 * turn)
                    nc.vector.tensor_tensor(
                        result[half][:, :, :],
                        ps_result[:, half, 0:quarters * SUB].rearrange("p (q n) -> p q n", q=quarters),
                        bias[half][:, :].unsqueeze(1).to_broadcast([P, quarters, SUB]), ALU.add).then_inc(biased, 1)


def collect(nc, place, weight, rows_out, mixed_t):
    turns = TOKEN_TILES // 2
    with ExitStack() as ctx:
        mem = Memory(nc, ctx, "collect")
        ident = mem.sbuf("ident", [P, P])
        places = [mem.sbuf(f"places{n}", [P, 2, PARTS], I32) for n in range(2)]
        rows = [mem.sbuf(f"rows{n}", [P, 2, PARTS, SUB]) for n in range(2)]
        scaled = [mem.sbuf(f"scaled{n}", [P, 2, PARTS, SUB]) for n in range(2)]
        mixed = [mem.sbuf(f"mixed{n}", [P, D_MODEL]) for n in range(2)]
        turned_out = [mem.sbuf(f"turned_out{n}", [P, CHUNKS, P]) for n in range(2)]
        ps_turned = mem.psum("ps_turned", [P, 2, D_MODEL])
        ident_zeroed = mem.sem("ident_zeroed")
        ident_ready = mem.sem("ident_ready")
        places_in = mem.sem("places_in")
        fetched = [mem.sem(f"fetched{n}") for n in range(2)]
        scaled_ready = mem.sem("scaled_ready")
        mixed_ready = mem.sem("mixed_ready")
        turned = mem.sem("turned")
        turned_copied = mem.sem("turned_copied")
        stored = [mem.sem(f"stored{n}") for n in range(2)]
        alone = mem.sem("alone")
        block = ctx.enter_context(nc.Block())
        per_tile = 16 * 2 * PARTS

        @block.gpsimd
        def _(pool):
            identity_matrix(pool, nc, ident, ident_zeroed, ident_ready)
            with pool.Fori(0, turns) as turn:
                for half in range(2):
                    pool.wait_ge(places_in, 2 * (2 * turn + half + 1))
                    pool.wait_ge(scaled_ready, 4 * turn)
                    stand(pool, alone)
                    for n in range(2):
                        for part in range(PARTS):
                            pool.indirect_dma_start(
                                out=rows[half][:, n, part, :], out_offset=None, in_=rows_out,
                                in_offset=bass.IndirectOffsetOnAxis(ap=places[half][:, n, part:part + 1], axis=0)
                            ).then_inc(fetched[half], 16)

        @block.vector
        def _(dve):
            with dve.Fori(0, turns) as turn:
                for half in range(2):
                    dve.wait_ge(fetched[half], per_tile * turn)
                    for n in range(2):
                        nc.vector.tensor_copy(places[half][:, n, :],
                                              place[n][:, bass.ds(PARTS * (2 * turn + half), PARTS)]
                                              ).then_inc(places_in, 1)
                for half in range(2):
                    number = 2 * turn + half
                    dve.wait_ge(fetched[half], per_tile * (turn + 1))
                    dve.wait_ge(mixed_ready, 2 * turn)
                    for n in range(2):
                        nc.vector.tensor_tensor(
                            scaled[half][:, n, :, :], rows[half][:, n, :, :],
                            weight[n][:, bass.ds(PARTS * number, PARTS)].unsqueeze(2).to_broadcast([P, PARTS, SUB]),
                            ALU.mult).then_inc(scaled_ready, 1)
                    dve.wait_ge(scaled_ready, 2 * (number + 1))
                    dve.wait_ge(turned, 2 * turn)
                    nc.vector.tensor_tensor(mixed[half][:, :], scaled[half][:, 0, :, :].rearrange("p a b -> p (a b)"),
                                            scaled[half][:, 1, :, :].rearrange("p a b -> p (a b)"),
                                            ALU.add).then_inc(mixed_ready, 1)

        @block.tensor
        def _(pe):
            pe.wait_ge(ident_ready, 1)
            with pe.Fori(0, turns) as turn:
                for half in range(2):
                    pe.wait_ge(mixed_ready, 2 * turn + half + 1)
                    pe.wait_ge(turned_copied, 2 * turn)
                    for chunk in range(CHUNKS):
                        last = nc.tensor.transpose(ps_turned[:, half, chunk * P:(chunk + 1) * P],
                                                   mixed[half][:, chunk * P:(chunk + 1) * P], ident[:, :])
                    last.then_inc(turned, 1)

        @block.scalar
        def _(act):
            with act.Fori(0, turns) as turn:
                for half in range(2):
                    number = 2 * turn + half
                    act.wait_ge(turned, number + 1)
                    act.wait_ge(stored[half], 16 * turn)
                    nc.scalar.activation(turned_out[half][:, :, :].rearrange("p c t -> p (c t)"),
                                         ps_turned[:, half, :], ACT.Copy).then_inc(turned_copied, 1)
                    act.wait_ge(turned_copied, number + 1)
                    act.dma_start(by_partition(mixed_t, (number // TOK_TILES) * (D_MODEL * SEQ)
                                               + (number % TOK_TILES) * P,
                                               [[SEQ, P], [P * SEQ, CHUNKS], [1, P]]),
                                  turned_out[half][:, :, :]).then_inc(stored[half], 16)
            for half in range(2):
                act.wait_ge(stored[half], 16 * turns)


def decoder_block(nc, x, x_t, ctx_t, w, out):

    def scratch(name, *shape):
        return nc.dram_tensor(name, list(shape), F32).ap()

    def activations(name):
        return scratch(name, BATCH, SEQ, D_MODEL)

    q_t, k_t, v = activations("q_t"), activations("k_t"), activations("v")
    attended_t = activations("attended_t")
    first, first_t = activations("first"), activations("first_t")
    second, second_t = activations("second"), activations("second_t")

    project(nc, "self", x_t, x_t, [w[f"self_w{n}"] for n in "qkv"], [w[f"self_b{n}"] for n in "qkv"], q_t, k_t, v)
    attend(nc, "self", q_t, k_t, v, attended_t,
           rel=(w["relative_k_t"], w["relative_v"], scratch("relative_scores", TILES * P * PITCH)))
    finish(nc, "self", attended_t, w["self_wo"], w["self_bo"], x, first, first_t)

    project(nc, "cross", first_t, ctx_t, [w[f"cross_w{n}"] for n in "qkv"], [w[f"cross_b{n}"] for n in "qkv"],
            q_t, k_t, v)
    attend(nc, "cross", q_t, k_t, v, attended_t)
    finish(nc, "cross", attended_t, w["cross_wo"], w["cross_bo"], first, second, second_t)

    rows = [scratch(name, BLOCKS * ROWS_AT_ONCE, SUB) for name in ("rows_in", "rows_out")]
    feed_forward(nc, second_t, w["ffn_wm"], w["ffn_bm"], w["expert_emb"], w["w1"], w["b1"], w["w2"], w["b2"],
                 activations("hidden"), *rows, attended_t)
    finish(nc, "ffn", attended_t, w["ffn_wo"], w["ffn_bo"], second, out)


def kernel(x, ctx_768, L0_attn_Wq, L0_attn_bq, L0_attn_Wk, L0_attn_bk, L0_attn_Wv, L0_attn_bv, L0_attn_Wo, L0_attn_bo,
           L0_attn_relative_k, L0_attn_relative_v, L0_xattn_Wq, L0_xattn_bq, L0_xattn_Wk, L0_xattn_bk, L0_xattn_Wv,
           L0_xattn_bv, L0_xattn_Wo, L0_xattn_bo, L0_ffn_Wm, L0_ffn_bm, L0_ffn_expert_emb, L0_ffn_W1, L0_ffn_b1,
           L0_ffn_W2, L0_ffn_b2, L0_ffn_Wo, L0_ffn_bo):
    from concourse import bacc
    from concourse.bass_utils import run_bass_kernel_spmd

    arrays = {
        "x": x, "x_t": np.transpose(x, (0, 2, 1)), "ctx_t": np.transpose(ctx_768, (0, 2, 1)),
        "self_wq": np.transpose(L0_attn_Wq), "self_wk": np.transpose(L0_attn_Wk), "self_wv": np.transpose(L0_attn_Wv),
        "self_wo": np.transpose(L0_attn_Wo), "self_bq": L0_attn_bq, "self_bk": L0_attn_bk, "self_bv": L0_attn_bv,
        "self_bo": L0_attn_bo, "relative_k_t": np.transpose(L0_attn_relative_k), "relative_v": L0_attn_relative_v,
        "cross_wq": L0_xattn_Wq, "cross_wk": L0_xattn_Wk, "cross_wv": L0_xattn_Wv, "cross_wo": L0_xattn_Wo,
        "cross_bq": L0_xattn_bq, "cross_bk": L0_xattn_bk, "cross_bv": L0_xattn_bv, "cross_bo": L0_xattn_bo,
        "ffn_wm": L0_ffn_Wm, "ffn_bm": L0_ffn_bm, "expert_emb": L0_ffn_expert_emb, "w1": L0_ffn_W1, "b1": L0_ffn_b1,
        "w2": L0_ffn_W2, "b2": L0_ffn_b2, "ffn_wo": L0_ffn_Wo, "ffn_bo": L0_ffn_bo,
    }
    arrays = {name: np.ascontiguousarray(a) for name, a in arrays.items()}
    nc = bacc.Bacc("TRN2", target_bir_lowering=False, num_devices=1)
    w = {name: nc.dram_tensor(f"in_{name}", a.shape, F32, kind="ExternalInput").ap() for name, a in arrays.items()}
    out = nc.dram_tensor("out", [BATCH, SEQ, D_MODEL], F32, kind="ExternalOutput").ap()
    decoder_block(nc, w["x"], w["x_t"], w["ctx_t"], w, out)
    result = run_bass_kernel_spmd(nc, [{f"in_{name}": a for name, a in arrays.items()}], core_ids=[0])
    return result.results[0]["out"]
```

```python
from contextlib import ExitStack

import numpy as np

import concourse.bass as bass
from concourse import mybir

ACT = mybir.ActivationFunctionType
ALU = mybir.AluOpType
AX_X = mybir.AxisListType.X
F32 = mybir.dt.float32
I32 = mybir.dt.int32
U32 = mybir.dt.uint32

P = 128
BATCH, SEQ, D_MODEL, D_CTX = 8, 512, 512, 384
HEADS, D_HEAD = 16, 32
CHUNKS = D_MODEL // P
TOK_TILES = SEQ // P
HEADS_PER_CHUNK = P // D_HEAD
SCALE = float(1.0 / np.sqrt(np.float32(D_HEAD)))
LN_EPS = 1e-5


class Memory:

    def __init__(self, nc, ctx, stage):
        self.nc, self.ctx, self.stage, self.sems = nc, ctx, stage, []
        ctx.callback(self.clear)

    def sbuf(self, name, shape, dtype=F32):
        return self.ctx.enter_context(self.nc.sbuf_tensor(f"{self.stage}_{name}", shape, dtype))

    def psum(self, name, shape, dtype=F32):
        return self.ctx.enter_context(self.nc.psum_tensor(f"{self.stage}_{name}", shape, dtype))

    def sem(self, name):
        self.sems.append(self.nc.alloc_semaphore(name=f"{self.stage}_{name}"))
        return self.sems[-1]

    def clear(self):
        if self.sems:
            self.nc.clear_and_free_semaphores(self.sems)
            self.nc.all_engine_barrier()


def stand(engine, alone):
    engine.sem_inc(alone, 1)


def by_partition(ap, offset, dims):
    return bass.AP(ap.tensor, offset, dims)


def project(nc, stage, q_src, kv_src, weights, biases, q_out, k_out, v_out):
    q_rows, kv_rows = q_src.shape[1] // P, kv_src.shape[1] // P
    w_q, w_k, w_v = weights
    b_q, b_k, b_v = biases
    banks = 4
    turns = BATCH // 2
    with ExitStack() as ctx:
        mem = Memory(nc, ctx, f"{stage}_project")
        wq = mem.sbuf("wq", [P, q_rows, D_MODEL])
        wk = mem.sbuf("wk", [P, kv_rows, D_MODEL])
        wv = mem.sbuf("wv", [P, kv_rows, D_MODEL])
        bias_q = mem.sbuf("bias_q", [P, CHUNKS])
        bias_k = mem.sbuf("bias_k", [P, CHUNKS])
        bias_k_scaled = mem.sbuf("bias_k_scaled", [P, CHUNKS])
        bias_v = mem.sbuf("bias_v", [P, D_MODEL])
        src_q = [mem.sbuf(f"src_q{n}", [P, q_rows, SEQ]) for n in range(2)]
        src_kv = [mem.sbuf(f"src_kv{n}", [P, kv_rows, SEQ]) for n in range(2)]
        out_q = [mem.sbuf(f"out_q{n}", [P, CHUNKS, SEQ]) for n in range(2)]
        out_k = [mem.sbuf(f"out_k{n}", [P, CHUNKS, SEQ]) for n in range(2)]
        out_v = [mem.sbuf(f"out_v{n}", [P, TOK_TILES, D_MODEL]) for n in range(2)]
        ps_qk = mem.psum("ps_qk", [P, banks, SEQ])
        ps_v = mem.psum("ps_v", [P, banks, D_MODEL])
        weights_in = mem.sem("weights_in")
        biases_in = mem.sem("biases_in")
        bias_scaled = mem.sem("bias_scaled")
        src_in = [mem.sem(f"src_in{n}") for n in range(2)]
        src_free = mem.sem("src_free")
        qk_product = mem.sem("qk_product")
        qk_bank_free = mem.sem("qk_bank_free")
        v_product = mem.sem("v_product")
        v_bank_free = mem.sem("v_bank_free")
        qk_stored = [mem.sem(f"qk_stored{n}") for n in range(2)]
        v_stored = [mem.sem(f"v_stored{n}") for n in range(2)]
        block = ctx.enter_context(nc.Block())

        @block.sync
        def _(sp):
            sp.dma_start(wq[:, :, :], w_q.rearrange("(r p) n -> p r n", p=P)).then_inc(weights_in, 16)
            sp.dma_start(wk[:, :, :], w_k.rearrange("(r p) n -> p r n", p=P)).then_inc(weights_in, 16)
            sp.dma_start(wv[:, :, :], w_v.rearrange("(r p) n -> p r n", p=P)).then_inc(weights_in, 16)
            sp.dma_start(bias_q[:, :], b_q.rearrange("(c p) -> p c", p=P),
                         allow_slow_non_contiguous=True).then_inc(biases_in, 16)
            sp.dma_start(bias_k[:, :], b_k.rearrange("(c p) -> p c", p=P),
                         allow_slow_non_contiguous=True).then_inc(biases_in, 16)
            sp.dma_start(bias_v[:, :], by_partition(b_v, 0, [[0, P], [1, D_MODEL]])).then_inc(biases_in, 16)
            with sp.Fori(0, turns) as turn:
                for half in range(2):
                    sp.wait_ge(src_free, 2 * turn + half + 1)
                    for dst, src in ((src_q, q_src), (src_kv, kv_src)):
                        sp.dma_start(dst[half][:, :, :],
                                     src[2 * turn + half].rearrange("(r p) t -> p r t", p=P)).then_inc(src_in[half], 16)

        @block.gpsimd
        def _(pool):
            with pool.Fori(0, turns) as turn:
                for half in range(2):
                    pool.wait_ge(v_bank_free, TOK_TILES * (2 * turn + half + 1) + banks)
                    pool.dma_start(v_out[2 * turn + half].rearrange("(r p) n -> p r n", p=P),
                                   out_v[half][:, :, :]).then_inc(v_stored[half], 16)
            for half in range(2):
                pool.wait_ge(v_stored[half], 16 * turns)

        @block.tensor
        def _(pe):
            pe.sem_inc(src_free, 2)
            pe.wait_ge(weights_in, 48)
            with pe.Fori(0, turns) as turn:
                for half in range(2):
                    pe.wait_ge(src_in[half], 32 * (turn + 1))
                    groups = [(wq, src_q, q_rows)] * CHUNKS + [(wk, src_kv, kv_rows)] * CHUNKS
                    for n, (w, src, rows) in enumerate(groups):
                        chunk = n % CHUNKS
                        pe.wait_ge(qk_bank_free, 2 * CHUNKS * (2 * turn + half) + n + 1)
                        for r in range(rows):
                            last = nc.tensor.matmul(ps_qk[:, n % banks, :], w[:, r, chunk * P:(chunk + 1) * P],
                                                    src[half][:, r, :], start=(r == 0), stop=(r == rows - 1))
                        last.then_inc(qk_product, 1)
                    for t in range(TOK_TILES):
                        pe.wait_ge(v_bank_free, TOK_TILES * (2 * turn + half) + t + 1)
                        for r in range(kv_rows):
                            last = nc.tensor.matmul(ps_v[:, t % banks, :], src_kv[half][:, r, t * P:(t + 1) * P],
                                                    wv[:, r, :], start=(r == 0), stop=(r == kv_rows - 1))
                        last.then_inc(v_product, 1)
                        if t == TOK_TILES - 1:
                            pe.wait_ge(v_product, TOK_TILES * (2 * turn + half + 1))
                            pe.sem_inc(src_free, 1)

        @block.scalar
        def _(act):
            act.sem_inc(qk_bank_free, banks)
            act.wait_ge(biases_in, 48)
            nc.scalar.activation(bias_k_scaled[:, :], bias_k[:, :], ACT.Copy, scale=SCALE).then_inc(bias_scaled, 1)
            act.wait_ge(bias_scaled, 1)
            with act.Fori(0, turns) as turn:
                for half in range(2):
                    act.wait_ge(qk_stored[half], 32 * turn)
                    for n in range(2 * CHUNKS):
                        chunk = n % CHUNKS
                        out, bias, scale = ((out_q, bias_q, 1.0), (out_k, bias_k_scaled, SCALE))[n // CHUNKS]
                        act.wait_ge(qk_product, 2 * CHUNKS * (2 * turn + half) + n + 1)
                        nc.scalar.activation(out[half][:, chunk, :], ps_qk[:, n % banks, :], ACT.Identity,
                                             bias=bias[:, chunk:chunk + 1], scale=scale).then_inc(qk_bank_free, 1)
                    act.wait_ge(qk_bank_free, 2 * CHUNKS * (2 * turn + half + 1) + banks)
                    for dst, out in ((q_out, out_q), (k_out, out_k)):
                        act.dma_start(dst[2 * turn + half].rearrange("(c p) t -> p c t", p=P),
                                      out[half][:, :, :]).then_inc(qk_stored[half], 16)
            for half in range(2):
                act.wait_ge(qk_stored[half], 32 * turns)

        @block.vector
        def _(dve):
            dve.sem_inc(v_bank_free, banks)
            dve.wait_ge(biases_in, 48)
            with dve.Fori(0, turns) as turn:
                for half in range(2):
                    dve.wait_ge(v_stored[half], 16 * turn)
                    for t in range(TOK_TILES):
                        dve.wait_ge(v_product, TOK_TILES * (2 * turn + half) + t + 1)
                        nc.vector.tensor_tensor(out_v[half][:, t, :], ps_v[:, t % banks, :], bias_v[:, :],
                                                ALU.add).then_inc(v_bank_free, 1)


BATCHES_AT_ONCE = 2
ROWS = 64
UNITS_PER_PAIR = SEQ // ROWS
UNITS = BATCH // BATCHES_AT_ONCE * UNITS_PER_PAIR
TILES = BATCHES_AT_ONCE * HEADS // 2
GROUPS = BATCHES_AT_ONCE * CHUNKS
WINDOW = SEQ + ROWS - 1
PITCH = WINDOW + 1
KEY_TILES = SEQ // P
BIG = 3.0e38


def identity_matrix(pool, nc, ident, zeroed, ready):
    nc.gpsimd.memset(ident[:, :], 0.0).then_inc(zeroed, 1)
    pool.wait_ge(zeroed, 1)
    nc.gpsimd.affine_select(out=ident[:, :], in_=ident[:, :], compare_op=ALU.not_equal, fill=1.0, base=0,
                            pattern=[[-1, P]], channel_multiplier=1).then_inc(ready, 1)


def attend(nc, stage, q_t, k_t, v, out_t, rel=None):
    with ExitStack() as ctx:
        mem = Memory(nc, ctx, f"{stage}_attend")
        ident = mem.sbuf("ident", [P, P])
        queries = mem.sbuf("queries", [P, TILES, 2, ROWS])
        keys = mem.sbuf("keys", [P, BATCHES_AT_ONCE, CHUNKS, SEQ])
        values = mem.sbuf("values", [P, KEY_TILES, BATCHES_AT_ONCE, D_MODEL])
        probs = mem.sbuf("probs", [P, TILES, SEQ])
        probs_t = mem.sbuf("probs_t", [P, KEY_TILES, TILES, 2, ROWS])
        low = mem.sbuf("low", [P, TILES])
        total = mem.sbuf("total", [P, TILES])
        inverse = mem.sbuf("inverse", [P, TILES])
        out = mem.sbuf("out", [P, GROUPS, ROWS])
        ps_scores = mem.psum("ps_scores", [P, 2, SEQ])
        ps_turned = mem.psum("ps_turned", [P, 2, SEQ])
        ps_out = mem.psum("ps_out", [P, GROUPS, ROWS])
        if rel:
            rel_k_t, rel_v, scratch = rel
            window_k = mem.sbuf("window_k", [P, PITCH])
            window_v = mem.sbuf("window_v", [P, KEY_TILES, ROWS, D_HEAD])
            shifted = [mem.sbuf(f"shifted{n}", [P, 2, PITCH]) for n in range(2)]
            rel_out = mem.sbuf("rel_out", [P, GROUPS, ROWS])
            ps_rel = mem.psum("ps_rel", [P, 2, SEQ])
            ps_rel_out = mem.psum("ps_rel_out", [P, ROWS // 4, TILES * 2])
        ident_zeroed = mem.sem("ident_zeroed")
        ident_ready = mem.sem("ident_ready")
        queries_zeroed = mem.sem("queries_zeroed")
        queries_in = mem.sem("queries_in")
        window_k_in = mem.sem("window_k_in")
        window_v_in = mem.sem("window_v_in")
        keys_in = mem.sem("keys_in")
        values_in = mem.sem("values_in")
        rel_product = mem.sem("rel_product")
        rel_copied = mem.sem("rel_copied")
        rel_stored = [mem.sem(f"rel_stored{n}") for n in range(2)]
        rel_in = [mem.sem(f"rel_in{n}") for n in range(2)]
        scored = mem.sem("scored")
        scores_read = mem.sem("scores_read")
        exps = mem.sem("exps")
        inverted = mem.sem("inverted")
        probs_ready = mem.sem("probs_ready")
        turned = mem.sem("turned")
        turned_copied = mem.sem("turned_copied")
        values_summed = mem.sem("values_summed")
        unit_done = mem.sem("unit_done")
        rel_out_act = mem.sem("rel_out_act")
        rel_out_dve = mem.sem("rel_out_dve")
        out_ready = mem.sem("out_ready")
        out_stored = mem.sem("out_stored")
        alone = mem.sem("alone")
        block = ctx.enter_context(nc.Block())

        LEAD = 8
        LAG = 3
        AHEAD = 2

        def relative_rows(sp, unit, row_block):
            for head in range(HEADS_PER_CHUNK):
                sp.dma_start(
                    window_k[D_HEAD * head:D_HEAD * (head + 1), 0:WINDOW],
                    by_partition(rel_k_t, SEQ - ROWS - row_block * ROWS,
                                 [[2 * SEQ - 1, D_HEAD], [1, WINDOW]])).then_inc(window_k_in, 16)
            for group in range(TILES // 2 + 1):
                if group < TILES // 2:
                    sp.wait_ge(rel_copied, TILES * unit + 2 * group + 2)
                    sp.dma_start(by_partition(scratch, 2 * group * P * PITCH,
                                              [[PITCH, P], [P * PITCH, 2], [1, WINDOW]]),
                                 shifted[group % 2][:, :, 0:WINDOW]).then_inc(rel_stored[group % 2], 16)
                if group > 0:
                    back = group - 1
                    sp.wait_ge(rel_stored[back % 2], 16 * (TILES // 4 * unit + back // 2 + 1))
                    stand(sp, alone)
                    sp.wait_ge(turned, TILES * unit + 2 * back + 2)
                    stand(sp, alone)
                    sp.wait_ge(rel_in[back % 2], 32 * (TILES // 4 * unit + back // 2))
                    for tile in range(2 * back, 2 * back + 2):
                        sp.dma_start(probs[:, tile, :],
                                     by_partition(scratch, tile * P * PITCH + ROWS - 1,
                                                  [[ROWS * PITCH, 2], [PITCH - 1, ROWS], [1, SEQ]])
                                     ).then_inc(rel_in[back % 2], 16)
                if group > LEAD // 2:
                    part = group - LEAD // 2 - 1
                    sp.wait_ge(unit_done, unit)
                    sp.dma_start(window_v[:, part, :, :],
                                 by_partition(rel_v, (SEQ - ROWS - row_block * ROWS + part * P) * D_HEAD,
                                              [[D_HEAD, P], [1, ROWS * D_HEAD]])).then_inc(window_v_in, 16)

        @block.sync
        def _(sp):
            sp.wait_ge(queries_zeroed, 1)
            with sp.Fori(0, UNITS // UNITS_PER_PAIR) as pair:
                sp.wait_ge(scored, TILES * UNITS_PER_PAIR * pair)
                sp.dma_start(keys[:, :, :, :],
                             by_partition(k_t, pair * (BATCHES_AT_ONCE * D_MODEL * SEQ),
                                          [[SEQ, P], [P * SEQ, GROUPS], [1, SEQ]])).then_inc(keys_in, 16)
                with sp.Fori(0, UNITS_PER_PAIR) as row_block:
                    unit = UNITS_PER_PAIR * pair + row_block
                    sp.wait_ge(scored, TILES * unit)
                    for head in range(HEADS_PER_CHUNK):
                        sp.dma_start(
                            queries[D_HEAD * head:D_HEAD * (head + 1), head // 2:TILES:2, head % 2, :],
                            by_partition(q_t, pair * (BATCHES_AT_ONCE * D_MODEL * SEQ) + row_block * ROWS
                                         + D_HEAD * head * SEQ,
                                         [[SEQ, D_HEAD], [P * SEQ, GROUPS], [1, ROWS]])).then_inc(queries_in, 16)
                    if rel:
                        relative_rows(sp, unit, row_block)

        @block.gpsimd
        def _(pool):
            nc.gpsimd.memset(queries[:, :, :, :], 0.0).then_inc(queries_zeroed, 1)
            identity_matrix(pool, nc, ident, ident_zeroed, ident_ready)
            with pool.Fori(0, UNITS // UNITS_PER_PAIR) as pair:
                pool.wait_ge(values_summed, UNITS_PER_PAIR * pair)
                for b in range(BATCHES_AT_ONCE):
                    pool.dma_start(values[:, :, b, :],
                                 by_partition(v, pair * (BATCHES_AT_ONCE * D_MODEL * SEQ) + b * SEQ * D_MODEL,
                                              [[D_MODEL, P], [P * D_MODEL, KEY_TILES], [1, D_MODEL]])
                                 ).then_inc(values_in, 16)
                with pool.Fori(0, UNITS_PER_PAIR) as row_block:
                    unit = UNITS_PER_PAIR * pair + row_block
                    pool.wait_ge(out_ready, unit + 1)
                    pool.dma_start(
                        by_partition(out_t, pair * (BATCHES_AT_ONCE * D_MODEL * SEQ) + row_block * ROWS,
                                     [[SEQ, P], [P * SEQ, GROUPS], [1, ROWS]]), out[:, :, :]).then_inc(out_stored, 16)
            pool.wait_ge(out_stored, 16 * UNITS)

        @block.tensor
        def _(pe):
            def relative_scores(unit, tile):
                pe.wait_ge(rel_copied, TILES * unit + tile)
                lhs = queries[:, tile, :, :]
                nc.tensor.matmul(ps_rel[:, 0, :], lhs, window_k[:, 0:SEQ], start=True, stop=True)
                nc.tensor.matmul(ps_rel[:, 1, 0:WINDOW - SEQ], lhs, window_k[:, SEQ:WINDOW],
                                 start=True, stop=True).then_inc(rel_product, 1)

            def scores(unit, tile):
                pe.wait_ge(scores_read, TILES * unit + tile + 1)
                nc.tensor.matmul(ps_scores[:, tile % 2, :], queries[:, tile, :, :],
                                 keys[:, tile // (TILES // 2), tile // 2 % CHUNKS, :],
                                 start=True, stop=True).then_inc(scored, 1)

            def transpose(unit, tile):
                pe.wait_ge(probs_ready, TILES * unit + tile + 1)
                pe.wait_ge(turned_copied, TILES * unit + tile + 1)
                for part in range(KEY_TILES):
                    last = nc.tensor.transpose(ps_turned[:, tile % 2, part * P:(part + 1) * P],
                                               probs[:, tile, part * P:(part + 1) * P], ident[:, :])
                last.then_inc(turned, 1)

            def values_product(unit, group):
                b, chunk = group // CHUNKS, group % CHUNKS
                pe.wait_ge(turned_copied, TILES * unit + 2 * group + 4)
                if group == 0:
                    pe.wait_ge(out_ready, unit)
                for part in range(KEY_TILES):
                    for head in range(HEADS_PER_CHUNK):
                        first = chunk * P + head * D_HEAD
                        last = nc.tensor.matmul(ps_out[D_HEAD * head:D_HEAD * (head + 1), group, :],
                                                values[:, part, b, first:first + D_HEAD],
                                                probs_t[:, part, 2 * group + head // 2, head % 2, :],
                                                start=(part == 0), stop=(part == KEY_TILES - 1))
                if group == GROUPS - 1:
                    last.then_inc(values_summed, 1)

            def relative_values_product(unit, has_next):
                for n in range(ROWS // 4):
                    for part in range(KEY_TILES):
                        for lane in range(4):
                            row = 4 * n + lane
                            last = nc.tensor.matmul(
                                ps_rel_out[D_HEAD * lane:D_HEAD * (lane + 1), n, :],
                                window_v[:, part, ROWS - 1 - row, :],
                                probs_t[:, part, :, :, row], start=(part == 0), stop=(part == KEY_TILES - 1))
                    if has_next and n % 2 == 1:
                        relative_scores(unit + 1, n // 2)
                    if has_next and n in (8, 10):
                        first_scores(unit + 1, (n - 8) // 2)
                return last

            def arrivals(unit):
                pe.wait_ge(queries_in, 16 * HEADS_PER_CHUNK * (unit + 1))
                if rel:
                    pe.wait_ge(window_k_in, 16 * HEADS_PER_CHUNK * (unit + 1))

            def first_scores(unit, tile):
                pe.wait_ge(keys_in, 16 * (unit // UNITS_PER_PAIR + 1))
                scores(unit, tile)

            def unit_program(unit, has_next):
                pe.wait_ge(values_in, 16 * BATCHES_AT_ONCE * (unit // UNITS_PER_PAIR + 1))
                for tile in range(AHEAD, TILES + LAG):
                    ahead, behind = tile - AHEAD + LEAD, tile - LAG
                    if rel and ahead < TILES:
                        relative_scores(unit, ahead)
                    if tile < TILES:
                        scores(unit, tile)
                    if behind >= 0:
                        transpose(unit, behind)
                    if behind >= 2 and behind % 2 == 0:
                        values_product(unit, behind // 2 - 1)
                values_product(unit, GROUPS - 1)
                if has_next:
                    arrivals(unit + 1)
                if rel:
                    pe.wait_ge(window_v_in, 16 * KEY_TILES * (unit + 1))
                    pe.wait_ge(rel_out_act, 8 * unit)
                    pe.wait_ge(rel_out_dve, 8 * unit)
                    relative_values_product(unit, has_next).then_inc(unit_done, 1)
                elif has_next:
                    for tile in range(AHEAD):
                        first_scores(unit + 1, tile)

            pe.wait_ge(ident_ready, 1)
            arrivals(0)
            if rel:
                for tile in range(LEAD):
                    relative_scores(0, tile)
            for tile in range(AHEAD):
                first_scores(0, tile)
            with pe.Fori(0, UNITS - 1) as unit:
                unit_program(unit, True)
            unit_program(UNITS - 1, False)

        def relative_out(head, lane):
            return (rel_out[D_HEAD * head:D_HEAD * (head + 1), :, lane:ROWS:4],
                    ps_rel_out[D_HEAD * lane:D_HEAD * (lane + 1), :, head:TILES * 2:HEADS_PER_CHUNK]
                    .rearrange("p n g -> p g n"))

        @block.scalar
        def _(act):
            def copy_relative_scores(unit, tile):
                act.wait_ge(rel_product, TILES * unit + tile + 1)
                if tile % 2 == 0:
                    act.wait_ge(rel_stored[tile // 2 % 2], 16 * (TILES // 4 * unit + tile // 4))
                nc.scalar.activation(shifted[tile // 2 % 2][:, tile % 2, 0:WINDOW],
                                     ps_rel[:, :, :].rearrange("p b n -> p (b n)")[:, 0:WINDOW],
                                     ACT.Copy).then_inc(rel_copied, 1)

            def exponentials(unit, tile):
                act.wait_ge(scores_read, TILES * unit + tile + 3)
                nc.scalar.activation(probs[:, tile, :], probs[:, tile, :], ACT.Exp, bias=low[:, tile:tile + 1],
                                     scale=-1.0, accum_out=total[:, tile:tile + 1]).then_inc(exps, 1)

            def normalise(unit, tile):
                act.wait_ge(inverted, TILES * unit + tile + 1)
                nc.scalar.activation(probs[:, tile, :], probs[:, tile, :], ACT.Copy,
                                     scale=inverse[:, tile:tile + 1]).then_inc(probs_ready, 1)

            def first_tiles(unit):
                if rel:
                    for tile in range(LEAD):
                        copy_relative_scores(unit, tile)
                for tile in range(AHEAD):
                    exponentials(unit, tile)
                normalise(unit, 0)

            def unit_program(unit, has_next):
                for tile in range(AHEAD, TILES + 1):
                    if rel and tile - AHEAD + LEAD < TILES:
                        copy_relative_scores(unit, tile - AHEAD + LEAD)
                    if tile < TILES:
                        exponentials(unit, tile)
                    normalise(unit, tile - 1)
                if has_next:
                    first_tiles(unit + 1)
                if rel:
                    act.wait_ge(unit_done, unit + 1)
                    act.wait_ge(out_ready, unit)
                    for head in range(HEADS_PER_CHUNK):
                        for lane in range(2):
                            nc.scalar.activation(*relative_out(head, lane), ACT.Copy).then_inc(rel_out_act, 1)

            first_tiles(0)
            with act.Fori(0, UNITS - 1) as unit:
                unit_program(unit, True)
            unit_program(UNITS - 1, False)

        @block.vector
        def _(dve):
            dve.sem_inc(scores_read, 2)
            dve.sem_inc(turned_copied, 2)
            dve.sem_inc(turned, TILES)

            def read_scores(unit, tile):
                dve.wait_ge(scored, TILES * unit + tile + 1)
                if rel:
                    if tile % 2 == 0:
                        dve.wait_ge(rel_in[tile // 2 % 2], 32 * (TILES // 4 * unit + tile // 4 + 1))
                    stand(dve, alone)
                    nc.vector.tensor_tensor_reduce(
                        out=probs[:, tile, :], in0=ps_scores[:, tile % 2, :], in1=probs[:, tile, :],
                        scale=-1.0, scalar=BIG, op0=ALU.add, op1=ALU.min,
                        accum_out=low[:, tile:tile + 1]).then_inc(scores_read, 1)
                else:
                    dve.wait_ge(turned, TILES * unit + tile + 1)
                    nc.vector.tensor_scalar(
                        probs[:, tile, :], ps_scores[:, tile % 2, :], -1.0, BIG, ALU.mult, ALU.min,
                        accum_out=low[:, tile:tile + 1]).then_inc(scores_read, 1)

            def invert(unit, tile):
                dve.wait_ge(exps, TILES * unit + tile + 1)
                nc.vector.reciprocal(inverse[:, tile:tile + 1], total[:, tile:tile + 1]).then_inc(inverted, 1)

            def copy_turned(unit, tile):
                if tile == 0:
                    dve.wait_ge(unit_done if rel else values_summed, unit)
                dve.wait_ge(turned, TILES * (unit + 1) + tile + 1)
                nc.vector.tensor_copy(
                    probs_t[:, :, tile, :, :].rearrange("p k h r -> p k (h r)"),
                    ps_turned[:, tile % 2, :].rearrange("p (k r) -> p k r", k=KEY_TILES)
                ).then_inc(turned_copied, 1)

            def first_tiles(unit):
                for tile in range(AHEAD):
                    read_scores(unit, tile)
                invert(unit, 0)

            def output(unit):
                dve.wait_ge(values_summed, unit + 1)
                dve.wait_ge(out_stored, 16 * unit)
                if rel:
                    dve.wait_ge(unit_done, unit + 1)
                    for head in range(HEADS_PER_CHUNK):
                        for lane in range(2, 4):
                            nc.vector.tensor_copy(*relative_out(head, lane)).then_inc(rel_out_dve, 1)
                    dve.wait_ge(rel_out_act, 8 * (unit + 1))
                    dve.wait_ge(rel_out_dve, 8 * (unit + 1))
                    nc.vector.tensor_tensor(out[:, :, :], ps_out[:, :, :], rel_out[:, :, :],
                                            ALU.add).then_inc(out_ready, 1)
                else:
                    nc.vector.tensor_copy(out[:, :, :], ps_out[:, :, :]).then_inc(out_ready, 1)

            def unit_program(unit, has_next):
                for tile in range(AHEAD, TILES + LAG):
                    if tile < TILES:
                        read_scores(unit, tile)
                    if tile <= TILES:
                        invert(unit, tile - 1)
                    if tile >= LAG:
                        copy_turned(unit, tile - LAG)
                if rel and has_next:
                    first_tiles(unit + 1)
                output(unit)
                if not rel and has_next:
                    first_tiles(unit + 1)

            first_tiles(0)
            with dve.Fori(0, UNITS - 1) as unit:
                unit_program(unit, True)
            unit_program(UNITS - 1, False)


def finish(nc, stage, a_t, w, bias, residual, out, out_t=None):
    turns = BATCH // 2
    tiles = TOK_TILES
    with ExitStack() as ctx:
        mem = Memory(nc, ctx, f"{stage}_finish")
        ident = mem.sbuf("ident", [P, P])
        weights = mem.sbuf("weights", [P, CHUNKS, D_MODEL])
        bias_all = mem.sbuf("bias_all", [P, D_MODEL])
        eps = mem.sbuf("eps", [P, 1])
        src = [mem.sbuf(f"src{n}", [P, CHUNKS, SEQ]) for n in range(2)]
        res = [mem.sbuf(f"res{n}", [P, tiles, D_MODEL]) for n in range(2)]
        stats = [mem.sbuf(f"stats{n}", [P, tiles, 6]) for n in range(2)]
        moments = [mem.sbuf(f"moments{n}", [P, tiles, 2]) for n in range(2)]
        deviation = [mem.sbuf(f"deviation{n}", [P, tiles]) for n in range(2)]
        factor = [mem.sbuf(f"factor{n}", [P, tiles]) for n in range(2)]
        turned_out = [mem.sbuf(f"turned_out{n}", [P, CHUNKS, SEQ]) for n in range(2)]
        ps = mem.psum("ps", [P, tiles, D_MODEL])
        ps_turned = mem.psum("ps_turned", [P, 2, D_MODEL])
        weights_in = mem.sem("weights_in")
        src_in = [mem.sem(f"src_in{n}") for n in range(2)]
        ident_zeroed = mem.sem("ident_zeroed")
        ident_ready = mem.sem("ident_ready")
        biased = mem.sem("biased")
        product = mem.sem("product")
        summed = mem.sem("summed")
        stats_ready = mem.sem("stats_ready")
        moments_ready = mem.sem("moments_ready")
        deviation_ready = mem.sem("deviation_ready")
        factor_ready = mem.sem("factor_ready")
        normalised = mem.sem("normalised")
        turned = mem.sem("turned")
        turned_copied = mem.sem("turned_copied")
        stored = [mem.sem(f"stored{n}") for n in range(2)]
        turned_stored = [mem.sem(f"turned_stored{n}") for n in range(2)]
        alone = mem.sem("alone")
        block = ctx.enter_context(nc.Block())

        @block.sync
        def _(sp):
            sp.dma_start(weights[:, :, :], w.rearrange("(r p) n -> p r n", p=P)).then_inc(weights_in, 16)
            sp.dma_start(bias_all[:, :], by_partition(bias, 0, [[0, P], [1, D_MODEL]])).then_inc(weights_in, 16)
            with sp.Fori(0, turns) as turn:
                for half in range(2):
                    sp.wait_ge(summed, tiles * (2 * turn + half))
                    sp.dma_start(src[half][:, :, :],
                                 a_t[2 * turn + half].rearrange("(r p) t -> p r t", p=P)).then_inc(src_in[half], 16)
                    sp.wait_ge(stored[half], 16 * turn)
                    stand(sp, alone)
                    if out_t is not None:
                        sp.wait_ge(turned, 2 * tiles * turn)
                    sp.dma_start(res[half][:, :, :],
                                 residual[2 * turn + half].rearrange("(t p) n -> p t n", p=P)).then_inc(src_in[half], 16)

        @block.gpsimd
        def _(pool):
            identity_matrix(pool, nc, ident, ident_zeroed, ident_ready)
            pool.wait_ge(weights_in, 32)
            with pool.Fori(0, turns) as turn:
                for half in range(2):
                    pool.wait_ge(src_in[half], 32 * (turn + 1))
                    for tile in range(tiles):
                        nc.gpsimd.tensor_tensor(res[half][:, tile, :], res[half][:, tile, :], bias_all[:, :],
                                                ALU.add).then_inc(biased, 1)

        @block.tensor
        def _(pe):
            pe.wait_ge(weights_in, 32)
            pe.wait_ge(ident_ready, 1)
            with pe.Fori(0, turns) as turn:
                for half in range(2):
                    pe.wait_ge(src_in[half], 32 * (turn + 1))
                    for tile in range(tiles):
                        pe.wait_ge(summed, tiles * (2 * turn + half) + tile + 1)
                        for r in range(CHUNKS):
                            last = nc.tensor.matmul(ps[:, tile, :], src[half][:, r, tile * P:(tile + 1) * P],
                                                    weights[:, r, :], start=(r == 0), stop=(r == CHUNKS - 1))
                        last.then_inc(product, 1)
                if out_t is not None:
                    for half in range(2):
                        for tile in range(tiles):
                            number = tiles * (2 * turn + half) + tile
                            pe.wait_ge(normalised, number + 1)
                            pe.wait_ge(turned_copied, number + 1)
                            for chunk in range(CHUNKS):
                                last = nc.tensor.transpose(ps_turned[:, tile % 2, chunk * P:(chunk + 1) * P],
                                                           res[half][:, tile, chunk * P:(chunk + 1) * P], ident[:, :])
                            last.then_inc(turned, 1)

        @block.scalar
        def _(act):
            act.wait_ge(summed, tiles)
            with act.Fori(0, turns) as turn:
                for half in range(2):
                    act.wait_ge(moments_ready, tiles * (2 * turn + half + 1))
                    nc.scalar.activation(deviation[half][:, :], moments[half][:, :, 1], ACT.Sqrt,
                                         bias=eps[:, :]).then_inc(deviation_ready, 1)
                    act.wait_ge(normalised, tiles * (2 * turn + half + 1))
                    act.dma_start(out[2 * turn + half].rearrange("(t p) n -> p t n", p=P),
                                  res[half][:, :, :]).then_inc(stored[half], 16)
                if out_t is not None:
                    for half in range(2):
                        act.wait_ge(turned_stored[half], 16 * turn)
                        for tile in range(tiles):
                            act.wait_ge(turned, tiles * (2 * turn + half) + tile + 1)
                            nc.scalar.activation(
                                turned_out[half][:, :, tile * P:(tile + 1) * P],
                                ps_turned[:, tile % 2, :].rearrange("p (c t) -> p c t", c=CHUNKS),
                                ACT.Copy).then_inc(turned_copied, 1)
                        act.wait_ge(turned_copied, tiles * (2 * turn + half + 1) + 2)
                        act.dma_start(out_t[2 * turn + half].rearrange("(c p) t -> p c t", p=P),
                                      turned_out[half][:, :, :]).then_inc(turned_stored[half], 16)
            for half in range(2):
                act.wait_ge(stored[half], 16 * turns)
                if out_t is not None:
                    act.wait_ge(turned_stored[half], 16 * turns)

        @block.vector
        def _(dve):
            nc.vector.memset(eps[:, :], LN_EPS).then_inc(summed, tiles)
            if out_t is not None:
                dve.sem_inc(turned_copied, 2)
            with dve.Fori(0, turns) as turn:
                for half in range(2):
                    batch = 2 * turn + half
                    for tile in range(tiles):
                        number = tiles * batch + tile
                        dve.wait_ge(product, number + 1)
                        dve.wait_ge(biased, number + 1)
                        nc.vector.tensor_tensor(res[half][:, tile, :], ps[:, tile, :], res[half][:, tile, :],
                                                ALU.add).then_inc(summed, 1)
                        dve.wait_ge(summed, number + 1 + tiles)
                        nc.vector.bn_stats(stats[half][:, tile, :], res[half][:, tile, :]).then_inc(stats_ready, 1)
                        dve.wait_ge(stats_ready, number + 1)
                        stand(dve, alone)
                        nc.vector.bn_aggr(moments[half][:, tile, :], stats[half][:, tile, :]).then_inc(moments_ready, 1)
                    dve.wait_ge(deviation_ready, batch + 1)
                    nc.vector.reciprocal(factor[half][:, :], deviation[half][:, :]).then_inc(factor_ready, 1)
                    dve.wait_ge(factor_ready, batch + 1)
                    for tile in range(tiles):
                        nc.vector.tensor_scalar(res[half][:, tile, :], res[half][:, tile, :],
                                                moments[half][:, tile, 0:1], factor[half][:, tile:tile + 1],
                                                ALU.subtract, ALU.mult).then_inc(normalised, 1)


EXPERTS, SUB, HIDDEN = 16, 64, 256
PARTS = D_MODEL // SUB
TOKEN_TILES = BATCH * TOK_TILES
COLUMNS = TOKEN_TILES * PARTS
ROWS_AT_ONCE = 512
BLOCKS = (2 * BATCH * SEQ * PARTS + EXPERTS * (ROWS_AT_ONCE - 1)) // ROWS_AT_ONCE + 1
BF16 = mybir.dt.bfloat16


def feed_forward(nc, x_t, w_m, b_m, expert_emb, w_1, b_1, w_2, b_2, hidden, rows_in, rows_out, mixed_t):
    assert BLOCKS % 4 == 0
    with ExitStack() as ctx:
        mem = Memory(nc, ctx, "moe")
        weight = [mem.sbuf(f"weight{n}", [P, COLUMNS]) for n in range(2)]
        place = [mem.sbuf(f"place{n}", [P, COLUMNS], I32) for n in range(2)]
        block_expert = mem.sbuf("block_expert", [P, BLOCKS], I32)
        route(nc, x_t, w_m, b_m, expert_emb, rows_in, hidden, weight, place, block_expert)
        dispatch(nc, hidden, place, rows_in)
        run_experts(nc, w_1, b_1, w_2, b_2, block_expert, rows_in, rows_out)
        collect(nc, place, weight, rows_out, mixed_t)


def route(nc, x_t, w_m, b_m, expert_emb, rows_in, hidden, weight, place, block_expert):
    per_batch = TOK_TILES * PARTS
    turns = BATCH // 2
    zero_len = 2048
    with ExitStack() as ctx:
        mem = Memory(nc, ctx, "route")
        ident = mem.sbuf("ident", [P, P])
        weights = mem.sbuf("weights", [P, CHUNKS, D_MODEL])
        bias_all = mem.sbuf("bias_all", [P, D_MODEL])
        emb = mem.sbuf("emb", [P, 2, EXPERTS])
        zeros = mem.sbuf("zeros", [P, zero_len])
        src = [mem.sbuf(f"src{n}", [P, CHUNKS, SEQ]) for n in range(2)]
        hid = [mem.sbuf(f"hid{n}", [P, TOK_TILES, D_MODEL]) for n in range(2)]
        hid_t = [mem.sbuf(f"hid_t{n}", [P, CHUNKS, P]) for n in range(2)]
        steps_int = mem.sbuf("steps_int", [P, BLOCKS], I32)
        steps = mem.sbuf("steps", [P, BLOCKS])
        limits = mem.sbuf("limits", [P, COLUMNS // 4])
        countdown = mem.sbuf("countdown", [P, EXPERTS])
        best = mem.sbuf("best", [P, per_batch])
        second = mem.sbuf("second", [P, per_batch])
        picked = mem.sbuf("picked", [P, per_batch])
        gap = mem.sbuf("gap", [P, per_batch])
        gap_exp = mem.sbuf("gap_exp", [P, per_batch])
        exp_sum = mem.sbuf("exp_sum", [P, per_batch])
        inverse = mem.sbuf("inverse", [P, per_batch])
        work = mem.sbuf("work", [P, per_batch, EXPERTS])
        logits = mem.sbuf("logits", [P, per_batch, EXPERTS])
        exps = mem.sbuf("exps", [P, per_batch, EXPERTS])
        chosen = [mem.sbuf(f"chosen{n}", [P, COLUMNS, EXPERTS], BF16) for n in range(2)]
        mask = mem.sbuf("mask", [P, COLUMNS, EXPERTS], BF16)
        before = mem.sbuf("before", [P, P], BF16)
        ones = mem.sbuf("ones", [P, P], BF16)
        rank = mem.sbuf("rank", [P, COLUMNS, EXPERTS])
        counts = mem.sbuf("counts", [P, EXPERTS, COLUMNS])
        until = mem.sbuf("until", [P, EXPERTS, COLUMNS])
        carry = mem.sbuf("carry", [P, EXPERTS, COLUMNS])
        over = mem.sbuf("over", [P, EXPERTS * BLOCKS])
        blocks = mem.sbuf("blocks", [P, EXPERTS])
        blocks_until = mem.sbuf("blocks_until", [P, EXPERTS])
        first_row = mem.sbuf("first_row", [P, EXPERTS])
        place_float = mem.sbuf("place_float", [P, COLUMNS])
        expert_float = mem.sbuf("expert_float", [P, BLOCKS])
        ps = mem.psum("ps", [P, TOK_TILES, D_MODEL])
        ps_turned = mem.psum("ps_turned", [P, 2, D_MODEL])
        ps_logits = mem.psum("ps_logits", [P, per_batch, EXPERTS])
        weights_in = mem.sem("weights_in")
        emb_zeroed = mem.sem("emb_zeroed")
        emb_in = mem.sem("emb_in")
        zeroed = mem.sem("zeroed")
        rows_zeroed = mem.sem("rows_zeroed")
        src_in = [mem.sem(f"src_in{n}") for n in range(2)]
        ident_zeroed = mem.sem("ident_zeroed")
        ident_ready = mem.sem("ident_ready")
        masks_ready = mem.sem("masks_ready")
        product = mem.sem("product")
        summed = mem.sem("summed")
        stored = [mem.sem(f"stored{n}") for n in range(2)]
        turned = mem.sem("turned")
        turned_copied = mem.sem("turned_copied")
        scored = mem.sem("scored")
        logits_read = mem.sem("logits_read")
        chain = mem.sem("chain")
        shifted = mem.sem("shifted")
        exps_ready = mem.sem("exps_ready")
        gap_ready = mem.sem("gap_ready")
        gap_exp_ready = mem.sem("gap_exp_ready")
        mask_ready = mem.sem("mask_ready")
        counted = mem.sem("counted")
        rank_copied = mem.sem("rank_copied")
        counts_copied = mem.sem("counts_copied")
        block = ctx.enter_context(nc.Block())

        @block.sync
        def _(sp):
            sp.dma_start(weights[:, :, :], w_m.rearrange("(r p) n -> p r n", p=P)).then_inc(weights_in, 16)
            sp.dma_start(bias_all[:, :], by_partition(b_m, 0, [[0, P], [1, D_MODEL]])).then_inc(weights_in, 16)
            sp.wait_ge(emb_zeroed, 1)
            for part in range(2):
                sp.dma_start(emb[SUB * part:SUB * (part + 1), part, :], expert_emb).then_inc(emb_in, 16)
            with sp.Fori(0, turns) as turn:
                for half in range(2):
                    sp.wait_ge(product, 2 * TOK_TILES * turn)
                    sp.dma_start(src[half][:, :, :],
                                 x_t[2 * turn + half].rearrange("(r p) t -> p r t", p=P)).then_inc(src_in[half], 16)
            sp.wait_ge(zeroed, 1)
            repeats = BLOCKS * ROWS_AT_ONCE * SUB // P // zero_len
            sp.dma_start(by_partition(rows_in, 0, [[repeats * zero_len, P], [zero_len, repeats], [1, zero_len]]),
                         zeros[:, :].unsqueeze(1).to_broadcast([P, repeats, zero_len])).then_inc(rows_zeroed, 16)
            sp.wait_ge(rows_zeroed, 16)

        @block.gpsimd
        def _(pool):
            nc.gpsimd.memset(emb[:, :, :], 0.0).then_inc(emb_zeroed, 1)
            nc.gpsimd.memset(zeros[:, :], 0.0).then_inc(zeroed, 1)
            identity_matrix(pool, nc, ident, ident_zeroed, ident_ready)
            nc.gpsimd.memset(before[:, :], 0.0).then_inc(masks_ready, 1)
            nc.gpsimd.memset(ones[:, :], 1.0).then_inc(masks_ready, 1)
            nc.gpsimd.iota(steps_int[:, :], pattern=[[1, BLOCKS]], base=0, channel_multiplier=0).then_inc(masks_ready, 1)
            pool.wait_ge(masks_ready, 3)
            nc.gpsimd.affine_select(out=before[:, :], in_=before[:, :], compare_op=ALU.is_ge, fill=1.0, base=0,
                                    pattern=[[-1, P]], channel_multiplier=1).then_inc(masks_ready, 1)

        @block.tensor
        def _(pe):
            def hidden_product(batch, half, tile):
                pe.wait_ge(summed, TOK_TILES * batch + tile + 1)
                for r in range(CHUNKS):
                    last = nc.tensor.matmul(ps[:, tile, :], src[half][:, r, tile * P:(tile + 1) * P],
                                            weights[:, r, :], start=(r == 0), stop=(r == CHUNKS - 1))
                last.then_inc(product, 1)

            def transpose(batch, half, tile):
                pe.wait_ge(summed, TOK_TILES * (batch + 1) + tile + 1)
                pe.wait_ge(turned_copied, TOK_TILES * batch + tile + 1)
                for chunk in range(CHUNKS):
                    last = nc.tensor.transpose(ps_turned[:, tile % 2, chunk * P:(chunk + 1) * P],
                                               hid[half][:, tile, chunk * P:(chunk + 1) * P], ident[:, :])
                last.then_inc(turned, 1)

            def logits_product(batch, tile):
                if tile == 0:
                    pe.wait_ge(logits_read, batch)
                pe.wait_ge(turned_copied, TOK_TILES * batch + tile + 3)
                for chunk in range(CHUNKS):
                    first = tile * PARTS + 2 * chunk
                    last = nc.tensor.matmul(ps_logits[:, first:first + 2, :], hid_t[tile % 2][:, chunk, :],
                                            emb[:, :, :], start=True, stop=True)
                last.then_inc(scored, 1)

            pe.wait_ge(weights_in, 32)
            pe.wait_ge(ident_ready, 1)
            pe.wait_ge(emb_in, 32)
            with pe.Fori(0, turns) as turn:
                for half in range(2):
                    batch = 2 * turn + half
                    pe.wait_ge(src_in[half], 16 * (turn + 1))
                    for tile in range(TOK_TILES + 2):
                        if tile < TOK_TILES:
                            hidden_product(batch, half, tile)
                        if 1 <= tile <= TOK_TILES:
                            transpose(batch, half, tile - 1)
                        if tile >= 2:
                            logits_product(batch, tile - 2)
            pe.wait_ge(masks_ready, 4)
            pe.wait_ge(mask_ready, BATCH)
            with pe.Fori(0, BATCH) as batch:
                pe.wait_ge(rank_copied, batch)
                pe.wait_ge(counts_copied, batch)
                chose = mask[:, bass.ds(per_batch * batch, per_batch), :].rearrange("p c e -> p (c e)")
                nc.tensor.matmul(ps_turned[:, 0, :], before[:, :], chose, start=True, stop=True)
                nc.tensor.matmul(ps_turned[:, 1, :], ones[:, :], chose, start=True, stop=True).then_inc(counted, 1)

        @block.scalar
        def _(act):
            with act.Fori(0, turns) as turn:
                for half in range(2):
                    batch = 2 * turn + half
                    for tile in range(TOK_TILES):
                        act.wait_ge(turned, TOK_TILES * batch + tile + 1)
                        act.wait_ge(scored, TOK_TILES * batch + tile + 1)
                        nc.scalar.activation(hid_t[tile % 2][:, :, :].rearrange("p c t -> p (c t)"),
                                             ps_turned[:, tile % 2, :], ACT.Copy).then_inc(turned_copied, 1)
                    act.wait_ge(summed, TOK_TILES * (batch + 2))
                    act.dma_start(hidden[batch].rearrange("(t p) n -> p t n", p=P),
                                  hid[half][:, :, :]).then_inc(stored[half], 16)
                    act.wait_ge(shifted, batch + 1)
                    nc.scalar.activation(exps[:, :, :], work[:, :, :], ACT.Exp).then_inc(exps_ready, 1)
                    act.wait_ge(gap_ready, batch + 1)
                    nc.scalar.activation(gap_exp[:, :], gap[:, :], ACT.Exp).then_inc(gap_exp_ready, 1)
            with act.Fori(0, BATCH) as batch:
                act.wait_ge(counted, batch + 1)
                nc.scalar.activation(rank[:, bass.ds(per_batch * batch, per_batch), :].rearrange("p c e -> p (c e)"),
                                     ps_turned[:, 0, :], ACT.Copy).then_inc(rank_copied, 1)
            for half in range(2):
                act.wait_ge(stored[half], 16 * turns)

        @block.vector
        def _(dve):
            setup_steps, batch_steps = 4, 13

            def over_experts(ap, count):
                return ap.unsqueeze(2).to_broadcast([P, count, EXPERTS])

            def over_columns(ap, count):
                return ap.unsqueeze(1).to_broadcast([P, count, EXPERTS])

            def choose(values, top, batch, out, number):
                nc.vector.tensor_tensor(work[:, :, :], values, over_experts(top, per_batch),
                                        ALU.is_equal).then_inc(chain, 1)
                dve.wait_ge(chain, number + 1)
                nc.vector.tensor_tensor(work[:, :, :], work[:, :, :], over_columns(countdown[:, :], per_batch),
                                        ALU.mult).then_inc(chain, 1)
                dve.wait_ge(chain, number + 2)
                nc.vector.tensor_reduce(picked[:, :], work[:, :, :], AX_X, ALU.max).then_inc(chain, 1)
                dve.wait_ge(chain, number + 3)
                nc.vector.tensor_tensor(out[:, bass.ds(per_batch * batch, per_batch), :],
                                        over_columns(countdown[:, :], per_batch),
                                        over_experts(picked[:, :], per_batch), ALU.is_equal).then_inc(chain, 1)
                dve.wait_ge(chain, number + 4)

            dve.sem_inc(turned_copied, 2)
            dve.sem_inc(scored, 2)
            dve.sem_inc(summed, TOK_TILES)
            dve.wait_ge(masks_ready, 3)
            nc.vector.tensor_copy(steps[:, :], steps_int[:, :]).then_inc(chain, 1)
            nc.vector.memset(carry[:, :, :], 1.0).then_inc(chain, 1)
            dve.wait_ge(chain, 2)
            nc.vector.tensor_scalar(countdown[:, :], steps[:, 0:EXPERTS], -1.0, float(EXPERTS),
                                    ALU.mult, ALU.add).then_inc(chain, 1)
            nc.vector.memset(carry[:, :, 0:1], 0.0).then_inc(chain, 1)
            dve.wait_ge(chain, setup_steps)
            dve.wait_ge(weights_in, 32)
            with dve.Fori(0, turns) as turn:
                for half in range(2):
                    batch = 2 * turn + half
                    number = setup_steps + batch_steps * batch
                    dve.wait_ge(stored[half], 16 * turn)
                    for tile in range(TOK_TILES):
                        dve.wait_ge(product, TOK_TILES * batch + tile + 1)
                        nc.vector.tensor_tensor(hid[half][:, tile, :], ps[:, tile, :], bias_all[:, :],
                                                ALU.add).then_inc(summed, 1)
                    dve.wait_ge(scored, TOK_TILES * (batch + 1) + 2)
                    nc.vector.tensor_copy(logits[:, :, :], ps_logits[:, :, :]).then_inc(logits_read, 1)
                    dve.wait_ge(logits_read, batch + 1)
                    nc.vector.tensor_reduce(best[:, :], logits[:, :, :], AX_X, ALU.max).then_inc(chain, 1)
                    dve.wait_ge(chain, number + 1)
                    nc.vector.tensor_tensor(work[:, :, :], logits[:, :, :], over_experts(best[:, :], per_batch),
                                            ALU.subtract).then_inc(shifted, 1)
                    dve.wait_ge(exps_ready, batch + 1)
                    choose(logits[:, :, :], best[:, :], batch, chosen[0], number + 1)
                    nc.vector.scalar_tensor_tensor(
                        logits[:, :, :], chosen[0][:, bass.ds(per_batch * batch, per_batch), :], -BIG,
                        logits[:, :, :], ALU.mult, ALU.add).then_inc(chain, 1)
                    dve.wait_ge(chain, number + 6)
                    nc.vector.tensor_reduce(second[:, :], logits[:, :, :], AX_X, ALU.max).then_inc(chain, 1)
                    dve.wait_ge(chain, number + 7)
                    nc.vector.tensor_tensor(gap[:, :], second[:, :], best[:, :], ALU.subtract).then_inc(gap_ready, 1)
                    choose(logits[:, :, :], second[:, :], batch, chosen[1], number + 7)
                    nc.vector.tensor_tensor(mask[:, bass.ds(per_batch * batch, per_batch), :],
                                            chosen[0][:, bass.ds(per_batch * batch, per_batch), :],
                                            chosen[1][:, bass.ds(per_batch * batch, per_batch), :],
                                            ALU.add).then_inc(mask_ready, 1)
                    nc.vector.tensor_reduce(exp_sum[:, :], exps[:, :, :], AX_X, ALU.add).then_inc(chain, 1)
                    dve.wait_ge(chain, number + 12)
                    nc.vector.reciprocal(weight[0][:, bass.ds(per_batch * batch, per_batch)],
                                         exp_sum[:, :]).then_inc(chain, 1)
                    dve.wait_ge(chain, number + 13)
                    dve.wait_ge(gap_exp_ready, batch + 1)
                    nc.vector.tensor_tensor(weight[1][:, bass.ds(per_batch * batch, per_batch)], gap_exp[:, :],
                                            weight[0][:, bass.ds(per_batch * batch, per_batch)], ALU.mult)
            with dve.Fori(0, BATCH) as batch:
                dve.wait_ge(counted, batch + 1)
                nc.vector.tensor_copy(counts[:, :, bass.ds(per_batch * batch, per_batch)],
                                      ps_turned[:, 1, :].rearrange("p (c e) -> p e c", e=EXPERTS)
                                      ).then_inc(counts_copied, 1)
            dve.wait_ge(counts_copied, BATCH)

            done = [setup_steps + batch_steps * BATCH]

            def then(instruction):
                done[0] += 1
                instruction.then_inc(chain, 1)
                dve.wait_ge(chain, done[0])

            flat = "p e c -> p (e c)"
            then(nc.vector.tensor_tensor_scan(until[:, :, :].rearrange(flat), carry[:, :, :].rearrange(flat),
                                              counts[:, :, :].rearrange(flat), 0.0, ALU.mult, ALU.add))
            then(nc.vector.tensor_tensor(counts[:, :, :].rearrange(flat), until[:, :, :].rearrange(flat),
                                         counts[:, :, :].rearrange(flat), ALU.subtract))
            most = COLUMNS // 4
            then(nc.vector.tensor_scalar(limits[:, :], steps[:, 0:most], float(ROWS_AT_ONCE), None, ALU.mult))
            is_over = over[:, 0:EXPERTS * most].rearrange("p (e k) -> p e k", e=EXPERTS)
            then(nc.vector.tensor_tensor(is_over, until[:, :, COLUMNS - 1:COLUMNS].to_broadcast([P, EXPERTS, most]),
                                         limits[:, :].unsqueeze(1).to_broadcast([P, EXPERTS, most]), ALU.is_gt))
            then(nc.vector.tensor_reduce(blocks[:, :], is_over, AX_X, ALU.add))
            then(nc.vector.tensor_tensor_scan(blocks_until[:, :], carry[:, 0, 1:EXPERTS + 1], blocks[:, :], 0.0,
                                              ALU.mult, ALU.add))
            then(nc.vector.tensor_tensor(first_row[:, :], blocks_until[:, :], blocks[:, :], ALU.subtract))
            then(nc.vector.tensor_scalar(first_row[:, :], first_row[:, :], float(ROWS_AT_ONCE), None, ALU.mult))
            then(nc.vector.tensor_tensor(counts[:, :, :], counts[:, :, :],
                                         first_row[:, :].unsqueeze(2).to_broadcast([P, EXPERTS, COLUMNS]), ALU.add))
            dve.wait_ge(rank_copied, BATCH)
            then(nc.vector.tensor_tensor(rank[:, :, :], rank[:, :, :], counts[:, :, :].rearrange("p e c -> p c e"),
                                         ALU.add))
            by_column = until[:, :, :].rearrange(flat).rearrange("p (c e) -> p c e", e=EXPERTS)
            for n in range(2):
                then(nc.vector.tensor_tensor(by_column, rank[:, :, :], chosen[n][:, :, :], ALU.mult))
                then(nc.vector.tensor_reduce(place_float[:, :], by_column, AX_X, ALU.add))
                then(nc.vector.tensor_copy(place[n][:, :], place_float[:, :]))
            is_past = over[:, :].rearrange("p (b e) -> p b e", e=EXPERTS)
            then(nc.vector.tensor_tensor(is_past, steps[:, :].unsqueeze(2).to_broadcast([P, BLOCKS, EXPERTS]),
                                         blocks_until[:, :].unsqueeze(1).to_broadcast([P, BLOCKS, EXPERTS]),
                                         ALU.is_ge))
            then(nc.vector.tensor_reduce(expert_float[:, :], is_past, AX_X, ALU.add))
            then(nc.vector.tensor_scalar(expert_float[:, :], expert_float[:, :], float(EXPERTS - 1), None, ALU.min))
            then(nc.vector.tensor_copy(block_expert[:, :], expert_float[:, :]))


def dispatch(nc, hidden, place, rows_in):
    turns = TOKEN_TILES // 2
    with ExitStack() as ctx:
        mem = Memory(nc, ctx, "dispatch")
        tokens = [mem.sbuf(f"tokens{n}", [P, D_MODEL]) for n in range(2)]
        places = [mem.sbuf(f"places{n}", [P, 2, PARTS], I32) for n in range(2)]
        tokens_in = [mem.sem(f"tokens_in{n}") for n in range(2)]
        places_in = mem.sem("places_in")
        sent = [mem.sem(f"sent{n}") for n in range(2)]
        alone = mem.sem("alone")
        block = ctx.enter_context(nc.Block())
        per_tile = 16 * 2 * PARTS

        @block.sync
        def _(sp):
            with sp.Fori(0, turns) as turn:
                for half in range(2):
                    sp.wait_ge(sent[half], per_tile * turn)
                    sp.dma_start(tokens[half][:, :],
                                 by_partition(hidden, (2 * turn + half) * (P * D_MODEL), [[D_MODEL, P], [1, D_MODEL]])
                                 ).then_inc(tokens_in[half], 16)

        @block.vector
        def _(dve):
            with dve.Fori(0, turns) as turn:
                for half in range(2):
                    dve.wait_ge(sent[half], per_tile * turn)
                    for n in range(2):
                        nc.vector.tensor_copy(places[half][:, n, :],
                                              place[n][:, bass.ds(PARTS * (2 * turn + half), PARTS)]
                                              ).then_inc(places_in, 1)

        @block.gpsimd
        def _(pool):
            with pool.Fori(0, turns) as turn:
                for half in range(2):
                    pool.wait_ge(tokens_in[half], 16 * (turn + 1))
                    pool.wait_ge(places_in, 2 * (2 * turn + half + 1))
                    stand(pool, alone)
                    for n in range(2):
                        for part in range(PARTS):
                            pool.indirect_dma_start(
                                out=rows_in, out_offset=bass.IndirectOffsetOnAxis(
                                    ap=places[half][:, n, part:part + 1], axis=0),
                                in_=tokens[half][:, part * SUB:(part + 1) * SUB], in_offset=None
                            ).then_inc(sent[half], 16)
            for half in range(2):
                pool.wait_ge(sent[half], per_tile * turns)


def run_experts(nc, w_1, b_1, w_2, b_2, block_expert, rows_in, rows_out):
    slots = 4
    turns = BLOCKS // slots
    quarters = ROWS_AT_ONCE // P
    parts = HIDDEN // P
    depth = 96
    with ExitStack() as ctx:
        mem = Memory(nc, ctx, "experts")
        ident = mem.sbuf("ident", [P, P])
        rows = [mem.sbuf(f"rows{n}", [P, quarters, SUB]) for n in range(slots)]
        first = [mem.sbuf(f"first{n}", [depth, HIDDEN]) for n in range(slots)]
        second = [mem.sbuf(f"second{n}", [P, parts, SUB]) for n in range(slots)]
        bias = [mem.sbuf(f"bias{n}", [P, SUB]) for n in range(slots)]
        rows_t = [mem.sbuf(f"rows_t{n}", [depth, ROWS_AT_ONCE]) for n in range(2)]
        middle = [mem.sbuf(f"middle{n}", [P, parts, ROWS_AT_ONCE]) for n in range(2)]
        result = [mem.sbuf(f"result{n}", [P, quarters, SUB]) for n in range(2)]
        ps_turned = mem.psum("ps_turned", [P, 2, ROWS_AT_ONCE])
        ps_middle = mem.psum("ps_middle", [P, 2 * parts, ROWS_AT_ONCE])
        ps_result = mem.psum("ps_result", [P, 2, 512])
        ident_zeroed = mem.sem("ident_zeroed")
        ident_ready = mem.sem("ident_ready")
        padded = mem.sem("padded")
        rows_arrived = [mem.sem(f"rows_arrived{n}") for n in range(slots)]
        first_in = [mem.sem(f"first_in{n}") for n in range(slots)]
        second_in = [mem.sem(f"second_in{n}") for n in range(slots)]
        turned = mem.sem("turned")
        turned_copied = mem.sem("turned_copied")
        multiplied = mem.sem("multiplied")
        activated = mem.sem("activated")
        produced = mem.sem("produced")
        biased = mem.sem("biased")
        stored = [mem.sem(f"stored{n}") for n in range(2)]
        alone = mem.sem("alone")
        block = ctx.enter_context(nc.Block())

        @block.sync
        def _(sp):
            for half in range(2):
                sp.sem_inc(stored[half], 16)
            sp.wait_ge(padded, 2 * slots)
            with sp.Fori(0, turns) as turn:
                for slot in range(slots):
                    number = slots * turn + slot
                    sp.wait_ge(turned, number + 1)
                    stand(sp, alone)
                    sp.dma_start(rows[slot][:, :, :],
                                 by_partition(rows_in, number * (ROWS_AT_ONCE * SUB),
                                              [[quarters * SUB, P], [SUB, quarters], [1, SUB]])
                                 ).then_inc(rows_arrived[slot], 16)
                    expert = sp.value_load(block_expert[0:1, bass.ds(number, 1)], min_val=0, max_val=EXPERTS - 1)
                    sp.wait_ge(multiplied, number + 1)
                    sp.dma_start(first[slot][0:SUB, :],
                                 by_partition(w_1, expert * (SUB * HIDDEN), [[HIDDEN, SUB], [1, HIDDEN]])
                                 ).then_inc(first_in[slot], 16)
                    sp.dma_start(first[slot][SUB:SUB + 1, :],
                                 by_partition(b_1, expert * HIDDEN, [[HIDDEN, 1], [1, HIDDEN]])
                                 ).then_inc(first_in[slot], 16)
                    sp.wait_ge(biased, number + 1)
                    sp.dma_start(second[slot][:, :, :],
                                 by_partition(w_2, expert * (HIDDEN * SUB), [[SUB, P], [P * SUB, parts], [1, SUB]])
                                 ).then_inc(second_in[slot], 16)
                    sp.dma_start(bias[slot][:, :],
                                 by_partition(b_2, expert * SUB, [[0, P], [1, SUB]])).then_inc(second_in[slot], 16)

        @block.gpsimd
        def _(pool):
            identity_matrix(pool, nc, ident, ident_zeroed, ident_ready)

        @block.tensor
        def _(pe):
            def transpose(turn, slot):
                half = slot % 2
                pe.wait_ge(rows_arrived[slot], 16 * (turn + 1))
                pe.wait_ge(turned_copied, slots * turn + slot + 1)
                stand(pe, alone)
                for quarter in range(quarters):
                    last = nc.tensor.transpose(ps_turned[0:SUB, half, quarter * P:(quarter + 1) * P],
                                               rows[slot][:, quarter, :], ident[:, :])
                last.then_inc(turned, 1)

            def first_product(turn, slot):
                number, half = slots * turn + slot, slot % 2
                pe.wait_ge(turned_copied, number + 3)
                pe.wait_ge(first_in[slot], 32 * (turn + 1))
                pe.wait_ge(activated, parts * (number + 1))
                for part in range(parts):
                    last = nc.tensor.matmul(ps_middle[:, parts * half + part, :],
                                            first[slot][:, part * P:(part + 1) * P], rows_t[half][:, :],
                                            start=True, stop=True)
                last.then_inc(multiplied, 1)

            def second_product(turn, slot):
                number, half = slots * turn + slot, slot % 2
                pe.wait_ge(activated, parts * (number + 3))
                pe.wait_ge(second_in[slot], 32 * (turn + 1))
                pe.wait_ge(biased, number + slots - 1)
                for quarter in range(quarters):
                    for part in range(parts):
                        last = nc.tensor.matmul(ps_result[:, half, quarter * SUB:(quarter + 1) * SUB],
                                                middle[half][:, part, quarter * P:(quarter + 1) * P],
                                                second[slot][:, part, :],
                                                start=(part == 0), stop=(part == parts - 1))
                last.then_inc(produced, 1)

            def turn_program(turn, has_next):
                for slot in range(slots):
                    if has_next or slot + 2 < slots:
                        transpose(turn + (slot + 2) // slots, (slot + 2) % slots)
                    if has_next or slot + 1 < slots:
                        first_product(turn + (slot + 1) // slots, (slot + 1) % slots)
                    second_product(turn, slot)

            pe.wait_ge(ident_ready, 1)
            transpose(0, 0)
            transpose(0, 1)
            first_product(0, 0)
            with pe.Fori(0, turns - 1) as turn:
                turn_program(turn, True)
            turn_program(turns - 1, False)

        @block.scalar
        def _(act):
            act.sem_inc(activated, 2 * parts)

            def activate(turn, slot):
                number, half = slots * turn + slot, slot % 2
                act.wait_ge(multiplied, number + slots + 1)
                act.wait_ge(produced, number + 1)
                for part in range(parts):
                    nc.scalar.activation(middle[half][:, part, :], ps_middle[:, parts * half + part, :],
                                         ACT.Gelu).then_inc(activated, 1)

            def store(turn, slot):
                number = slots * turn + slot
                act.wait_ge(biased, number + slots + 1)
                stand(act, alone)
                act.dma_start(by_partition(rows_out, number * (ROWS_AT_ONCE * SUB),
                                           [[quarters * SUB, P], [SUB, quarters], [1, SUB]]),
                              result[slot % 2][:, :, :]).then_inc(stored[slot % 2], 16)

            def turn_program(turn, has_next):
                for slot in range(slots):
                    if has_next or slot + 2 < slots:
                        activate(turn + (slot + 2) // slots, (slot + 2) % slots)
                    store(turn, slot)

            activate(0, 0)
            activate(0, 1)
            with act.Fori(0, turns - 1) as turn:
                turn_program(turn, True)
            turn_program(turns - 1, False)
            for half in range(2):
                act.wait_ge(stored[half], 16 * (BLOCKS // 2 + 1))

        @block.vector
        def _(dve):
            dve.sem_inc(turned, slots)
            dve.sem_inc(turned_copied, 2)
            dve.sem_inc(multiplied, slots)
            dve.sem_inc(produced, 2)
            dve.sem_inc(biased, slots)
            for n in range(slots):
                nc.vector.memset(first[n][SUB:depth, :], 0.0).then_inc(padded, 1)
            for n in range(2):
                nc.vector.memset(rows_t[n][SUB:depth, :], 1.0).then_inc(padded, slots // 2)
            dve.wait_ge(padded, 2 * slots)

            def copy_turned(turn, slot):
                number, half = slots * turn + slot, slot % 2
                dve.wait_ge(turned, number + slots + 1)
                dve.wait_ge(multiplied, number + slots - 1)
                nc.vector.tensor_copy(rows_t[half][0:SUB, :], ps_turned[0:SUB, half, :]).then_inc(turned_copied, 1)

            def add_bias(turn, slot):
                number, half = slots * turn + slot, slot % 2
                dve.wait_ge(produced, number + 3)
                dve.wait_ge(stored[half], 16 * (number // 2 + 1))
                nc.vector.tensor_tensor(
                    result[half][:, :, :],
                    ps_result[:, half, 0:quarters * SUB].rearrange("p (q n) -> p q n", q=quarters),
                    bias[slot][:, :].unsqueeze(1).to_broadcast([P, quarters, SUB]), ALU.add).then_inc(biased, 1)

            def turn_program(turn, has_next):
                for slot in range(slots):
                    if has_next or slot + 2 < slots:
                        copy_turned(turn + (slot + 2) // slots, (slot + 2) % slots)
                    add_bias(turn, slot)

            copy_turned(0, 0)
            copy_turned(0, 1)
            with dve.Fori(0, turns - 1) as turn:
                turn_program(turn, True)
            turn_program(turns - 1, False)


def collect(nc, place, weight, rows_out, mixed_t):
    turns = TOKEN_TILES // 2
    with ExitStack() as ctx:
        mem = Memory(nc, ctx, "collect")
        ident = mem.sbuf("ident", [P, P])
        places = [mem.sbuf(f"places{n}", [P, 2, PARTS], I32) for n in range(2)]
        rows = [mem.sbuf(f"rows{n}", [P, 2, PARTS, SUB]) for n in range(2)]
        scaled = [mem.sbuf(f"scaled{n}", [P, 2, PARTS, SUB]) for n in range(2)]
        mixed = [mem.sbuf(f"mixed{n}", [P, D_MODEL]) for n in range(2)]
        turned_out = [mem.sbuf(f"turned_out{n}", [P, CHUNKS, P]) for n in range(2)]
        ps_turned = mem.psum("ps_turned", [P, 2, D_MODEL])
        ident_zeroed = mem.sem("ident_zeroed")
        ident_ready = mem.sem("ident_ready")
        places_in = mem.sem("places_in")
        fetched = [mem.sem(f"fetched{n}") for n in range(2)]
        scaled_ready = mem.sem("scaled_ready")
        mixed_ready = mem.sem("mixed_ready")
        turned = mem.sem("turned")
        turned_copied = mem.sem("turned_copied")
        stored = [mem.sem(f"stored{n}") for n in range(2)]
        alone = mem.sem("alone")
        block = ctx.enter_context(nc.Block())
        per_tile = 16 * 2 * PARTS

        @block.gpsimd
        def _(pool):
            identity_matrix(pool, nc, ident, ident_zeroed, ident_ready)
            with pool.Fori(0, turns) as turn:
                for half in range(2):
                    pool.wait_ge(places_in, 2 * (2 * turn + half + 1))
                    pool.wait_ge(scaled_ready, 4 * turn)
                    stand(pool, alone)
                    for n in range(2):
                        for part in range(PARTS):
                            pool.indirect_dma_start(
                                out=rows[half][:, n, part, :], out_offset=None, in_=rows_out,
                                in_offset=bass.IndirectOffsetOnAxis(ap=places[half][:, n, part:part + 1], axis=0)
                            ).then_inc(fetched[half], 16)

        @block.vector
        def _(dve):
            with dve.Fori(0, turns) as turn:
                for half in range(2):
                    dve.wait_ge(fetched[half], per_tile * turn)
                    for n in range(2):
                        nc.vector.tensor_copy(places[half][:, n, :],
                                              place[n][:, bass.ds(PARTS * (2 * turn + half), PARTS)]
                                              ).then_inc(places_in, 1)
                for half in range(2):
                    number = 2 * turn + half
                    dve.wait_ge(fetched[half], per_tile * (turn + 1))
                    dve.wait_ge(mixed_ready, 2 * turn)
                    for n in range(2):
                        nc.vector.tensor_tensor(
                            scaled[half][:, n, :, :], rows[half][:, n, :, :],
                            weight[n][:, bass.ds(PARTS * number, PARTS)].unsqueeze(2).to_broadcast([P, PARTS, SUB]),
                            ALU.mult).then_inc(scaled_ready, 1)
                    dve.wait_ge(scaled_ready, 2 * (number + 1))
                    dve.wait_ge(turned, 2 * turn)
                    nc.vector.tensor_tensor(mixed[half][:, :], scaled[half][:, 0, :, :].rearrange("p a b -> p (a b)"),
                                            scaled[half][:, 1, :, :].rearrange("p a b -> p (a b)"),
                                            ALU.add).then_inc(mixed_ready, 1)

        @block.tensor
        def _(pe):
            pe.wait_ge(ident_ready, 1)
            with pe.Fori(0, turns) as turn:
                for half in range(2):
                    pe.wait_ge(mixed_ready, 2 * turn + half + 1)
                    pe.wait_ge(turned_copied, 2 * turn)
                    for chunk in range(CHUNKS):
                        last = nc.tensor.transpose(ps_turned[:, half, chunk * P:(chunk + 1) * P],
                                                   mixed[half][:, chunk * P:(chunk + 1) * P], ident[:, :])
                    last.then_inc(turned, 1)

        @block.scalar
        def _(act):
            with act.Fori(0, turns) as turn:
                for half in range(2):
                    number = 2 * turn + half
                    act.wait_ge(turned, number + 1)
                    act.wait_ge(stored[half], 16 * turn)
                    nc.scalar.activation(turned_out[half][:, :, :].rearrange("p c t -> p (c t)"),
                                         ps_turned[:, half, :], ACT.Copy).then_inc(turned_copied, 1)
                    act.wait_ge(turned_copied, number + 1)
                    act.dma_start(by_partition(mixed_t, (number // TOK_TILES) * (D_MODEL * SEQ)
                                               + (number % TOK_TILES) * P,
                                               [[SEQ, P], [P * SEQ, CHUNKS], [1, P]]),
                                  turned_out[half][:, :, :]).then_inc(stored[half], 16)
            for half in range(2):
                act.wait_ge(stored[half], 16 * turns)


def decoder_block(nc, x, x_t, ctx_t, w, out):

    def scratch(name, *shape):
        return nc.dram_tensor(name, list(shape), F32).ap()

    def activations(name):
        return scratch(name, BATCH, SEQ, D_MODEL)

    q_t, k_t, v = activations("q_t"), activations("k_t"), activations("v")
    attended_t = activations("attended_t")
    first, first_t = activations("first"), activations("first_t")
    second, second_t = activations("second"), activations("second_t")

    project(nc, "self", x_t, x_t, [w[f"self_w{n}"] for n in "qkv"], [w[f"self_b{n}"] for n in "qkv"], q_t, k_t, v)
    attend(nc, "self", q_t, k_t, v, attended_t,
           rel=(w["relative_k_t"], w["relative_v"], scratch("relative_scores", TILES * P * PITCH)))
    finish(nc, "self", attended_t, w["self_wo"], w["self_bo"], x, first, first_t)

    project(nc, "cross", first_t, ctx_t, [w[f"cross_w{n}"] for n in "qkv"], [w[f"cross_b{n}"] for n in "qkv"],
            q_t, k_t, v)
    attend(nc, "cross", q_t, k_t, v, attended_t)
    finish(nc, "cross", attended_t, w["cross_wo"], w["cross_bo"], first, second, second_t)

    rows = [scratch(name, BLOCKS * ROWS_AT_ONCE, SUB) for name in ("rows_in", "rows_out")]
    feed_forward(nc, second_t, w["ffn_wm"], w["ffn_bm"], w["expert_emb"], w["w1"], w["b1"], w["w2"], w["b2"],
                 activations("hidden"), *rows, attended_t)
    finish(nc, "ffn", attended_t, w["ffn_wo"], w["ffn_bo"], second, out)


def kernel(x, ctx_768, L0_attn_Wq, L0_attn_bq, L0_attn_Wk, L0_attn_bk, L0_attn_Wv, L0_attn_bv, L0_attn_Wo, L0_attn_bo,
           L0_attn_relative_k, L0_attn_relative_v, L0_xattn_Wq, L0_xattn_bq, L0_xattn_Wk, L0_xattn_bk, L0_xattn_Wv,
           L0_xattn_bv, L0_xattn_Wo, L0_xattn_bo, L0_ffn_Wm, L0_ffn_bm, L0_ffn_expert_emb, L0_ffn_W1, L0_ffn_b1,
           L0_ffn_W2, L0_ffn_b2, L0_ffn_Wo, L0_ffn_bo):
    from concourse import bacc
    from concourse.bass_utils import run_bass_kernel_spmd

    arrays = {
        "x": x, "x_t": np.transpose(x, (0, 2, 1)), "ctx_t": np.transpose(ctx_768, (0, 2, 1)),
        "self_wq": np.transpose(L0_attn_Wq), "self_wk": np.transpose(L0_attn_Wk), "self_wv": np.transpose(L0_attn_Wv),
        "self_wo": np.transpose(L0_attn_Wo), "self_bq": L0_attn_bq, "self_bk": L0_attn_bk, "self_bv": L0_attn_bv,
        "self_bo": L0_attn_bo, "relative_k_t": np.transpose(L0_attn_relative_k), "relative_v": L0_attn_relative_v,
        "cross_wq": L0_xattn_Wq, "cross_wk": L0_xattn_Wk, "cross_wv": L0_xattn_Wv, "cross_wo": L0_xattn_Wo,
        "cross_bq": L0_xattn_bq, "cross_bk": L0_xattn_bk, "cross_bv": L0_xattn_bv, "cross_bo": L0_xattn_bo,
        "ffn_wm": L0_ffn_Wm, "ffn_bm": L0_ffn_bm, "expert_emb": L0_ffn_expert_emb, "w1": L0_ffn_W1, "b1": L0_ffn_b1,
        "w2": L0_ffn_W2, "b2": L0_ffn_b2, "ffn_wo": L0_ffn_Wo, "ffn_bo": L0_ffn_bo,
    }
    arrays = {name: np.ascontiguousarray(a) for name, a in arrays.items()}
    nc = bacc.Bacc("TRN2", target_bir_lowering=False, num_devices=1)
    w = {name: nc.dram_tensor(f"in_{name}", a.shape, F32, kind="ExternalInput").ap() for name, a in arrays.items()}
    out = nc.dram_tensor("out", [BATCH, SEQ, D_MODEL], F32, kind="ExternalOutput").ap()
    decoder_block(nc, w["x"], w["x_t"], w["ctx_t"], w, out)
    result = run_bass_kernel_spmd(nc, [{f"in_{name}": a for name, a in arrays.items()}], core_ids=[0])
    return result.results[0]["out"]
```

```python
from contextlib import ExitStack

import numpy as np

import concourse.bass as bass
from concourse import mybir

ACT = mybir.ActivationFunctionType
ALU = mybir.AluOpType
AX_X = mybir.AxisListType.X
F32 = mybir.dt.float32
BF16 = mybir.dt.bfloat16
I32 = mybir.dt.int32
U32 = mybir.dt.uint32

P = 128
BATCH, SEQ, D_MODEL, D_CTX = 8, 512, 512, 384
HEADS, D_HEAD = 16, 32
CHUNKS = D_MODEL // P
TOK_TILES = SEQ // P
HEADS_PER_CHUNK = P // D_HEAD
SCALE = float(1.0 / np.sqrt(np.float32(D_HEAD)))
LN_EPS = 1e-5


class Memory:

    def __init__(self, nc, ctx, stage):
        self.nc, self.ctx, self.stage, self.sems = nc, ctx, stage, []
        ctx.callback(self.clear)

    def sbuf(self, name, shape, dtype=F32):
        return self.ctx.enter_context(self.nc.sbuf_tensor(f"{self.stage}_{name}", shape, dtype))

    def psum(self, name, shape, dtype=F32):
        return self.ctx.enter_context(self.nc.psum_tensor(f"{self.stage}_{name}", shape, dtype))

    def sem(self, name):
        self.sems.append(self.nc.alloc_semaphore(name=f"{self.stage}_{name}"))
        return self.sems[-1]

    def clear(self):
        if self.sems:
            self.nc.clear_and_free_semaphores(self.sems)
            self.nc.all_engine_barrier()


def stand(engine, alone):
    engine.sem_inc(alone, 1)


def by_partition(ap, offset, dims):
    return bass.AP(ap.tensor, ap.offset + offset, dims)


def project(nc, stage, q_src, kv_src, weights, biases, q_out, k_out, v_out):
    q_rows, kv_rows = q_src.shape[1] // P, kv_src.shape[1] // P
    w_q, w_k, w_v = weights
    b_q, b_k, b_v = biases
    banks = 4
    turns = BATCH // 2
    with ExitStack() as ctx:
        mem = Memory(nc, ctx, f"{stage}_project")
        wq = mem.sbuf("wq", [P, q_rows, D_MODEL])
        wk = mem.sbuf("wk", [P, kv_rows, D_MODEL])
        wv = mem.sbuf("wv", [P, kv_rows, D_MODEL])
        bias_q = mem.sbuf("bias_q", [P, CHUNKS])
        bias_k = mem.sbuf("bias_k", [P, CHUNKS])
        bias_k_scaled = mem.sbuf("bias_k_scaled", [P, CHUNKS])
        bias_v = mem.sbuf("bias_v", [P, D_MODEL])
        src_q = [mem.sbuf(f"src_q{n}", [P, q_rows, SEQ]) for n in range(2)]
        src_kv = [mem.sbuf(f"src_kv{n}", [P, kv_rows, SEQ]) for n in range(2)]
        out_q = [mem.sbuf(f"out_q{n}", [P, CHUNKS, SEQ]) for n in range(2)]
        out_k = [mem.sbuf(f"out_k{n}", [P, CHUNKS, SEQ]) for n in range(2)]
        out_v = [mem.sbuf(f"out_v{n}", [P, TOK_TILES, D_MODEL]) for n in range(2)]
        ps_qk = mem.psum("ps_qk", [P, banks, SEQ])
        ps_v = mem.psum("ps_v", [P, banks, D_MODEL])
        weights_in = mem.sem("weights_in")
        biases_in = mem.sem("biases_in")
        bias_scaled = mem.sem("bias_scaled")
        src_in = [mem.sem(f"src_in{n}") for n in range(2)]
        src_free = mem.sem("src_free")
        qk_product = mem.sem("qk_product")
        qk_bank_free = mem.sem("qk_bank_free")
        v_product = mem.sem("v_product")
        v_bank_free = mem.sem("v_bank_free")
        qk_stored = [mem.sem(f"qk_stored{n}") for n in range(2)]
        v_stored = [mem.sem(f"v_stored{n}") for n in range(2)]
        block = ctx.enter_context(nc.Block())

        @block.sync
        def _(sp):
            sp.dma_start(wq[:, :, :], w_q.rearrange("(r p) n -> p r n", p=P)).then_inc(weights_in, 16)
            sp.dma_start(wk[:, :, :], w_k.rearrange("(r p) n -> p r n", p=P)).then_inc(weights_in, 16)
            sp.dma_start(wv[:, :, :], w_v.rearrange("(r p) n -> p r n", p=P)).then_inc(weights_in, 16)
            sp.dma_start(bias_q[:, :], b_q.rearrange("(c p) -> p c", p=P),
                         allow_slow_non_contiguous=True).then_inc(biases_in, 16)
            sp.dma_start(bias_k[:, :], b_k.rearrange("(c p) -> p c", p=P),
                         allow_slow_non_contiguous=True).then_inc(biases_in, 16)
            sp.dma_start(bias_v[:, :], by_partition(b_v, 0, [[0, P], [1, D_MODEL]])).then_inc(biases_in, 16)
            with sp.Fori(0, turns) as turn:
                for half in range(2):
                    sp.wait_ge(src_free, 2 * turn + half + 1)
                    for dst, src in ((src_q, q_src), (src_kv, kv_src)):
                        sp.dma_start(dst[half][:, :, :],
                                     src[2 * turn + half].rearrange("(r p) t -> p r t", p=P)).then_inc(src_in[half], 16)

        @block.gpsimd
        def _(pool):
            with pool.Fori(0, turns) as turn:
                for half in range(2):
                    pool.wait_ge(v_bank_free, TOK_TILES * (2 * turn + half + 1) + banks)
                    pool.dma_start(v_out[2 * turn + half].rearrange("(r p) n -> p r n", p=P),
                                   out_v[half][:, :, :]).then_inc(v_stored[half], 16)
            for half in range(2):
                pool.wait_ge(v_stored[half], 16 * turns)

        @block.tensor
        def _(pe):
            pe.sem_inc(src_free, 2)
            pe.wait_ge(weights_in, 48)
            with pe.Fori(0, turns) as turn:
                for half in range(2):
                    pe.wait_ge(src_in[half], 32 * (turn + 1))
                    groups = [(wq, src_q, q_rows)] * CHUNKS + [(wk, src_kv, kv_rows)] * CHUNKS
                    for n, (w, src, rows) in enumerate(groups):
                        chunk = n % CHUNKS
                        pe.wait_ge(qk_bank_free, 2 * CHUNKS * (2 * turn + half) + n + 1)
                        for r in range(rows):
                            last = nc.tensor.matmul(ps_qk[:, n % banks, :], w[:, r, chunk * P:(chunk + 1) * P],
                                                    src[half][:, r, :], start=(r == 0), stop=(r == rows - 1))
                        last.then_inc(qk_product, 1)
                    for t in range(TOK_TILES):
                        pe.wait_ge(v_bank_free, TOK_TILES * (2 * turn + half) + t + 1)
                        for r in range(kv_rows):
                            last = nc.tensor.matmul(ps_v[:, t % banks, :], src_kv[half][:, r, t * P:(t + 1) * P],
                                                    wv[:, r, :], start=(r == 0), stop=(r == kv_rows - 1))
                        last.then_inc(v_product, 1)
                        if t == TOK_TILES - 1:
                            pe.wait_ge(v_product, TOK_TILES * (2 * turn + half + 1))
                            pe.sem_inc(src_free, 1)

        @block.scalar
        def _(act):
            act.sem_inc(qk_bank_free, banks)
            act.wait_ge(biases_in, 48)
            nc.scalar.activation(bias_k_scaled[:, :], bias_k[:, :], ACT.Copy, scale=SCALE).then_inc(bias_scaled, 1)
            act.wait_ge(bias_scaled, 1)
            with act.Fori(0, turns) as turn:
                for half in range(2):
                    act.wait_ge(qk_stored[half], 32 * turn)
                    for n in range(2 * CHUNKS):
                        chunk = n % CHUNKS
                        out, bias, scale = ((out_q, bias_q, 1.0), (out_k, bias_k_scaled, SCALE))[n // CHUNKS]
                        act.wait_ge(qk_product, 2 * CHUNKS * (2 * turn + half) + n + 1)
                        nc.scalar.activation(out[half][:, chunk, :], ps_qk[:, n % banks, :], ACT.Identity,
                                             bias=bias[:, chunk:chunk + 1], scale=scale).then_inc(qk_bank_free, 1)
                    act.wait_ge(qk_bank_free, 2 * CHUNKS * (2 * turn + half + 1) + banks)
                    for dst, out in ((q_out, out_q), (k_out, out_k)):
                        act.dma_start(dst[2 * turn + half].rearrange("(c p) t -> p c t", p=P),
                                      out[half][:, :, :]).then_inc(qk_stored[half], 16)
            for half in range(2):
                act.wait_ge(qk_stored[half], 32 * turns)

        @block.vector
        def _(dve):
            dve.sem_inc(v_bank_free, banks)
            dve.wait_ge(biases_in, 48)
            with dve.Fori(0, turns) as turn:
                for half in range(2):
                    dve.wait_ge(v_stored[half], 16 * turn)
                    for t in range(TOK_TILES):
                        dve.wait_ge(v_product, TOK_TILES * (2 * turn + half) + t + 1)
                        nc.vector.tensor_tensor(out_v[half][:, t, :], ps_v[:, t % banks, :], bias_v[:, :],
                                                ALU.add).then_inc(v_bank_free, 1)


BATCHES_AT_ONCE = 2
ROWS = 64
UNITS_PER_PAIR = SEQ // ROWS
TILES = BATCHES_AT_ONCE * HEADS // 2
GROUPS = BATCHES_AT_ONCE * CHUNKS
WINDOW = SEQ + ROWS - 1
PITCH = WINDOW + 1
KEY_TILES = SEQ // P
BIG = 3.0e38


def identity_matrix(pool, nc, ident, zeroed, ready):
    nc.gpsimd.memset(ident[:, :], 0.0).then_inc(zeroed, 1)
    pool.wait_ge(zeroed, 1)
    nc.gpsimd.affine_select(out=ident[:, :], in_=ident[:, :], compare_op=ALU.not_equal, fill=1.0, base=0,
                            pattern=[[-1, P]], channel_multiplier=1).then_inc(ready, 1)


def attend(nc, stage, q_t, k_t, v, out_t, rel=None, beside=None):
    units = q_t.shape[0] // BATCHES_AT_ONCE * UNITS_PER_PAIR
    with ExitStack() as ctx:
        mem = Memory(nc, ctx, f"{stage}_attend")
        ident = mem.sbuf("ident", [P, P])
        queries = mem.sbuf("queries", [P, TILES, 2, ROWS])
        keys = mem.sbuf("keys", [P, BATCHES_AT_ONCE, CHUNKS, SEQ])
        values = mem.sbuf("values", [P, KEY_TILES, BATCHES_AT_ONCE, D_MODEL])
        probs = mem.sbuf("probs", [P, TILES, SEQ])
        probs_t = mem.sbuf("probs_t", [P, KEY_TILES, TILES, 2, ROWS])
        low = mem.sbuf("low", [P, TILES])
        total = mem.sbuf("total", [P, TILES])
        inverse = mem.sbuf("inverse", [P, TILES])
        out = mem.sbuf("out", [P, GROUPS, ROWS])
        ps_scores = mem.psum("ps_scores", [P, 2, SEQ])
        ps_turned = mem.psum("ps_turned", [P, 2, SEQ])
        ps_out = mem.psum("ps_out", [P, GROUPS, ROWS])
        if rel:
            rel_k_t, rel_v, scratch = rel
            raw = mem.sbuf("raw", [P, TILES * P])
            high = mem.sbuf("high", [P, TILES * P], BF16)
            middle = mem.sbuf("middle", [P, TILES * P], BF16)
            low_part = mem.sbuf("low_part", [2 * D_HEAD, TILES * P], BF16)
            rel_k_stacks = [mem.sbuf(f"rel_k_stack{n}", [rows, TILES * P // 2], BF16)
                            for n, rows in enumerate((P, 3 * D_HEAD))]
            query_stacks = [mem.sbuf(f"query_stack{n}", [rows, TILES * P], BF16)
                            for n, rows in enumerate((P, 3 * D_HEAD))]
            window_v = mem.sbuf("window_v", [P, KEY_TILES, ROWS, D_HEAD])
            shifted = [mem.sbuf(f"shifted{n}", [P, 2, PITCH]) for n in range(2)]
            rel_out = mem.sbuf("rel_out", [P, GROUPS, ROWS])
            ps_rel = mem.psum("ps_rel", [P, 2, SEQ])
            ps_rel_out = mem.psum("ps_rel_out", [P, ROWS // 4, TILES * 2])
        ident_zeroed = mem.sem("ident_zeroed")
        ident_ready = mem.sem("ident_ready")
        queries_zeroed = mem.sem("queries_zeroed")
        queries_in = mem.sem("queries_in")
        raw_in = mem.sem("raw_in")
        split_steps = mem.sem("split_steps")
        stacked = mem.sem("stacked")
        window_v_in = mem.sem("window_v_in")
        keys_in = mem.sem("keys_in")
        values_in = mem.sem("values_in")
        rel_product = mem.sem("rel_product")
        rel_copied = mem.sem("rel_copied")
        rel_stored = [mem.sem(f"rel_stored{n}") for n in range(2)]
        rel_in = [mem.sem(f"rel_in{n}") for n in range(2)]
        scored = mem.sem("scored")
        scores_read = mem.sem("scores_read")
        exps = mem.sem("exps")
        inverted = mem.sem("inverted")
        probs_ready = mem.sem("probs_ready")
        turned = mem.sem("turned")
        turned_copied = mem.sem("turned_copied")
        values_summed = mem.sem("values_summed")
        unit_done = mem.sem("unit_done")
        rel_out_act = mem.sem("rel_out_act")
        rel_out_dve = mem.sem("rel_out_dve")
        out_ready = mem.sem("out_ready")
        out_stored = mem.sem("out_stored")
        alone = mem.sem("alone")
        block = ctx.enter_context(nc.Block())

        LEAD = 8
        LAG = 3
        AHEAD = 2
        REST = 1 if rel else 0

        def store(engine, unit):
            engine.wait_ge(out_ready, unit + 1)
            engine.dma_start(
                by_partition(out_t, unit // UNITS_PER_PAIR * (BATCHES_AT_ONCE * D_MODEL * SEQ)
                             + unit % UNITS_PER_PAIR * ROWS,
                             [[SEQ, P], [P * SEQ, GROUPS], [1, ROWS]]), out[:, :, :]).then_inc(out_stored, 16)

        def relative_rows(sp, unit, row_block):
            for group in range(TILES // 2 + 1):
                if group < TILES // 2:
                    sp.wait_ge(rel_copied, TILES * unit + 2 * group + 2)
                    sp.dma_start(by_partition(scratch, 2 * group * P * PITCH,
                                              [[PITCH, P], [P * PITCH, 2], [1, WINDOW]]),
                                 shifted[group % 2][:, :, 0:WINDOW]).then_inc(rel_stored[group % 2], 16)
                if group > 0:
                    back = group - 1
                    sp.wait_ge(rel_stored[back % 2], 16 * (TILES // 4 * unit + back // 2 + 1))
                    stand(sp, alone)
                    sp.wait_ge(turned, TILES * unit + 2 * back + 2)
                    stand(sp, alone)
                    sp.wait_ge(rel_in[back % 2], 32 * (TILES // 4 * unit + back // 2))
                    for tile in range(2 * back, 2 * back + 2):
                        sp.dma_start(probs[:, tile, :],
                                     by_partition(scratch, tile * P * PITCH + ROWS - 1,
                                                  [[ROWS * PITCH, 2], [PITCH - 1, ROWS], [1, SEQ]])
                                     ).then_inc(rel_in[back % 2], 16)
                if group > LEAD // 2:
                    part = group - LEAD // 2 - 1
                    sp.wait_ge(unit_done, unit)
                    stand(sp, alone)
                    sp.dma_start(window_v[:, part, :, :],
                                 by_partition(rel_v, (SEQ - ROWS - row_block * ROWS + part * P) * D_HEAD,
                                              [[D_HEAD, P], [1, ROWS * D_HEAD]])).then_inc(window_v_in, 16)

        copies, steps = P // D_HEAD, 4

        def raw_queries(sp, unit):
            for copy in range(copies):
                sp.dma_start(raw[D_HEAD * copy:D_HEAD * (copy + 1), :].rearrange("p (h r) -> p h r", r=ROWS),
                             by_partition(q_t, unit // UNITS_PER_PAIR * (BATCHES_AT_ONCE * D_MODEL * SEQ)
                                          + unit % UNITS_PER_PAIR * ROWS,
                                          [[SEQ, D_HEAD], [D_HEAD * SEQ, 2 * TILES], [1, ROWS]])).then_inc(raw_in, 16)

        def split(engine, ops, number, width, is_first=False):
            engine.wait_ge(raw_in, 16 * copies * (number + 1))
            if not is_first:
                engine.wait_ge(stacked, 4 * number + 2)
                stand(engine, alone)
            ops.tensor_copy(high[:, 0:width], raw[:, 0:width]).then_inc(split_steps, 1)
            engine.wait_ge(split_steps, steps * number + 1)
            ops.tensor_tensor(raw[:, 0:width], raw[:, 0:width], high[:, 0:width], ALU.subtract).then_inc(split_steps, 1)
            engine.wait_ge(split_steps, steps * number + 2)
            stand(engine, alone)
            ops.tensor_copy(middle[:, 0:width], raw[:, 0:width]).then_inc(split_steps, 1)
            engine.wait_ge(split_steps, steps * number + 3)
            ops.tensor_tensor(low_part[:, 0:width], raw[0:2 * D_HEAD, 0:width], middle[0:2 * D_HEAD, 0:width],
                              ALU.subtract).then_inc(split_steps, 1)

        @block.sync
        def _(sp):
            if rel:
                for copy in range(copies):
                    sp.dma_start(raw[D_HEAD * copy:D_HEAD * (copy + 1), 0:2 * SEQ - 1], rel_k_t).then_inc(raw_in, 16)
                sp.wait_ge(split_steps, steps)
                raw_queries(sp, 0)
            sp.wait_ge(queries_zeroed, 1)
            with sp.Fori(0, units // UNITS_PER_PAIR) as pair:
                sp.wait_ge(scored, TILES * UNITS_PER_PAIR * pair)
                sp.dma_start(keys[:, :, :, :],
                             by_partition(k_t, pair * (BATCHES_AT_ONCE * D_MODEL * SEQ),
                                          [[SEQ, P], [P * SEQ, GROUPS], [1, SEQ]])).then_inc(keys_in, 16)
                sp.wait_ge(values_summed, UNITS_PER_PAIR * pair)
                for b in range(BATCHES_AT_ONCE):
                    sp.dma_start(values[:, :, b, :],
                                 by_partition(v, pair * (BATCHES_AT_ONCE * D_MODEL * SEQ) + b * SEQ * D_MODEL,
                                              [[D_MODEL, P], [P * D_MODEL, KEY_TILES], [1, D_MODEL]])
                                 ).then_inc(values_in, 16)
                with sp.Fori(0, UNITS_PER_PAIR) as row_block:
                    unit = UNITS_PER_PAIR * pair + row_block
                    sp.wait_ge(scored, TILES * unit)
                    for head in range(HEADS_PER_CHUNK):
                        sp.dma_start(
                            queries[D_HEAD * head:D_HEAD * (head + 1), head // 2:TILES:2, head % 2, :],
                            by_partition(q_t, pair * (BATCHES_AT_ONCE * D_MODEL * SEQ) + row_block * ROWS
                                         + D_HEAD * head * SEQ,
                                         [[SEQ, D_HEAD], [P * SEQ, GROUPS], [1, ROWS]])).then_inc(queries_in, 16)
                    if rel:
                        sp.wait_ge(split_steps, steps * (unit + 2))
                        stand(sp, alone)
                        raw_queries(sp, (unit + 1) % units)
                        relative_rows(sp, unit, row_block)
            if rel:
                sp.wait_ge(raw_in, 16 * copies * (units + 2))

        @block.gpsimd
        def _(pool):
            nc.gpsimd.memset(queries[:, :, :, :], 0.0).then_inc(queries_zeroed, 1)
            identity_matrix(pool, nc, ident, ident_zeroed, ident_ready)
            if rel:
                with pool.Fori(0, units - 1) as unit:
                    split(pool, nc.gpsimd, unit + 2, TILES * P)
                    store(pool, unit)
                store(pool, units - 1)
                pool.wait_ge(out_stored, 16 * units)
            elif beside:
                beside(pool)

        @block.tensor
        def _(pe):
            def relative_scores(unit, tile):
                pe.wait_ge(rel_copied, TILES * unit + tile)
                first = SEQ - ROWS - unit % UNITS_PER_PAIR * ROWS
                for bank, at, width in ((0, 0, SEQ), (1, SEQ, WINDOW - SEQ)):
                    for n in range(2):
                        last = nc.tensor.matmul(ps_rel[:, bank, 0:width], query_stacks[n][:, tile * P:(tile + 1) * P],
                                                rel_k_stacks[n][:, bass.ds(first + at, width)],
                                                start=(n == 0), stop=(n == 1))
                last.then_inc(rel_product, 1)

            def scores(unit, tile):
                pe.wait_ge(scores_read, TILES * unit + tile + 1)
                nc.tensor.matmul(ps_scores[:, tile % 2, :], queries[:, tile, :, :],
                                 keys[:, tile // (TILES // 2), tile // 2 % CHUNKS, :],
                                 start=True, stop=True).then_inc(scored, 1)

            def transpose(unit, tile):
                pe.wait_ge(probs_ready, TILES * unit + tile + 1)
                pe.wait_ge(turned_copied, TILES * unit + tile + 1)
                for part in range(KEY_TILES):
                    last = nc.tensor.transpose(ps_turned[:, tile % 2, part * P:(part + 1) * P],
                                               probs[:, tile, part * P:(part + 1) * P], ident[:, :])
                last.then_inc(turned, 1)

            def values_product(unit, group):
                b, chunk = group // CHUNKS, group % CHUNKS
                pe.wait_ge(turned_copied, TILES * unit + 2 * group + 4)
                if group == 0:
                    pe.wait_ge(out_ready, unit)
                for part in range(KEY_TILES):
                    for head in range(HEADS_PER_CHUNK):
                        first = chunk * P + head * D_HEAD
                        last = nc.tensor.matmul(ps_out[D_HEAD * head:D_HEAD * (head + 1), group, :],
                                                values[:, part, b, first:first + D_HEAD],
                                                probs_t[:, part, 2 * group + head // 2, head % 2, :],
                                                start=(part == 0), stop=(part == KEY_TILES - 1))
                if group == GROUPS - 1:
                    last.then_inc(values_summed, 1)

            def relative_values_product(unit, has_next):
                for n in range(ROWS // 4):
                    for part in range(KEY_TILES):
                        for lane in range(4):
                            row = 4 * n + lane
                            last = nc.tensor.matmul(
                                ps_rel_out[D_HEAD * lane:D_HEAD * (lane + 1), n, :],
                                window_v[:, part, ROWS - 1 - row, :],
                                probs_t[:, part, :, :, row], start=(part == 0), stop=(part == KEY_TILES - 1))
                    if has_next and n % 2 == 1:
                        relative_scores(unit + 1, n // 2)
                    if has_next and n in (8, 10):
                        first_scores(unit + 1, (n - 8) // 2)
                return last

            def arrivals(unit):
                pe.wait_ge(queries_in, 16 * HEADS_PER_CHUNK * (unit + 1))
                if rel:
                    pe.wait_ge(stacked, 4 * (unit + 2) + 2)

            def first_scores(unit, tile):
                pe.wait_ge(keys_in, 16 * (unit // UNITS_PER_PAIR + 1))
                scores(unit, tile)

            def unit_program(unit, has_next):
                pe.wait_ge(values_in, 16 * BATCHES_AT_ONCE * (unit // UNITS_PER_PAIR + 1))
                for tile in range(AHEAD, TILES + LAG):
                    ahead, behind = tile - AHEAD + LEAD, tile - LAG
                    if rel and ahead < TILES:
                        relative_scores(unit, ahead)
                    if tile < TILES:
                        scores(unit, tile)
                    if behind >= 0:
                        transpose(unit, behind)
                    if behind >= 2 and behind % 2 == 0:
                        values_product(unit, behind // 2 - 1)
                values_product(unit, GROUPS - 1)
                if has_next:
                    arrivals(unit + 1)
                if rel:
                    pe.wait_ge(window_v_in, 16 * KEY_TILES * (unit + 1))
                    pe.wait_ge(rel_out_act, 8 * unit)
                    pe.wait_ge(rel_out_dve, 8 * unit)
                    relative_values_product(unit, has_next).then_inc(unit_done, 1)
                elif has_next:
                    for tile in range(AHEAD):
                        first_scores(unit + 1, tile)

            pe.wait_ge(ident_ready, 1)
            arrivals(0)
            if rel:
                for tile in range(LEAD):
                    relative_scores(0, tile)
            for tile in range(AHEAD):
                first_scores(0, tile)
            with pe.Fori(0, units - 1) as unit:
                unit_program(unit, True)
            unit_program(units - 1, False)

        def relative_out(head, lane):
            return (rel_out[D_HEAD * head:D_HEAD * (head + 1), :, lane:ROWS:4],
                    ps_rel_out[D_HEAD * lane:D_HEAD * (lane + 1), :, head:TILES * 2:HEADS_PER_CHUNK]
                    .rearrange("p n g -> p g n"))

        @block.scalar
        def _(act):
            def copy_relative_scores(unit, tile):
                act.wait_ge(rel_product, TILES * unit + tile + 1)
                if tile % 2 == 0:
                    act.wait_ge(rel_stored[tile // 2 % 2], 16 * (TILES // 4 * unit + tile // 4))
                nc.scalar.activation(shifted[tile // 2 % 2][:, tile % 2, 0:WINDOW],
                                     ps_rel[:, :, :].rearrange("p b n -> p (b n)")[:, 0:WINDOW],
                                     ACT.Copy).then_inc(rel_copied, 1)

            def exponentials(unit, tile):
                act.wait_ge(scores_read, TILES * unit + tile + 3)
                nc.scalar.activation(probs[:, tile, :], probs[:, tile, :], ACT.Exp, bias=low[:, tile:tile + 1],
                                     scale=-1.0, accum_out=total[:, tile:tile + 1]).then_inc(exps, 1)

            def normalise(unit, tile):
                act.wait_ge(inverted, TILES * unit + tile + 1)
                nc.scalar.activation(probs[:, tile, :], probs[:, tile, :], ACT.Copy,
                                     scale=inverse[:, tile:tile + 1]).then_inc(probs_ready, 1)

            def first_tiles(unit):
                if rel:
                    for tile in range(LEAD):
                        copy_relative_scores(unit, tile)
                for tile in range(AHEAD - REST):
                    exponentials(unit, tile)
                if not REST:
                    normalise(unit, 0)

            def unit_program(unit, has_next):
                for tile in range(AHEAD, TILES + REST + 1):
                    if rel and tile - AHEAD + LEAD < TILES:
                        copy_relative_scores(unit, tile - AHEAD + LEAD)
                    if tile < TILES + REST:
                        exponentials(unit, tile - REST)
                    normalise(unit, tile - REST - 1)
                if has_next:
                    first_tiles(unit + 1)
                if rel:
                    act.wait_ge(unit_done, unit + 1)
                    act.wait_ge(out_ready, unit)
                    for head in range(HEADS_PER_CHUNK):
                        for lane in range(2):
                            nc.scalar.activation(*relative_out(head, lane), ACT.Copy).then_inc(rel_out_act, 1)
                else:
                    store(act, unit)

            first_tiles(0)
            with act.Fori(0, units - 1) as unit:
                unit_program(unit, True)
            unit_program(units - 1, False)
            if not rel:
                act.wait_ge(out_stored, 16 * units)

        @block.vector
        def _(dve):
            dve.sem_inc(scores_read, 2)
            dve.sem_inc(turned_copied, 2)
            dve.sem_inc(turned, TILES)
            if rel:
                for stacks in (rel_k_stacks, query_stacks):
                    nc.vector.memset(stacks[1][2 * D_HEAD:3 * D_HEAD, :], 0.0)

            def stack(number, stacks, width, places):
                dve.wait_ge(split_steps, steps * (number + 1))
                for n, first, end, part in places:
                    nc.vector.tensor_copy(stacks[n][D_HEAD * first:D_HEAD * end, 0:width],
                                          part[D_HEAD * first:D_HEAD * end, 0:width]).then_inc(stacked, 1)

            def stack_queries(unit):
                dve.wait_ge(rel_product, TILES * unit)
                stack(unit + 1, query_stacks, TILES * P, ((0, 0, 2, high), (0, 2, 4, middle), (1, 0, 1, high),
                                                          (1, 1, 2, low_part)))

            def read_scores(unit, tile):
                dve.wait_ge(scored, TILES * unit + tile + 1)
                if rel:
                    if tile % 2 == 0:
                        dve.wait_ge(rel_in[tile // 2 % 2], 32 * (TILES // 4 * unit + tile // 4 + 1))
                    stand(dve, alone)
                    nc.vector.tensor_tensor_reduce(
                        out=probs[:, tile, :], in0=ps_scores[:, tile % 2, :], in1=probs[:, tile, :],
                        scale=-1.0, scalar=BIG, op0=ALU.add, op1=ALU.min,
                        accum_out=low[:, tile:tile + 1]).then_inc(scores_read, 1)
                else:
                    dve.wait_ge(turned, TILES * unit + tile + 1)
                    nc.vector.tensor_scalar(
                        probs[:, tile, :], ps_scores[:, tile % 2, :], -1.0, BIG, ALU.mult, ALU.min,
                        accum_out=low[:, tile:tile + 1]).then_inc(scores_read, 1)

            def invert(unit, tile):
                dve.wait_ge(exps, TILES * unit + tile + 1)
                nc.vector.reciprocal(inverse[:, tile:tile + 1], total[:, tile:tile + 1]).then_inc(inverted, 1)

            def copy_turned(unit, tile):
                if tile == 0:
                    dve.wait_ge(unit_done if rel else values_summed, unit)
                dve.wait_ge(turned, TILES * (unit + 1) + tile + 1)
                nc.vector.tensor_copy(
                    probs_t[:, :, tile, :, :].rearrange("p k h r -> p k (h r)"),
                    ps_turned[:, tile % 2, :].rearrange("p (k r) -> p k r", k=KEY_TILES)
                ).then_inc(turned_copied, 1)

            def first_tiles(unit):
                for tile in range(AHEAD):
                    read_scores(unit, tile)
                if not REST:
                    invert(unit, 0)

            def output(unit):
                dve.wait_ge(values_summed, unit + 1)
                dve.wait_ge(out_stored, 16 * unit)
                if rel:
                    dve.wait_ge(unit_done, unit + 1)
                    for head in range(HEADS_PER_CHUNK):
                        for lane in range(2, 4):
                            nc.vector.tensor_copy(*relative_out(head, lane)).then_inc(rel_out_dve, 1)
                    dve.wait_ge(rel_out_act, 8 * (unit + 1))
                    dve.wait_ge(rel_out_dve, 8 * (unit + 1))
                    nc.vector.tensor_tensor(out[:, :, :], ps_out[:, :, :], rel_out[:, :, :],
                                            ALU.add).then_inc(out_ready, 1)
                else:
                    nc.vector.tensor_copy(out[:, :, :], ps_out[:, :, :]).then_inc(out_ready, 1)

            def unit_program(unit, has_next):
                for tile in range(AHEAD, TILES + LAG):
                    if tile < TILES:
                        read_scores(unit, tile)
                    if tile < TILES + REST + 1:
                        invert(unit, tile - REST - 1)
                    if tile >= LAG:
                        copy_turned(unit, tile - LAG)
                    if rel and has_next and tile == TILES - LEAD + AHEAD + 2:
                        stack_queries(unit + 1)
                if rel and has_next:
                    first_tiles(unit + 1)
                output(unit)
                if not rel and has_next:
                    first_tiles(unit + 1)

            if rel:
                width = 2 * SEQ - 1
                split(dve, nc.vector, 0, width, is_first=True)
                stack(0, rel_k_stacks, width, ((0, 0, 1, high), (0, 1, 2, middle), (0, 2, 3, high), (0, 3, 4, middle),
                                               (1, 0, 1, low_part), (1, 1, 2, high)))
                split(dve, nc.vector, 1, TILES * P)
                stack_queries(0)
            first_tiles(0)
            with dve.Fori(0, units - 1) as unit:
                unit_program(unit, True)
            unit_program(units - 1, False)


def finish(nc, stage, a_t, w, bias, residual, out, out_t):
    turns = residual.shape[0] // 2
    tiles = TOK_TILES
    with ExitStack() as ctx:
        mem = Memory(nc, ctx, f"{stage}_finish")
        ident = mem.sbuf("ident", [P, P])
        weights = mem.sbuf("weights", [P, CHUNKS, D_MODEL])
        bias_all = mem.sbuf("bias_all", [P, D_MODEL])
        eps = mem.sbuf("eps", [P, 1])
        src = [mem.sbuf(f"src{n}", [P, CHUNKS, SEQ]) for n in range(2)]
        res = [mem.sbuf(f"res{n}", [P, tiles, D_MODEL]) for n in range(2)]
        stats = [mem.sbuf(f"stats{n}", [P, tiles, 6]) for n in range(2)]
        moments = [mem.sbuf(f"moments{n}", [P, tiles, 2]) for n in range(2)]
        deviation = [mem.sbuf(f"deviation{n}", [P, tiles]) for n in range(2)]
        factor = [mem.sbuf(f"factor{n}", [P, tiles]) for n in range(2)]
        turned_out = [mem.sbuf(f"turned_out{n}", [P, CHUNKS, SEQ]) for n in range(2)]
        ps = mem.psum("ps", [P, tiles, D_MODEL])
        ps_turned = mem.psum("ps_turned", [P, 2, D_MODEL])
        weights_in = mem.sem("weights_in")
        src_in = [mem.sem(f"src_in{n}") for n in range(2)]
        res_in = [mem.sem(f"res_in{n}") for n in range(2)]
        ident_zeroed = mem.sem("ident_zeroed")
        ident_ready = mem.sem("ident_ready")
        biased = mem.sem("biased")
        product = mem.sem("product")
        summed = mem.sem("summed")
        stats_ready = mem.sem("stats_ready")
        moments_ready = mem.sem("moments_ready")
        deviation_ready = mem.sem("deviation_ready")
        factor_ready = mem.sem("factor_ready")
        normalised = mem.sem("normalised")
        turned = mem.sem("turned")
        turned_copied = mem.sem("turned_copied")
        stored = [mem.sem(f"stored{n}") for n in range(2)]
        turned_stored = [mem.sem(f"turned_stored{n}") for n in range(2)]
        alone = mem.sem("alone")
        block = ctx.enter_context(nc.Block())

        @block.sync
        def _(sp):
            sp.dma_start(weights[:, :, :], w.rearrange("(r p) n -> p r n", p=P)).then_inc(weights_in, 16)
            sp.dma_start(bias_all[:, :], by_partition(bias, 0, [[0, P], [1, D_MODEL]])).then_inc(weights_in, 16)

            def load_source(turn, half):
                sp.wait_ge(product, tiles * (2 * turn + half + 1))
                stand(sp, alone)
                sp.dma_start(src[half][:, :, :],
                             by_partition(a_t, (2 * turn + half) * (SEQ * D_MODEL),
                                          [[SEQ, P], [P * SEQ, CHUNKS], [1, SEQ]])).then_inc(src_in[half], 16)

            def load_residual(turn, half):
                sp.wait_ge(stored[half], 16 * turn)
                stand(sp, alone)
                sp.wait_ge(turned, tiles * (2 * turn + half + 1))
                stand(sp, alone)
                sp.dma_start(res[half][:, :, :],
                             by_partition(residual, (2 * turn + half) * (SEQ * D_MODEL),
                                          [[D_MODEL, P], [P * D_MODEL, tiles], [1, D_MODEL]])
                             ).then_inc(res_in[half], 16)

            load_source(0, 0)
            with sp.Fori(0, turns - 1) as turn:
                for half in range(2):
                    load_source(turn + half, 1 - half)
                    load_residual(turn, half)
            load_source(turns - 1, 1)
            load_residual(turns - 1, 0)
            load_residual(turns - 1, 1)

        @block.gpsimd
        def _(pool):
            identity_matrix(pool, nc, ident, ident_zeroed, ident_ready)
            pool.wait_ge(weights_in, 32)
            with pool.Fori(0, turns) as turn:
                for half in range(2):
                    pool.wait_ge(res_in[half], 16 * (turn + 1))
                    for tile in range(tiles):
                        nc.gpsimd.tensor_tensor(res[half][:, tile, :], res[half][:, tile, :], bias_all[:, :],
                                                ALU.add).then_inc(biased, 1)

        @block.tensor
        def _(pe):
            pe.wait_ge(weights_in, 32)
            pe.wait_ge(ident_ready, 1)
            def multiply(turn, half):
                pe.wait_ge(src_in[half], 16 * (turn + 1))
                for tile in range(tiles):
                    pe.wait_ge(summed, tiles * (2 * turn + half) + tile + 1)
                    for r in range(CHUNKS):
                        last = nc.tensor.matmul(ps[:, tile, :], src[half][:, r, tile * P:(tile + 1) * P],
                                                weights[:, r, :], start=(r == 0), stop=(r == CHUNKS - 1))
                    last.then_inc(product, 1)

            def transpose(turn, half):
                for tile in range(tiles):
                    number = tiles * (2 * turn + half) + tile
                    pe.wait_ge(normalised, number + 1)
                    pe.wait_ge(turned_copied, number + 1)
                    for chunk in range(CHUNKS):
                        last = nc.tensor.transpose(ps_turned[:, tile % 2, chunk * P:(chunk + 1) * P],
                                                   res[half][:, tile, chunk * P:(chunk + 1) * P], ident[:, :])
                    last.then_inc(turned, 1)

            multiply(0, 0)
            with pe.Fori(0, turns - 1) as turn:
                for half in range(2):
                    multiply(turn + half, 1 - half)
                    transpose(turn, half)
            multiply(turns - 1, 1)
            transpose(turns - 1, 0)
            transpose(turns - 1, 1)

        @block.scalar
        def _(act):
            act.wait_ge(summed, tiles)
            def deviate(turn, half):
                act.wait_ge(moments_ready, tiles * (2 * turn + half + 1))
                nc.scalar.activation(deviation[half][:, :], moments[half][:, :, 1], ACT.Sqrt,
                                     bias=eps[:, :]).then_inc(deviation_ready, 1)

            def store(turn, half):
                batch = 2 * turn + half
                act.wait_ge(normalised, tiles * (batch + 1))
                stand(act, alone)
                act.dma_start(by_partition(out, batch * (SEQ * D_MODEL),
                                           [[D_MODEL, P], [P * D_MODEL, tiles], [1, D_MODEL]]),
                              res[half][:, :, :]).then_inc(stored[half], 16)
                act.wait_ge(turned_stored[half], 16 * turn)
                for tile in range(tiles):
                    act.wait_ge(turned, tiles * (batch + 2) + tile + 1)
                    nc.scalar.activation(
                        turned_out[half][:, :, tile * P:(tile + 1) * P],
                        ps_turned[:, tile % 2, :].rearrange("p (c t) -> p c t", c=CHUNKS),
                        ACT.Copy).then_inc(turned_copied, 1)
                act.wait_ge(turned_copied, tiles * (batch + 1) + 2)
                stand(act, alone)
                act.dma_start(by_partition(out_t, batch * (SEQ * D_MODEL), [[SEQ, P], [P * SEQ, CHUNKS], [1, SEQ]]),
                              turned_out[half][:, :, :]).then_inc(turned_stored[half], 16)

            deviate(0, 0)
            with act.Fori(0, turns - 1) as turn:
                for half in range(2):
                    deviate(turn + half, 1 - half)
                    store(turn, half)
            deviate(turns - 1, 1)
            store(turns - 1, 0)
            store(turns - 1, 1)
            for half in range(2):
                act.wait_ge(stored[half], 16 * turns)
                act.wait_ge(turned_stored[half], 16 * turns)

        @block.vector
        def _(dve):
            nc.vector.memset(eps[:, :], LN_EPS).then_inc(summed, tiles)
            dve.sem_inc(turned_copied, 2)
            dve.sem_inc(turned, 2 * tiles)
            dve.sem_inc(product, 2 * tiles)
            with dve.Fori(0, turns) as turn:
                for half in range(2):
                    batch = 2 * turn + half
                    for tile in range(tiles):
                        number = tiles * batch + tile
                        dve.wait_ge(product, number + 2 * tiles + 1)
                        dve.wait_ge(biased, number + 1)
                        nc.vector.tensor_tensor(res[half][:, tile, :], ps[:, tile, :], res[half][:, tile, :],
                                                ALU.add).then_inc(summed, 1)
                        dve.wait_ge(summed, number + 1 + tiles)
                        nc.vector.bn_stats(stats[half][:, tile, :], res[half][:, tile, :]).then_inc(stats_ready, 1)
                        dve.wait_ge(stats_ready, number + 1)
                        stand(dve, alone)
                        nc.vector.bn_aggr(moments[half][:, tile, :], stats[half][:, tile, :]).then_inc(moments_ready, 1)
                    dve.wait_ge(deviation_ready, batch + 1)
                    nc.vector.reciprocal(factor[half][:, :], deviation[half][:, :]).then_inc(factor_ready, 1)
                    dve.wait_ge(factor_ready, batch + 1)
                    for tile in range(tiles):
                        nc.vector.tensor_scalar(res[half][:, tile, :], res[half][:, tile, :],
                                                moments[half][:, tile, 0:1], factor[half][:, tile:tile + 1],
                                                ALU.subtract, ALU.mult).then_inc(normalised, 1)


EXPERTS, SUB, HIDDEN = 16, 64, 256
PARTS = D_MODEL // SUB
GROUP_BATCHES = BATCH // 2
TOKEN_TILES = GROUP_BATCHES * TOK_TILES
COLUMNS = TOKEN_TILES * PARTS
ROWS_AT_ONCE = 512
BLOCKS = (2 * COLUMNS * P + EXPERTS * (ROWS_AT_ONCE - 1)) // ROWS_AT_ONCE + 1


class Routing:

    def __init__(self, mem, group):
        self.group = group
        self.weight = [mem.sbuf(f"weight{group}{n}", [P, COLUMNS]) for n in range(2)]
        self.place = [mem.sbuf(f"place{group}{n}", [P, COLUMNS], I32) for n in range(2)]
        self.block_expert = mem.sbuf(f"block_expert{group}", [P, BLOCKS], I32)


def route(nc, x_t, w_m, b_m, expert_emb, rows_in, hidden, routing):
    weight, place, block_expert = routing.weight, routing.place, routing.block_expert
    per_batch = TOK_TILES * PARTS
    turns = GROUP_BATCHES // 2
    zero_len = 2048
    with ExitStack() as ctx:
        mem = Memory(nc, ctx, f"route{routing.group}")
        ident = mem.sbuf("ident", [P, P])
        weights = mem.sbuf("weights", [P, CHUNKS, D_MODEL])
        bias_all = mem.sbuf("bias_all", [P, D_MODEL])
        emb = mem.sbuf("emb", [P, 2, EXPERTS])
        zeros = mem.sbuf("zeros", [P, zero_len])
        src = [mem.sbuf(f"src{n}", [P, CHUNKS, SEQ]) for n in range(2)]
        hid = [mem.sbuf(f"hid{n}", [P, TOK_TILES, D_MODEL]) for n in range(2)]
        hid_t = [mem.sbuf(f"hid_t{n}", [P, CHUNKS, P]) for n in range(2)]
        steps_int = mem.sbuf("steps_int", [P, BLOCKS], I32)
        steps = mem.sbuf("steps", [P, BLOCKS])
        limits = mem.sbuf("limits", [P, COLUMNS // 4])
        countdown = mem.sbuf("countdown", [P, EXPERTS])
        best = mem.sbuf("best", [P, per_batch])
        second = mem.sbuf("second", [P, per_batch])
        picked = mem.sbuf("picked", [P, per_batch])
        gap = mem.sbuf("gap", [P, per_batch])
        gap_exp = mem.sbuf("gap_exp", [P, per_batch])
        exp_sum = mem.sbuf("exp_sum", [P, per_batch])
        inverse = mem.sbuf("inverse", [P, per_batch])
        work = mem.sbuf("work", [P, per_batch, EXPERTS])
        logits = mem.sbuf("logits", [P, per_batch, EXPERTS])
        exps = mem.sbuf("exps", [P, per_batch, EXPERTS])
        chosen = [mem.sbuf(f"chosen{n}", [P, COLUMNS, EXPERTS], BF16) for n in range(2)]
        mask = mem.sbuf("mask", [P, COLUMNS, EXPERTS], BF16)
        before = mem.sbuf("before", [P, P], BF16)
        ones = mem.sbuf("ones", [P, P], BF16)
        rank = mem.sbuf("rank", [P, COLUMNS, EXPERTS])
        counts = mem.sbuf("counts", [P, EXPERTS, COLUMNS])
        until = mem.sbuf("until", [P, EXPERTS, COLUMNS])
        carry = mem.sbuf("carry", [P, EXPERTS, COLUMNS])
        over = mem.sbuf("over", [P, EXPERTS * BLOCKS])
        blocks = mem.sbuf("blocks", [P, EXPERTS])
        blocks_until = mem.sbuf("blocks_until", [P, EXPERTS])
        first_row = mem.sbuf("first_row", [P, EXPERTS])
        place_float = mem.sbuf("place_float", [P, COLUMNS])
        expert_float = mem.sbuf("expert_float", [P, BLOCKS])
        ps = mem.psum("ps", [P, TOK_TILES, D_MODEL])
        ps_turned = mem.psum("ps_turned", [P, 2, D_MODEL])
        ps_logits = mem.psum("ps_logits", [P, per_batch, EXPERTS])
        weights_in = mem.sem("weights_in")
        emb_zeroed = mem.sem("emb_zeroed")
        emb_in = mem.sem("emb_in")
        zeroed = mem.sem("zeroed")
        rows_zeroed = mem.sem("rows_zeroed")
        src_in = [mem.sem(f"src_in{n}") for n in range(2)]
        ident_zeroed = mem.sem("ident_zeroed")
        ident_ready = mem.sem("ident_ready")
        masks_ready = mem.sem("masks_ready")
        product = mem.sem("product")
        summed = mem.sem("summed")
        stored = [mem.sem(f"stored{n}") for n in range(2)]
        turned = mem.sem("turned")
        turned_copied = mem.sem("turned_copied")
        scored = mem.sem("scored")
        logits_read = mem.sem("logits_read")
        chain = mem.sem("chain")
        shifted = mem.sem("shifted")
        exps_ready = mem.sem("exps_ready")
        gap_ready = mem.sem("gap_ready")
        gap_exp_ready = mem.sem("gap_exp_ready")
        mask_ready = mem.sem("mask_ready")
        counted = mem.sem("counted")
        rank_copied = mem.sem("rank_copied")
        counts_copied = mem.sem("counts_copied")
        block = ctx.enter_context(nc.Block())

        @block.sync
        def _(sp):
            sp.dma_start(weights[:, :, :], w_m.rearrange("(r p) n -> p r n", p=P)).then_inc(weights_in, 16)
            sp.dma_start(bias_all[:, :], by_partition(b_m, 0, [[0, P], [1, D_MODEL]])).then_inc(weights_in, 16)
            sp.wait_ge(emb_zeroed, 1)
            for part in range(2):
                sp.dma_start(emb[SUB * part:SUB * (part + 1), part, :], expert_emb).then_inc(emb_in, 16)
            with sp.Fori(0, turns) as turn:
                for half in range(2):
                    sp.wait_ge(product, TOK_TILES * (2 * turn + half + 1))
                    sp.dma_start(src[half][:, :, :],
                                 x_t[2 * turn + half].rearrange("(r p) t -> p r t", p=P)).then_inc(src_in[half], 16)
            sp.wait_ge(zeroed, 1)
            repeats = BLOCKS * ROWS_AT_ONCE * SUB // P // zero_len
            sp.dma_start(by_partition(rows_in, 0, [[repeats * zero_len, P], [zero_len, repeats], [1, zero_len]]),
                         zeros[:, :].unsqueeze(1).to_broadcast([P, repeats, zero_len])).then_inc(rows_zeroed, 16)
            sp.wait_ge(rows_zeroed, 16)

        @block.gpsimd
        def _(pool):
            nc.gpsimd.memset(emb[:, :, :], 0.0).then_inc(emb_zeroed, 1)
            nc.gpsimd.memset(zeros[:, :], 0.0).then_inc(zeroed, 1)
            identity_matrix(pool, nc, ident, ident_zeroed, ident_ready)
            nc.gpsimd.memset(before[:, :], 0.0).then_inc(masks_ready, 1)
            nc.gpsimd.memset(ones[:, :], 1.0).then_inc(masks_ready, 1)
            nc.gpsimd.iota(steps_int[:, :], pattern=[[1, BLOCKS]], base=0, channel_multiplier=0).then_inc(masks_ready, 1)
            pool.wait_ge(masks_ready, 3)
            nc.gpsimd.affine_select(out=before[:, :], in_=before[:, :], compare_op=ALU.is_ge, fill=1.0, base=0,
                                    pattern=[[-1, P]], channel_multiplier=1).then_inc(masks_ready, 1)

        @block.tensor
        def _(pe):
            def hidden_product(batch, half, tile):
                pe.wait_ge(summed, TOK_TILES * batch + tile + 1)
                for r in range(CHUNKS):
                    last = nc.tensor.matmul(ps[:, tile, :], src[half][:, r, tile * P:(tile + 1) * P],
                                            weights[:, r, :], start=(r == 0), stop=(r == CHUNKS - 1))
                last.then_inc(product, 1)

            def transpose(batch, half, tile):
                pe.wait_ge(summed, TOK_TILES * (batch + 1) + tile + 1)
                pe.wait_ge(turned_copied, TOK_TILES * batch + tile + 1)
                for chunk in range(CHUNKS):
                    last = nc.tensor.transpose(ps_turned[:, tile % 2, chunk * P:(chunk + 1) * P],
                                               hid[half][:, tile, chunk * P:(chunk + 1) * P], ident[:, :])
                last.then_inc(turned, 1)

            def logits_product(batch, tile):
                if tile == 0:
                    pe.wait_ge(logits_read, batch)
                pe.wait_ge(turned_copied, TOK_TILES * batch + tile + 3)
                for chunk in range(CHUNKS):
                    first = tile * PARTS + 2 * chunk
                    last = nc.tensor.matmul(ps_logits[:, first:first + 2, :], hid_t[tile % 2][:, chunk, :],
                                            emb[:, :, :], start=True, stop=True)
                last.then_inc(scored, 1)

            pe.wait_ge(weights_in, 32)
            pe.wait_ge(ident_ready, 1)
            pe.wait_ge(emb_in, 32)
            def products(turn, half):
                pe.wait_ge(src_in[half], 16 * (turn + 1))
                for tile in range(TOK_TILES):
                    hidden_product(2 * turn + half, half, tile)

            def logits_of(turn, half):
                for tile in range(TOK_TILES + 1):
                    if tile < TOK_TILES:
                        transpose(2 * turn + half, half, tile)
                    if tile > 0:
                        logits_product(2 * turn + half, tile - 1)

            products(0, 0)
            with pe.Fori(0, turns - 1) as turn:
                for half in range(2):
                    products(turn + half, 1 - half)
                    logits_of(turn, half)
            products(turns - 1, 1)
            logits_of(turns - 1, 0)
            logits_of(turns - 1, 1)
            pe.wait_ge(masks_ready, 4)
            pe.wait_ge(mask_ready, GROUP_BATCHES)
            with pe.Fori(0, GROUP_BATCHES) as batch:
                pe.wait_ge(rank_copied, batch)
                pe.wait_ge(counts_copied, batch)
                chose = mask[:, bass.ds(per_batch * batch, per_batch), :].rearrange("p c e -> p (c e)")
                nc.tensor.matmul(ps_turned[:, 0, :], before[:, :], chose, start=True, stop=True)
                nc.tensor.matmul(ps_turned[:, 1, :], ones[:, :], chose, start=True, stop=True).then_inc(counted, 1)

        @block.scalar
        def _(act):
            with act.Fori(0, turns) as turn:
                for half in range(2):
                    batch = 2 * turn + half
                    for tile in range(TOK_TILES):
                        act.wait_ge(turned, TOK_TILES * batch + tile + 1)
                        act.wait_ge(scored, TOK_TILES * batch + tile + 1)
                        nc.scalar.activation(hid_t[tile % 2][:, :, :].rearrange("p c t -> p (c t)"),
                                             ps_turned[:, tile % 2, :], ACT.Copy).then_inc(turned_copied, 1)
                    act.wait_ge(summed, TOK_TILES * (batch + 2))
                    act.dma_start(hidden[batch].rearrange("(t p) n -> p t n", p=P),
                                  hid[half][:, :, :]).then_inc(stored[half], 16)
                    act.wait_ge(shifted, batch + 1)
                    nc.scalar.activation(exps[:, :, :], work[:, :, :], ACT.Exp).then_inc(exps_ready, 1)
                    act.wait_ge(gap_ready, batch + 1)
                    nc.scalar.activation(gap_exp[:, :], gap[:, :], ACT.Exp).then_inc(gap_exp_ready, 1)
            with act.Fori(0, GROUP_BATCHES) as batch:
                act.wait_ge(counted, batch + 1)
                nc.scalar.activation(rank[:, bass.ds(per_batch * batch, per_batch), :].rearrange("p c e -> p (c e)"),
                                     ps_turned[:, 0, :], ACT.Copy).then_inc(rank_copied, 1)
            for half in range(2):
                act.wait_ge(stored[half], 16 * turns)

        @block.vector
        def _(dve):
            setup_steps, batch_steps = 4, 13

            def over_experts(ap, count):
                return ap.unsqueeze(2).to_broadcast([P, count, EXPERTS])

            def over_columns(ap, count):
                return ap.unsqueeze(1).to_broadcast([P, count, EXPERTS])

            def choose(values, top, batch, out, number):
                nc.vector.tensor_tensor(work[:, :, :], values, over_experts(top, per_batch),
                                        ALU.is_equal).then_inc(chain, 1)
                dve.wait_ge(chain, number + 1)
                nc.vector.tensor_tensor(work[:, :, :], work[:, :, :], over_columns(countdown[:, :], per_batch),
                                        ALU.mult).then_inc(chain, 1)
                dve.wait_ge(chain, number + 2)
                nc.vector.tensor_reduce(picked[:, :], work[:, :, :], AX_X, ALU.max).then_inc(chain, 1)
                dve.wait_ge(chain, number + 3)
                nc.vector.tensor_tensor(out[:, bass.ds(per_batch * batch, per_batch), :],
                                        over_columns(countdown[:, :], per_batch),
                                        over_experts(picked[:, :], per_batch), ALU.is_equal).then_inc(chain, 1)
                dve.wait_ge(chain, number + 4)

            dve.sem_inc(turned_copied, 2)
            dve.sem_inc(scored, 2)
            dve.sem_inc(summed, TOK_TILES)
            dve.sem_inc(product, 2 * TOK_TILES)
            dve.wait_ge(masks_ready, 3)
            nc.vector.tensor_copy(steps[:, :], steps_int[:, :]).then_inc(chain, 1)
            nc.vector.memset(carry[:, :, :], 1.0).then_inc(chain, 1)
            dve.wait_ge(chain, 2)
            nc.vector.tensor_scalar(countdown[:, :], steps[:, 0:EXPERTS], -1.0, float(EXPERTS),
                                    ALU.mult, ALU.add).then_inc(chain, 1)
            nc.vector.memset(carry[:, :, 0:1], 0.0).then_inc(chain, 1)
            dve.wait_ge(chain, setup_steps)
            dve.wait_ge(weights_in, 32)

            def add_bias(turn, half):
                dve.wait_ge(stored[half], 16 * turn)
                for tile in range(TOK_TILES):
                    dve.wait_ge(product, TOK_TILES * (2 * turn + half + 2) + tile + 1)
                    nc.vector.tensor_tensor(hid[half][:, tile, :], ps[:, tile, :], bias_all[:, :],
                                            ALU.add).then_inc(summed, 1)

            def choose_experts(batch):
                number = setup_steps + batch_steps * batch
                dve.wait_ge(scored, TOK_TILES * (batch + 1) + 2)
                nc.vector.tensor_copy(logits[:, :, :], ps_logits[:, :, :]).then_inc(logits_read, 1)
                dve.wait_ge(logits_read, batch + 1)
                nc.vector.tensor_reduce(best[:, :], logits[:, :, :], AX_X, ALU.max).then_inc(chain, 1)
                dve.wait_ge(chain, number + 1)
                nc.vector.tensor_tensor(work[:, :, :], logits[:, :, :], over_experts(best[:, :], per_batch),
                                        ALU.subtract).then_inc(shifted, 1)
                dve.wait_ge(exps_ready, batch + 1)
                choose(logits[:, :, :], best[:, :], batch, chosen[0], number + 1)
                nc.vector.scalar_tensor_tensor(
                    logits[:, :, :], chosen[0][:, bass.ds(per_batch * batch, per_batch), :], -BIG,
                    logits[:, :, :], ALU.mult, ALU.add).then_inc(chain, 1)
                dve.wait_ge(chain, number + 6)
                nc.vector.tensor_reduce(second[:, :], logits[:, :, :], AX_X, ALU.max).then_inc(chain, 1)
                dve.wait_ge(chain, number + 7)
                nc.vector.tensor_tensor(gap[:, :], second[:, :], best[:, :], ALU.subtract).then_inc(gap_ready, 1)
                choose(logits[:, :, :], second[:, :], batch, chosen[1], number + 7)
                nc.vector.tensor_tensor(mask[:, bass.ds(per_batch * batch, per_batch), :],
                                        chosen[0][:, bass.ds(per_batch * batch, per_batch), :],
                                        chosen[1][:, bass.ds(per_batch * batch, per_batch), :],
                                        ALU.add).then_inc(mask_ready, 1)
                nc.vector.tensor_reduce(exp_sum[:, :], exps[:, :, :], AX_X, ALU.add).then_inc(chain, 1)
                dve.wait_ge(chain, number + 12)
                nc.vector.reciprocal(weight[0][:, bass.ds(per_batch * batch, per_batch)],
                                     exp_sum[:, :]).then_inc(chain, 1)
                dve.wait_ge(chain, number + 13)
                dve.wait_ge(gap_exp_ready, batch + 1)
                nc.vector.tensor_tensor(weight[1][:, bass.ds(per_batch * batch, per_batch)], gap_exp[:, :],
                                        weight[0][:, bass.ds(per_batch * batch, per_batch)], ALU.mult)

            add_bias(0, 0)
            with dve.Fori(0, turns - 1) as turn:
                for half in range(2):
                    add_bias(turn + half, 1 - half)
                    choose_experts(2 * turn + half)
            add_bias(turns - 1, 1)
            choose_experts(2 * turns - 2)
            choose_experts(2 * turns - 1)
            with dve.Fori(0, GROUP_BATCHES) as batch:
                dve.wait_ge(counted, batch + 1)
                nc.vector.tensor_copy(counts[:, :, bass.ds(per_batch * batch, per_batch)],
                                      ps_turned[:, 1, :].rearrange("p (c e) -> p e c", e=EXPERTS)
                                      ).then_inc(counts_copied, 1)
            dve.wait_ge(counts_copied, GROUP_BATCHES)

            done = [setup_steps + batch_steps * GROUP_BATCHES]

            def then(instruction):
                done[0] += 1
                instruction.then_inc(chain, 1)
                dve.wait_ge(chain, done[0])

            flat = "p e c -> p (e c)"
            then(nc.vector.tensor_tensor_scan(until[:, :, :].rearrange(flat), carry[:, :, :].rearrange(flat),
                                              counts[:, :, :].rearrange(flat), 0.0, ALU.mult, ALU.add))
            then(nc.vector.tensor_tensor(counts[:, :, :].rearrange(flat), until[:, :, :].rearrange(flat),
                                         counts[:, :, :].rearrange(flat), ALU.subtract))
            most = COLUMNS // 4
            then(nc.vector.tensor_scalar(limits[:, :], steps[:, 0:most], float(ROWS_AT_ONCE), None, ALU.mult))
            is_over = over[:, 0:EXPERTS * most].rearrange("p (e k) -> p e k", e=EXPERTS)
            then(nc.vector.tensor_tensor(is_over, until[:, :, COLUMNS - 1:COLUMNS].to_broadcast([P, EXPERTS, most]),
                                         limits[:, :].unsqueeze(1).to_broadcast([P, EXPERTS, most]), ALU.is_gt))
            then(nc.vector.tensor_reduce(blocks[:, :], is_over, AX_X, ALU.add))
            then(nc.vector.tensor_tensor_scan(blocks_until[:, :], carry[:, 0, 1:EXPERTS + 1], blocks[:, :], 0.0,
                                              ALU.mult, ALU.add))
            then(nc.vector.tensor_tensor(first_row[:, :], blocks_until[:, :], blocks[:, :], ALU.subtract))
            then(nc.vector.tensor_scalar(first_row[:, :], first_row[:, :], float(ROWS_AT_ONCE), None, ALU.mult))
            then(nc.vector.tensor_tensor(counts[:, :, :], counts[:, :, :],
                                         first_row[:, :].unsqueeze(2).to_broadcast([P, EXPERTS, COLUMNS]), ALU.add))
            dve.wait_ge(rank_copied, GROUP_BATCHES)
            then(nc.vector.tensor_tensor(rank[:, :, :], rank[:, :, :], counts[:, :, :].rearrange("p e c -> p c e"),
                                         ALU.add))
            by_column = until[:, :, :].rearrange(flat).rearrange("p (c e) -> p c e", e=EXPERTS)
            for n in range(2):
                then(nc.vector.tensor_tensor(by_column, rank[:, :, :], chosen[n][:, :, :], ALU.mult))
                then(nc.vector.tensor_reduce(place_float[:, :], by_column, AX_X, ALU.add))
                then(nc.vector.tensor_copy(place[n][:, :], place_float[:, :]))
            is_past = over[:, :].rearrange("p (b e) -> p b e", e=EXPERTS)
            then(nc.vector.tensor_tensor(is_past, steps[:, :].unsqueeze(2).to_broadcast([P, BLOCKS, EXPERTS]),
                                         blocks_until[:, :].unsqueeze(1).to_broadcast([P, BLOCKS, EXPERTS]),
                                         ALU.is_ge))
            then(nc.vector.tensor_reduce(expert_float[:, :], is_past, AX_X, ALU.add))
            then(nc.vector.tensor_scalar(expert_float[:, :], expert_float[:, :], float(EXPERTS - 1), None, ALU.min))
            then(nc.vector.tensor_copy(block_expert[:, :], expert_float[:, :]))


def dispatch(nc, mem, hidden, routing, rows_in):
    turns = TOKEN_TILES // 2
    per_tile = 16 * 2 * PARTS
    tokens = [mem.sbuf(f"tokens{n}", [P, D_MODEL]) for n in range(2)]
    places = [mem.sbuf(f"places{n}", [P, 2, PARTS], I32) for n in range(2)]
    tokens_in = [mem.sem(f"tokens_in{n}") for n in range(2)]
    places_in = mem.sem("places_in")
    sent = [mem.sem(f"sent{n}") for n in range(2)]
    alone = mem.sem("alone")

    def program(pool):
        def prepare(turn, half):
            pool.wait_ge(sent[half], per_tile * turn)
            pool.dma_start(tokens[half][:, :],
                           by_partition(hidden, (2 * turn + half) * (P * D_MODEL), [[D_MODEL, P], [1, D_MODEL]])
                           ).then_inc(tokens_in[half], 16)
            for n in range(2):
                nc.gpsimd.tensor_copy(places[half][:, n, :],
                                      routing.place[n][:, bass.ds(PARTS * (2 * turn + half), PARTS)]
                                      ).then_inc(places_in, 1)

        def send(turn, half, has_next):
            pool.wait_ge(tokens_in[half], 16 * (turn + 1))
            pool.wait_ge(places_in, 2 * (2 * turn + half + 1))
            stand(pool, alone)
            for n in range(2):
                for part in range(PARTS):
                    pool.indirect_dma_start(
                        out=rows_in, out_offset=bass.IndirectOffsetOnAxis(ap=places[half][:, n, part:part + 1], axis=0),
                        in_=tokens[half][:, part * SUB:(part + 1) * SUB], in_offset=None).then_inc(sent[half], 16)
                if n == 0 and has_next:
                    prepare(turn + half, 1 - half)

        prepare(0, 0)
        with pool.Fori(0, turns - 1) as turn:
            send(turn, 0, True)
            send(turn, 1, True)
        send(turns - 1, 0, True)
        send(turns - 1, 1, False)
        for half in range(2):
            pool.wait_ge(sent[half], per_tile * turns)

    return program


def gather(nc, mem, rows_out, routing, gathered):
    turns = TOKEN_TILES // 2
    per_tile = 16 * 2 * PARTS
    rows = [mem.sbuf(f"rows{n}", [P, 2, D_MODEL]) for n in range(2)]
    places = [mem.sbuf(f"places{n}", [P, 2, PARTS], I32) for n in range(2)]
    places_in = mem.sem("places_in")
    fetched = [mem.sem(f"fetched{n}") for n in range(2)]
    landed = [mem.sem(f"landed{n}") for n in range(2)]
    alone = mem.sem("alone")

    def program(pool):
        def prepare(turn, half):
            for n in range(2):
                nc.gpsimd.tensor_copy(places[half][:, n, :],
                                      routing.place[n][:, bass.ds(PARTS * (2 * turn + half), PARTS)]
                                      ).then_inc(places_in, 1)

        def fetch(turn, half, is_first=False, is_last=False):
            pool.wait_ge(places_in, 2 * (2 * turn + half + 1))
            pool.wait_ge(landed[half], 16 * turn)
            stand(pool, alone)
            for n in range(2):
                for part in range(PARTS):
                    pool.indirect_dma_start(
                        out=rows[half][:, n, part * SUB:(part + 1) * SUB], out_offset=None, in_=rows_out,
                        in_offset=bass.IndirectOffsetOnAxis(ap=places[half][:, n, part:part + 1], axis=0)
                    ).then_inc(fetched[half], 16)
                if n == 0 and not is_first:
                    store(turn + half - 1, 1 - half)
                    if not is_last:
                        prepare(turn + half, 1 - half)

        def store(turn, half):
            pool.wait_ge(fetched[half], per_tile * (turn + 1))
            stand(pool, alone)
            pool.dma_start(by_partition(gathered, (2 * turn + half) * (P * 2 * D_MODEL),
                                        [[2 * D_MODEL, P], [1, 2 * D_MODEL]]),
                           rows[half][:, :, :].rearrange("p n m -> p (n m)")).then_inc(landed[half], 16)

        for half in range(2):
            prepare(0, half)
        fetch(0, 0, is_first=True)
        fetch(0, 1)
        with pool.Fori(1, turns - 1) as turn:
            for half in range(2):
                fetch(turn, half)
        fetch(turns - 1, 0)
        fetch(turns - 1, 1, is_last=True)
        store(turns - 1, 1)
        for half in range(2):
            pool.wait_ge(landed[half], 16 * turns)

    return program, landed


def run_experts(nc, stage, w_1, b_1, w_2, b_2, block_expert, rows_in, rows_out, beside):
    assert BLOCKS % 4 == 0
    slots = 4
    turns = BLOCKS // slots
    quarters = ROWS_AT_ONCE // P
    parts = HIDDEN // P
    depth = 96
    with ExitStack() as ctx:
        mem = Memory(nc, ctx, f"{stage}_experts")
        ident = mem.sbuf("ident", [P, P])
        rows = [mem.sbuf(f"rows{n}", [P, quarters, SUB]) for n in range(slots)]
        first = [mem.sbuf(f"first{n}", [depth, HIDDEN]) for n in range(slots)]
        second = [mem.sbuf(f"second{n}", [P, parts, SUB]) for n in range(slots)]
        bias = [mem.sbuf(f"bias{n}", [P, SUB]) for n in range(slots)]
        rows_t = [mem.sbuf(f"rows_t{n}", [depth, ROWS_AT_ONCE]) for n in range(2)]
        middle = [mem.sbuf(f"middle{n}", [P, parts, ROWS_AT_ONCE]) for n in range(2)]
        result = [mem.sbuf(f"result{n}", [P, quarters, SUB]) for n in range(2)]
        ps_turned = mem.psum("ps_turned", [P, 2, ROWS_AT_ONCE])
        ps_middle = mem.psum("ps_middle", [P, 2 * parts, ROWS_AT_ONCE])
        ps_result = mem.psum("ps_result", [P, 2, 512])
        ident_zeroed = mem.sem("ident_zeroed")
        ident_ready = mem.sem("ident_ready")
        padded = mem.sem("padded")
        rows_arrived = [mem.sem(f"rows_arrived{n}") for n in range(slots)]
        first_in = [mem.sem(f"first_in{n}") for n in range(slots)]
        second_in = [mem.sem(f"second_in{n}") for n in range(slots)]
        turned = mem.sem("turned")
        turned_copied = mem.sem("turned_copied")
        multiplied = mem.sem("multiplied")
        activated = mem.sem("activated")
        produced = mem.sem("produced")
        biased = mem.sem("biased")
        stored = [mem.sem(f"stored{n}") for n in range(2)]
        alone = mem.sem("alone")
        block = ctx.enter_context(nc.Block())

        @block.sync
        def _(sp):
            for half in range(2):
                sp.sem_inc(stored[half], 16)
            sp.wait_ge(padded, 2 * slots)
            with sp.Fori(0, turns) as turn:
                for slot in range(slots):
                    number = slots * turn + slot
                    sp.wait_ge(turned, number + 1)
                    stand(sp, alone)
                    sp.dma_start(rows[slot][:, :, :],
                                 by_partition(rows_in, number * (ROWS_AT_ONCE * SUB),
                                              [[quarters * SUB, P], [SUB, quarters], [1, SUB]])
                                 ).then_inc(rows_arrived[slot], 16)
                    expert = sp.value_load(block_expert[0:1, bass.ds(number, 1)], min_val=0, max_val=EXPERTS - 1)
                    sp.wait_ge(multiplied, number + 1)
                    sp.dma_start(first[slot][0:SUB, :],
                                 by_partition(w_1, expert * (SUB * HIDDEN), [[HIDDEN, SUB], [1, HIDDEN]])
                                 ).then_inc(first_in[slot], 16)
                    sp.dma_start(first[slot][SUB:SUB + 1, :],
                                 by_partition(b_1, expert * HIDDEN, [[HIDDEN, 1], [1, HIDDEN]])
                                 ).then_inc(first_in[slot], 16)
                    sp.wait_ge(biased, number + 1)
                    sp.dma_start(second[slot][:, :, :],
                                 by_partition(w_2, expert * (HIDDEN * SUB), [[SUB, P], [P * SUB, parts], [1, SUB]])
                                 ).then_inc(second_in[slot], 16)
                    sp.dma_start(bias[slot][:, :],
                                 by_partition(b_2, expert * SUB, [[0, P], [1, SUB]])).then_inc(second_in[slot], 16)

        @block.gpsimd
        def _(pool):
            identity_matrix(pool, nc, ident, ident_zeroed, ident_ready)
            beside(pool)

        @block.tensor
        def _(pe):
            def transpose(turn, slot):
                half = slot % 2
                pe.wait_ge(rows_arrived[slot], 16 * (turn + 1))
                pe.wait_ge(turned_copied, slots * turn + slot + 1)
                stand(pe, alone)
                for quarter in range(quarters):
                    last = nc.tensor.transpose(ps_turned[0:SUB, half, quarter * P:(quarter + 1) * P],
                                               rows[slot][:, quarter, :], ident[:, :])
                last.then_inc(turned, 1)

            def first_product(turn, slot):
                number, half = slots * turn + slot, slot % 2
                pe.wait_ge(turned_copied, number + 3)
                pe.wait_ge(first_in[slot], 32 * (turn + 1))
                pe.wait_ge(activated, parts * (number + 1))
                for part in range(parts):
                    last = nc.tensor.matmul(ps_middle[:, parts * half + part, :],
                                            first[slot][:, part * P:(part + 1) * P], rows_t[half][:, :],
                                            start=True, stop=True)
                last.then_inc(multiplied, 1)

            def second_product(turn, slot):
                number, half = slots * turn + slot, slot % 2
                pe.wait_ge(activated, parts * (number + 3))
                pe.wait_ge(second_in[slot], 32 * (turn + 1))
                pe.wait_ge(biased, number + slots - 1)
                for quarter in range(quarters):
                    for part in range(parts):
                        last = nc.tensor.matmul(ps_result[:, half, quarter * SUB:(quarter + 1) * SUB],
                                                middle[half][:, part, quarter * P:(quarter + 1) * P],
                                                second[slot][:, part, :],
                                                start=(part == 0), stop=(part == parts - 1))
                last.then_inc(produced, 1)

            def turn_program(turn, has_next):
                for slot in range(slots):
                    if has_next or slot + 2 < slots:
                        transpose(turn + (slot + 2) // slots, (slot + 2) % slots)
                    if has_next or slot + 1 < slots:
                        first_product(turn + (slot + 1) // slots, (slot + 1) % slots)
                    second_product(turn, slot)

            pe.wait_ge(ident_ready, 1)
            transpose(0, 0)
            transpose(0, 1)
            first_product(0, 0)
            with pe.Fori(0, turns - 1) as turn:
                turn_program(turn, True)
            turn_program(turns - 1, False)

        @block.scalar
        def _(act):
            act.sem_inc(activated, 2 * parts)

            def activate(turn, slot):
                number, half = slots * turn + slot, slot % 2
                act.wait_ge(multiplied, number + slots + 1)
                act.wait_ge(produced, number + 1)
                for part in range(parts):
                    nc.scalar.activation(middle[half][:, part, :], ps_middle[:, parts * half + part, :],
                                         ACT.Gelu).then_inc(activated, 1)

            def store(turn, slot):
                number = slots * turn + slot
                act.wait_ge(biased, number + slots + 1)
                stand(act, alone)
                act.dma_start(by_partition(rows_out, number * (ROWS_AT_ONCE * SUB),
                                           [[quarters * SUB, P], [SUB, quarters], [1, SUB]]),
                              result[slot % 2][:, :, :]).then_inc(stored[slot % 2], 16)

            def turn_program(turn, has_next):
                for slot in range(slots):
                    if has_next or slot + 2 < slots:
                        activate(turn + (slot + 2) // slots, (slot + 2) % slots)
                    store(turn, slot)

            activate(0, 0)
            activate(0, 1)
            with act.Fori(0, turns - 1) as turn:
                turn_program(turn, True)
            turn_program(turns - 1, False)
            for half in range(2):
                act.wait_ge(stored[half], 16 * (BLOCKS // 2 + 1))

        @block.vector
        def _(dve):
            dve.sem_inc(turned, slots)
            dve.sem_inc(turned_copied, 2)
            dve.sem_inc(multiplied, slots)
            dve.sem_inc(produced, 2)
            dve.sem_inc(biased, slots)
            for n in range(slots):
                nc.vector.memset(first[n][SUB:depth, :], 0.0).then_inc(padded, 1)
            for n in range(2):
                nc.vector.memset(rows_t[n][SUB:depth, :], 1.0).then_inc(padded, slots // 2)
            dve.wait_ge(padded, 2 * slots)

            def copy_turned(turn, slot):
                number, half = slots * turn + slot, slot % 2
                dve.wait_ge(turned, number + slots + 1)
                dve.wait_ge(multiplied, number + slots - 1)
                nc.vector.tensor_copy(rows_t[half][0:SUB, :], ps_turned[0:SUB, half, :]).then_inc(turned_copied, 1)

            def add_bias(turn, slot):
                number, half = slots * turn + slot, slot % 2
                dve.wait_ge(produced, number + 3)
                dve.wait_ge(stored[half], 16 * (number // 2 + 1))
                nc.vector.tensor_tensor(
                    result[half][:, :, :],
                    ps_result[:, half, 0:quarters * SUB].rearrange("p (q n) -> p q n", q=quarters),
                    bias[slot][:, :].unsqueeze(1).to_broadcast([P, quarters, SUB]), ALU.add).then_inc(biased, 1)

            def turn_program(turn, has_next):
                for slot in range(slots):
                    if has_next or slot + 2 < slots:
                        copy_turned(turn + (slot + 2) // slots, (slot + 2) % slots)
                    add_bias(turn, slot)

            copy_turned(0, 0)
            copy_turned(0, 1)
            with dve.Fori(0, turns - 1) as turn:
                turn_program(turn, True)
            turn_program(turns - 1, False)


def finish_mixture(nc, gathered, weights_of, w, bias, residual, out, beside, landed):
    tiles = TOK_TILES
    with ExitStack() as ctx:
        mem = Memory(nc, ctx, "mixture")
        ident = mem.sbuf("ident", [P, P])
        weights = mem.sbuf("weights", [P, CHUNKS, D_MODEL])
        bias_all = mem.sbuf("bias_all", [P, D_MODEL])
        eps = mem.sbuf("eps", [P, 1])
        pair = [mem.sbuf(f"pair{n}", [P, tiles, 2, D_MODEL]) for n in range(2)]
        mixed = [mem.sbuf(f"mixed{n}", [P, tiles, D_MODEL]) for n in range(2)]
        mixed_t = [mem.sbuf(f"mixed_t{n}", [P, CHUNKS, P]) for n in range(2)]
        res = [mem.sbuf(f"res{n}", [P, tiles, D_MODEL]) for n in range(2)]
        stats = [mem.sbuf(f"stats{n}", [P, tiles, 6]) for n in range(2)]
        moments = [mem.sbuf(f"moments{n}", [P, tiles, 2]) for n in range(2)]
        deviation = [mem.sbuf(f"deviation{n}", [P, tiles]) for n in range(2)]
        factor = [mem.sbuf(f"factor{n}", [P, tiles]) for n in range(2)]
        ps = mem.psum("ps", [P, tiles, D_MODEL])
        ps_turned = mem.psum("ps_turned", [P, 2, D_MODEL])
        weights_in = mem.sem("weights_in")
        pair_in = [mem.sem(f"pair_in{n}") for n in range(2)]
        res_in = [mem.sem(f"res_in{n}") for n in range(2)]
        ident_zeroed = mem.sem("ident_zeroed")
        ident_ready = mem.sem("ident_ready")
        eps_ready = mem.sem("eps_ready")
        scaled_ready = mem.sem("scaled_ready")
        mixed_ready = mem.sem("mixed_ready")
        turned = mem.sem("turned")
        turned_copied = mem.sem("turned_copied")
        product = mem.sem("product")
        biased = mem.sem("biased")
        summed = mem.sem("summed")
        stats_ready = mem.sem("stats_ready")
        moments_ready = mem.sem("moments_ready")
        deviation_ready = mem.sem("deviation_ready")
        factor_ready = mem.sem("factor_ready")
        normalised = mem.sem("normalised")
        stored = [mem.sem(f"stored{n}") for n in range(2)]
        alone = mem.sem("alone")
        block = ctx.enter_context(nc.Block())
        turns = GROUP_BATCHES // 2
        groups = len(weights_of)
        all_turns = groups * turns

        @block.sync
        def _(sp):
            sp.dma_start(weights[:, :, :], w.rearrange("(r p) n -> p r n", p=P)).then_inc(weights_in, 16)
            sp.dma_start(bias_all[:, :], by_partition(bias, 0, [[0, P], [1, D_MODEL]])).then_inc(weights_in, 16)
            for group in range(groups):
                with sp.Fori(0, turns) as step:
                    turn = step + group * turns
                    for half in range(2):
                        sp.wait_ge(stored[half], 16 * turn)
                        stand(sp, alone)
                        sp.dma_start(res[half][:, :, :],
                                     by_partition(residual, (2 * turn + half) * (SEQ * D_MODEL),
                                                  [[D_MODEL, P], [P * D_MODEL, tiles], [1, D_MODEL]])
                                     ).then_inc(res_in[half], 16)
                        sp.wait_ge(mixed_ready, tiles * 2 * turn)
                        if group == groups - 1:
                            for parity in range(2):
                                sp.wait_ge(landed[parity], 16 * tiles // 2 * (2 * step + half + 1))
                        stand(sp, alone)
                        sp.dma_start(pair[half][:, :, :, :].rearrange("p t n m -> p t (n m)"),
                                     by_partition(gathered, (2 * turn + half) * (SEQ * 2 * D_MODEL),
                                                  [[2 * D_MODEL, P], [P * 2 * D_MODEL, tiles], [1, 2 * D_MODEL]])
                                     ).then_inc(pair_in[half], 16)

        @block.gpsimd
        def _(pool):
            identity_matrix(pool, nc, ident, ident_zeroed, ident_ready)
            beside(pool)

        @block.tensor
        def _(pe):
            def transpose(batch, half, tile):
                pe.wait_ge(mixed_ready, tiles * batch + tile + 1)
                pe.wait_ge(turned_copied, tiles * batch + tile + 1)
                for chunk in range(CHUNKS):
                    last = nc.tensor.transpose(ps_turned[:, tile % 2, chunk * P:(chunk + 1) * P],
                                               mixed[half][:, tile, chunk * P:(chunk + 1) * P], ident[:, :])
                last.then_inc(turned, 1)

            def multiply(batch, tile):
                pe.wait_ge(turned_copied, tiles * batch + tile + 3)
                pe.wait_ge(summed, tiles * batch + tile + 1)
                for r in range(CHUNKS):
                    last = nc.tensor.matmul(ps[:, tile, :], mixed_t[tile % 2][:, r, :], weights[:, r, :],
                                            start=(r == 0), stop=(r == CHUNKS - 1))
                last.then_inc(product, 1)

            pe.wait_ge(weights_in, 32)
            pe.wait_ge(ident_ready, 1)
            with pe.Fori(0, all_turns) as turn:
                for half in range(2):
                    for tile in range(tiles + 1):
                        if tile < tiles:
                            transpose(2 * turn + half, half, tile)
                        if tile > 0:
                            multiply(2 * turn + half, tile - 1)

        @block.scalar
        def _(act):
            act.wait_ge(eps_ready, 1)
            with act.Fori(0, all_turns) as turn:
                for half in range(2):
                    batch = 2 * turn + half
                    for tile in range(tiles):
                        act.wait_ge(turned, tiles * (batch + 1) + tile + 1)
                        act.wait_ge(product, tiles * batch + tile + 1)
                        nc.scalar.activation(mixed_t[tile % 2][:, :, :].rearrange("p c t -> p (c t)"),
                                             ps_turned[:, tile % 2, :], ACT.Copy).then_inc(turned_copied, 1)
                    act.wait_ge(moments_ready, tiles * (batch + 1))
                    nc.scalar.activation(deviation[half][:, :], moments[half][:, :, 1], ACT.Sqrt,
                                         bias=eps[:, :]).then_inc(deviation_ready, 1)
                    act.wait_ge(normalised, tiles * (batch + 1))
                    stand(act, alone)
                    act.dma_start(by_partition(out, batch * (SEQ * D_MODEL),
                                               [[D_MODEL, P], [P * D_MODEL, tiles], [1, D_MODEL]]),
                                  res[half][:, :, :]).then_inc(stored[half], 16)
            for half in range(2):
                act.wait_ge(stored[half], 16 * all_turns)

        @block.vector
        def _(dve):
            nc.vector.memset(eps[:, :], LN_EPS).then_inc(eps_ready, 1)
            dve.sem_inc(summed, tiles)
            dve.sem_inc(turned, tiles)
            dve.sem_inc(turned_copied, 2)
            dve.sem_inc(product, 2)
            dve.wait_ge(weights_in, 32)
            for group in range(groups):
                with dve.Fori(0, turns) as step:
                    turn = step + group * turns
                    for half in range(2):
                        batch = 2 * turn + half
                        dve.wait_ge(pair_in[half], 16 * (turn + 1))
                        dve.wait_ge(res_in[half], 16 * (turn + 1))
                        for tile in range(tiles):
                            column = PARTS * (tiles * (2 * step + half) + tile)
                            for n in range(2):
                                rows = pair[half][:, tile, n, :].rearrange("p (a b) -> p a b", a=PARTS)
                                nc.vector.tensor_tensor(
                                    rows, rows, weights_of[group][n][:, bass.ds(column, PARTS)].unsqueeze(2)
                                    .to_broadcast([P, PARTS, SUB]), ALU.mult).then_inc(scaled_ready, 1)
                            dve.wait_ge(scaled_ready, 2 * (tiles * batch + tile + 1))
                            dve.wait_ge(turned, tiles * batch + tile + 1)
                            nc.vector.tensor_tensor(mixed[half][:, tile, :], pair[half][:, tile, 0, :],
                                                    pair[half][:, tile, 1, :], ALU.add).then_inc(mixed_ready, 1)
                            nc.vector.tensor_tensor(res[half][:, tile, :], res[half][:, tile, :], bias_all[:, :],
                                                    ALU.add).then_inc(biased, 1)
                        for tile in range(tiles):
                            number = tiles * batch + tile
                            dve.wait_ge(product, number + 3)
                            dve.wait_ge(biased, number + 1)
                            nc.vector.tensor_tensor(res[half][:, tile, :], ps[:, tile, :], res[half][:, tile, :],
                                                    ALU.add).then_inc(summed, 1)
                            dve.wait_ge(summed, number + 1 + tiles)
                            nc.vector.bn_stats(stats[half][:, tile, :], res[half][:, tile, :]).then_inc(stats_ready, 1)
                            dve.wait_ge(stats_ready, number + 1)
                            stand(dve, alone)
                            nc.vector.bn_aggr(moments[half][:, tile, :],
                                              stats[half][:, tile, :]).then_inc(moments_ready, 1)
                        dve.wait_ge(deviation_ready, batch + 1)
                        nc.vector.reciprocal(factor[half][:, :], deviation[half][:, :]).then_inc(factor_ready, 1)
                        dve.wait_ge(factor_ready, batch + 1)
                        for tile in range(tiles):
                            nc.vector.tensor_scalar(res[half][:, tile, :], res[half][:, tile, :],
                                                    moments[half][:, tile, 0:1], factor[half][:, tile:tile + 1],
                                                    ALU.subtract, ALU.mult).then_inc(normalised, 1)




def decoder_block(nc, x, x_t, ctx_t, w, out):

    def scratch(name, *shape):
        return nc.dram_tensor(name, list(shape), F32).ap()

    def activations(name):
        return scratch(name, BATCH, SEQ, D_MODEL)

    q_t, k_t, v = activations("q_t"), activations("k_t"), activations("v")
    attended_t = activations("attended_t")
    first, first_t = activations("first"), activations("first_t")
    second, second_t = activations("second"), activations("second_t")
    hidden = activations("hidden")
    gathered = scratch("gathered", BATCH, SEQ, 2, D_MODEL)
    groups = [slice(n * GROUP_BATCHES, (n + 1) * GROUP_BATCHES) for n in range(2)]
    rows_in = [scratch(f"rows_in{n}", BLOCKS * ROWS_AT_ONCE, SUB) for n in range(2)]
    rows_out = [scratch(f"rows_out{n}", BLOCKS * ROWS_AT_ONCE, SUB) for n in range(2)]

    project(nc, "self", x_t, x_t, [w[f"self_w{n}"] for n in "qkv"], [w[f"self_b{n}"] for n in "qkv"], q_t, k_t, v)
    attend(nc, "self", q_t, k_t, v, attended_t,
           rel=(w["relative_k_t"], w["relative_v"], scratch("relative_scores", TILES * P * PITCH)))
    finish(nc, "self", attended_t, w["self_wo"], w["self_bo"], x, first, first_t)
    project(nc, "cross", first_t, ctx_t, [w[f"cross_w{n}"] for n in "qkv"], [w[f"cross_b{n}"] for n in "qkv"],
            q_t, k_t, v)

    with ExitStack() as ctx:
        mem = Memory(nc, ctx, "moe")
        routing = [Routing(mem, n) for n in range(2)]

        def cross_attend(n, beside=None):
            some = groups[n]
            attend(nc, f"cross{n}", q_t[some], k_t[some], v[some], attended_t[some], beside=beside)
            finish(nc, f"cross{n}", attended_t[some], w["cross_wo"], w["cross_bo"], first[some], second[some],
                   second_t[some])
            route(nc, second_t[some], w["ffn_wm"], w["ffn_bm"], w["expert_emb"], rows_in[n], hidden[some], routing[n])

        def experts(n, beside):
            run_experts(nc, f"group{n}", w["w1"], w["b1"], w["w2"], w["b2"], routing[n].block_expert,
                        rows_in[n], rows_out[n], beside)

        cross_attend(0)
        with ExitStack() as moves:
            cross_attend(1, dispatch(nc, Memory(nc, moves, "dispatch0"), hidden[groups[0]], routing[0], rows_in[0]))
        with ExitStack() as moves:
            experts(0, dispatch(nc, Memory(nc, moves, "dispatch1"), hidden[groups[1]], routing[1], rows_in[1]))
        with ExitStack() as moves:
            experts(1, gather(nc, Memory(nc, moves, "gather0"), rows_out[0], routing[0], gathered[groups[0]])[0])
        with ExitStack() as moves:
            beside, landed = gather(nc, Memory(nc, moves, "gather1"), rows_out[1], routing[1], gathered[groups[1]])
            finish_mixture(nc, gathered, [r.weight for r in routing], w["ffn_wo"], w["ffn_bo"], second, out,
                           beside, landed)


def kernel(x, ctx_768, L0_attn_Wq, L0_attn_bq, L0_attn_Wk, L0_attn_bk, L0_attn_Wv, L0_attn_bv, L0_attn_Wo, L0_attn_bo,
           L0_attn_relative_k, L0_attn_relative_v, L0_xattn_Wq, L0_xattn_bq, L0_xattn_Wk, L0_xattn_bk, L0_xattn_Wv,
           L0_xattn_bv, L0_xattn_Wo, L0_xattn_bo, L0_ffn_Wm, L0_ffn_bm, L0_ffn_expert_emb, L0_ffn_W1, L0_ffn_b1,
           L0_ffn_W2, L0_ffn_b2, L0_ffn_Wo, L0_ffn_bo):
    from concourse import bacc
    from concourse.bass_utils import run_bass_kernel_spmd

    arrays = {
        "x": x, "x_t": np.transpose(x, (0, 2, 1)), "ctx_t": np.transpose(ctx_768, (0, 2, 1)),
        "self_wq": np.transpose(L0_attn_Wq), "self_wk": np.transpose(L0_attn_Wk), "self_wv": np.transpose(L0_attn_Wv),
        "self_wo": np.transpose(L0_attn_Wo), "self_bq": L0_attn_bq, "self_bk": L0_attn_bk, "self_bv": L0_attn_bv,
        "self_bo": L0_attn_bo, "relative_k_t": np.transpose(L0_attn_relative_k), "relative_v": L0_attn_relative_v,
        "cross_wq": L0_xattn_Wq, "cross_wk": L0_xattn_Wk, "cross_wv": L0_xattn_Wv, "cross_wo": L0_xattn_Wo,
        "cross_bq": L0_xattn_bq, "cross_bk": L0_xattn_bk, "cross_bv": L0_xattn_bv, "cross_bo": L0_xattn_bo,
        "ffn_wm": L0_ffn_Wm, "ffn_bm": L0_ffn_bm, "expert_emb": L0_ffn_expert_emb, "w1": L0_ffn_W1, "b1": L0_ffn_b1,
        "w2": L0_ffn_W2, "b2": L0_ffn_b2, "ffn_wo": L0_ffn_Wo, "ffn_bo": L0_ffn_bo,
    }
    arrays = {name: np.ascontiguousarray(a) for name, a in arrays.items()}
    nc = bacc.Bacc("TRN2", target_bir_lowering=False, num_devices=1)
    w = {name: nc.dram_tensor(f"in_{name}", a.shape, F32, kind="ExternalInput").ap() for name, a in arrays.items()}
    out = nc.dram_tensor("out", [BATCH, SEQ, D_MODEL], F32, kind="ExternalOutput").ap()
    decoder_block(nc, w["x"], w["x_t"], w["ctx_t"], w, out)
    result = run_bass_kernel_spmd(nc, [{f"in_{name}": a for name, a in arrays.items()}], core_ids=[0])
    return result.results[0]["out"]
```
